# Optimizing a Trainium2 kernel written in Bass

```python
import numpy as np
import jax
import jax.numpy as jnp

def _softmax(x, axis=-1):
    return jax.nn.softmax(x, axis=axis)

def _gelu(x):
    return jax.nn.gelu(x, approximate=True)

def _silu(x):
    return jax.nn.silu(x)

def _sigmoid(x):
    return jax.nn.sigmoid(x)

def _layernorm(x, axis=-1, eps=1e-05):
    m = jnp.mean(x, axis=axis, keepdims=True)
    v = jnp.var(x, axis=axis, keepdims=True)
    return (x - m) / jnp.sqrt(v + eps)

def _scatter_add(tgt, idx, src, axis=0):
    return tgt.at[idx].add(src)

def _segment_sum(src, seg, n):
    return jax.ops.segment_sum(src, seg, n)
kernel_name = 'mk_decoder_postln_d4_seqx_r8_143057'

def setup_inputs(seed: int=0):
    np.random.seed(seed)
    _w = jnp.asarray

    def _rec_inputs():
        import jax
        import jax.numpy as jnp
        _rk = jax.random.key(seed)
        x = -0.0002928 + 1 * jax.random.normal(jax.random.fold_in(_rk, 1), (16, 256, 128), jnp.float32)
        _lenS = 256 - jax.random.randint(jax.random.fold_in(_rk, 7), (16,), 0, max(1, 256 // 4) + 1, jnp.int32)
        _lenS2 = 64 - jax.random.randint(jax.random.fold_in(_rk, 8), (16,), 0, max(1, 64 // 4) + 1, jnp.int32)
        _ctx_512P = jax.random.normal(jax.random.fold_in(_rk, 11), (16, 16, 64), jnp.float32)
        _ctx_512c = jax.random.dirichlet(jax.random.fold_in(_rk, 511), 0.3 * jnp.ones((16,), jnp.float32), (16, 64))
        _ctx_512t = jnp.einsum('bsk,bkd->bsd', _ctx_512c, _ctx_512P)
        _ctx_512t = _ctx_512t * jax.lax.rsqrt(jnp.mean(jnp.square(_ctx_512t)) + 1e-12) * 0.953939
        ctx_512 = 0.00222621 + 0.99962 * (_ctx_512t + 0.3 * jax.random.normal(jax.random.fold_in(_rk, 611), (16, 64, 64), jnp.float32))
        return (x, ctx_512)
    x, ctx_512 = _rec_inputs()

    def _L0_attn_setup():
        import jax, jax.numpy as jnp
        import numpy as np
        D_MODEL = 128
        N_HEADS = 16
        HEAD_DIM = D_MODEL // N_HEADS
        SCALE = HEAD_DIM ** (-0.5)

        def apply_rotary(x):
            seq_len = x.shape[-2]
            freqs = 10000.0 ** (jnp.arange(0, HEAD_DIM, 2.0, dtype=jnp.float32) / HEAD_DIM)
            t = jnp.arange(seq_len, dtype=jnp.float32)
            angles = t[:, None] * freqs[None, :]
            sin = jnp.sin(angles)[None, None]
            cos = jnp.cos(angles)[None, None]
            x1, x2 = (x[..., ::2], x[..., 1::2])
            return jnp.concatenate([x1 * cos - x2 * sin, x2 * cos + x1 * sin], axis=-1)
        key = jax.random.key(seed)
        ks = jax.random.split(key, 5)
        B, T = (2, 256)
        std = D_MODEL ** (-0.5)
        return {'x': jax.random.normal(ks[0], (B, T, D_MODEL), dtype=jnp.float32), 'qkv_w': jax.random.normal(ks[1], (D_MODEL, 3 * D_MODEL), dtype=jnp.float32) * std, 'qkv_b': jnp.zeros((3 * D_MODEL,), dtype=jnp.float32), 'out_w': jax.random.normal(ks[2], (D_MODEL, D_MODEL), dtype=jnp.float32) * std, 'out_b': jnp.zeros((D_MODEL,), dtype=jnp.float32)}
    _L0_attn_all = _L0_attn_setup()
    _L0_attn_in = {k: v for k, v in _L0_attn_all.items() if k in ('qkv_w', 'qkv_b', 'out_w', 'out_b')}
    del _L0_attn_all

    def _L0_xattn_setup():
        import jax, jax.numpy as jnp
        import numpy as np
        B, T, TC, C, CC, H = (2, 256, 64, 128, 64, 16)
        D = C // H

        def _heads(t):
            b, l, _ = t.shape
            return t.reshape(b, l, H, D).transpose(0, 2, 1, 3)
        key = jax.random.key(seed)
        ks = jax.random.split(key, 18)
        w = lambda k, i, o: jax.random.normal(k, (i, o), jnp.float32) / np.sqrt(i).astype(np.float32)
        return {'x': jax.random.normal(ks[0], (B, T, C), jnp.float32), 'cross_input': jax.random.normal(ks[1], (B, TC, CC), jnp.float32), 'Wk': w(ks[2], C, C), 'bk': jnp.zeros((C,), jnp.float32), 'Wq': w(ks[3], C, C), 'bq': jnp.zeros((C,), jnp.float32), 'Wv': w(ks[4], C, C), 'bv': jnp.zeros((C,), jnp.float32), 'Wck': w(ks[5], CC, C), 'bck': jnp.zeros((C,), jnp.float32), 'Wcq': w(ks[6], C, C), 'bcq': jnp.zeros((C,), jnp.float32), 'Wcv': w(ks[7], CC, C), 'bcv': jnp.zeros((C,), jnp.float32), 'Wp': w(ks[8], C, C), 'bp': jnp.zeros((C,), jnp.float32)}
    _L0_xattn_all = _L0_xattn_setup()
    _L0_xattn_in = {k: v for k, v in _L0_xattn_all.items() if k in ('Wk', 'bk', 'Wq', 'bq', 'Wv', 'bv', 'Wck', 'bck', 'Wcq', 'bcq', 'Wcv', 'bcv', 'Wp', 'bp')}
    del _L0_xattn_all

    def _L0_ffn_setup():
        import jax, jax.numpy as jnp
        import numpy as np
        D_MODEL = 128
        E = 4
        MIN_E = 1
        TH_LO = 0.5
        TH_HI = 2.0
        key = jax.random.key(seed)
        ks = jax.random.split(key, 12)
        B, N, D, H = (4, 256, D_MODEL, 2 * D_MODEL)
        s = 0.02
        return {'x': jax.random.normal(ks[0], (B, N, D), dtype=jnp.float32), 'gate_w': jax.random.normal(ks[1], (D, E), dtype=jnp.float32) * s, 'gate_b': jnp.zeros((E,), dtype=jnp.float32), 'dp_w1': jax.random.normal(ks[2], (D, D // 2), dtype=jnp.float32) * s, 'dp_b1': jnp.zeros((D // 2,), dtype=jnp.float32), 'dp_w2': jax.random.normal(ks[3], (D // 2, 1), dtype=jnp.float32) * s, 'dp_b2': jnp.zeros((1,), dtype=jnp.float32), 'ew1': jax.random.normal(ks[4], (E, D, H), dtype=jnp.float32) * s, 'eb1': jnp.zeros((E, H), dtype=jnp.float32), 'ew2': jax.random.normal(ks[5], (E, H, D), dtype=jnp.float32) * s, 'eb2': jnp.zeros((E, D), dtype=jnp.float32)}
    _L0_ffn_all = _L0_ffn_setup()
    _L0_ffn_in = {k: v for k, v in _L0_ffn_all.items() if k in ('gate_w', 'gate_b', 'dp_w1', 'dp_b1', 'dp_w2', 'dp_b2', 'ew1', 'eb1', 'ew2', 'eb2')}
    del _L0_ffn_all

    def _L1_attn_setup():
        import jax, jax.numpy as jnp
        import numpy as np
        import math
        _DENSE_LOCAL_W = 64
        _DYADIC = [96, 128, 192, 32, 48, 64, 96, 128, 192]
        OFFSETS = sorted(set(range(0, _DENSE_LOCAL_W + 1)) | set(_DYADIC))
        B, N, D, H = (1, 256, 128, 16)
        HD = D // H
        key = jax.random.key(seed)
        ks = jax.random.split(key, 8)
        s = 1.0 / math.sqrt(D)
        x = jax.random.normal(ks[0], (B, N, D), dtype=jnp.float32)
        Wqkv = jax.random.uniform(ks[1], (3 * D, D), jnp.float32, -s, s)
        bqkv = jax.random.uniform(ks[2], (3 * D,), jnp.float32, -s, s)
        Wgate = jax.random.uniform(ks[3], (D, D), jnp.float32, -s, s)
        bgate = jax.random.uniform(ks[4], (D,), jnp.float32, -s, s)
        Wout = jax.random.uniform(ks[5], (D, D), jnp.float32, -s, s)
        bout = jax.random.uniform(ks[6], (D,), jnp.float32, -s, s)
        alphas = jnp.linspace(0.2, 2.0, H)
        deltas = jnp.array([math.log(1.0 + d) for d in OFFSETS], dtype=jnp.float32)
        pos_bias = -deltas[:, None] * alphas[None, :]
        offsets = jnp.array(OFFSETS, dtype=jnp.int32)
        return {'x': x, 'Wqkv': Wqkv, 'bqkv': bqkv, 'Wgate': Wgate, 'bgate': bgate, 'Wout': Wout, 'bout': bout, 'pos_bias': pos_bias, 'offsets': offsets}
    _L1_attn_all = _L1_attn_setup()
    _L1_attn_in = {k: v for k, v in _L1_attn_all.items() if k in ('Wqkv', 'bqkv', 'Wgate', 'bgate', 'Wout', 'bout', 'pos_bias', 'offsets')}
    del _L1_attn_all

    def _L1_xattn_setup():
        import jax, jax.numpy as jnp
        import numpy as np
        DIM = 128
        LATENT_DIM = 64
        NUM_HEADS = 16
        HEAD_DIM = DIM // NUM_HEADS
        SCALE = HEAD_DIM ** (-0.5)
        key = jax.random.key(seed)
        k1, k2, k3, k4, k5 = jax.random.split(key, 5)
        B, xN, zN = (2, 256, 256)
        x = jax.random.normal(k1, (B, xN, DIM), dtype=jnp.float32)
        z = jax.random.normal(k2, (B, zN, LATENT_DIM), dtype=jnp.float32)
        Wq = jax.random.normal(k3, (DIM, DIM), dtype=jnp.float32) * DIM ** (-0.5)
        Wkv = jax.random.normal(k4, (2 * DIM, LATENT_DIM), dtype=jnp.float32) * LATENT_DIM ** (-0.5)
        Wo = jax.random.normal(k5, (DIM, DIM), dtype=jnp.float32) * DIM ** (-0.5)
        return {'x': x, 'z': z, 'Wq': Wq, 'Wkv': Wkv, 'Wo': Wo}
    _L1_xattn_all = _L1_xattn_setup()
    _L1_xattn_in = {k: v for k, v in _L1_xattn_all.items() if k in ('Wq', 'Wkv', 'Wo')}
    del _L1_xattn_all

    def _L1_ffn_setup():
        import jax, jax.numpy as jnp
        import numpy as np
        E, K, D, F = (8, 2, 128, 512)
        EPS = 1e-06
        B, S = (2, 128)
        key = jax.random.key(seed)
        ks = jax.random.split(key, 6)
        s_in = 1.0 / np.sqrt(D)
        s_mid = 1.0 / np.sqrt(F)
        return {'x': jax.random.normal(ks[0], (B, S, D), dtype=jnp.float32), 'Wg': jax.random.normal(ks[1], (D, E), dtype=jnp.float32) * s_in, 'gamma': jnp.ones((E, D), dtype=jnp.float32), 'beta': jnp.zeros((E, D), dtype=jnp.float32), 'W1': jax.random.normal(ks[2], (E, D, F), dtype=jnp.float32) * s_in, 'b1': jnp.zeros((E, F), dtype=jnp.float32), 'W2': jax.random.normal(ks[3], (E, F, D), dtype=jnp.float32) * s_mid, 'b2': jnp.zeros((E, D), dtype=jnp.float32)}
    _L1_ffn_all = _L1_ffn_setup()
    _L1_ffn_in = {k: v for k, v in _L1_ffn_all.items() if k in ('Wg', 'gamma', 'beta', 'W1', 'b1', 'W2', 'b2')}
    del _L1_ffn_all

    def _L2_attn_setup():
        import jax, jax.numpy as jnp
        import numpy as np
        import math
        D_MODEL = 128
        NUM_HEADS = 16
        HEAD_DIM = D_MODEL // NUM_HEADS
        REPETITIONS = 3
        NEG = -10000.0

        def _self_attention(q, k, v, mask):
            scale = 1.0 / math.sqrt(q.shape[-1])
            scores = jnp.einsum('bthd,bshd->bhts', q, k * scale) + mask
            attn = jax.nn.softmax(scores, axis=-1)
            return jnp.einsum('bhts,bshd->bthd', attn, v)
        key = jax.random.key(seed)
        ks = jax.random.split(key, 5)
        B, S = (2, 256)
        x = jax.random.normal(ks[0], (B, S, D_MODEL), dtype=jnp.float32)
        Wqkv_w = jax.random.normal(ks[1], (3 * D_MODEL, D_MODEL), dtype=jnp.float32) * (1.0 / math.sqrt(D_MODEL))
        Wqkv_b = jax.random.normal(ks[2], (3 * D_MODEL,), dtype=jnp.float32) * 0.02
        out_w = jax.random.normal(ks[3], (D_MODEL, D_MODEL), dtype=jnp.float32) * (1.0 / math.sqrt(D_MODEL))
        out_b = jax.random.normal(ks[4], (D_MODEL,), dtype=jnp.float32) * 0.02
        return {'x': x, 'Wqkv_w': Wqkv_w, 'Wqkv_b': Wqkv_b, 'out_w': out_w, 'out_b': out_b}
    _L2_attn_all = _L2_attn_setup()
    _L2_attn_in = {k: v for k, v in _L2_attn_all.items() if k in ('Wqkv_w', 'Wqkv_b', 'out_w', 'out_b')}
    del _L2_attn_all

    def _L2_xattn_setup():
        import jax, jax.numpy as jnp
        import numpy as np
        HEADS = 16
        D_MODEL = 128
        IMG_MODEL = 64
        D_K = D_MODEL // HEADS
        key = jax.random.key(seed)
        ks = jax.random.split(key, 12)
        B, LQ, LKV = (8, 256, 128)
        s_dm = 1.0 / np.sqrt(D_MODEL)
        s_im = 1.0 / np.sqrt(IMG_MODEL)
        return {'q': jax.random.normal(ks[0], (B, LQ, D_MODEL), jnp.float32), 'k': jax.random.normal(ks[1], (B, LKV, IMG_MODEL), jnp.float32), 'v': jax.random.normal(ks[2], (B, LKV, IMG_MODEL), jnp.float32), 'Wq': jax.random.normal(ks[3], (D_MODEL, D_MODEL), jnp.float32) * s_dm, 'bq': jnp.zeros((D_MODEL,), jnp.float32), 'Wk': jax.random.normal(ks[4], (IMG_MODEL, D_MODEL), jnp.float32) * s_im, 'bk': jnp.zeros((D_MODEL,), jnp.float32), 'Wv': jax.random.normal(ks[5], (IMG_MODEL, D_MODEL), jnp.float32) * s_im, 'bv': jnp.zeros((D_MODEL,), jnp.float32), 'Wo': jax.random.normal(ks[6], (D_MODEL, D_MODEL), jnp.float32) * s_dm, 'bo': jnp.zeros((D_MODEL,), jnp.float32)}
    _L2_xattn_all = _L2_xattn_setup()
    _L2_xattn_in = {k: v for k, v in _L2_xattn_all.items() if k in ('Wq', 'bq', 'Wk', 'bk', 'Wv', 'bv', 'Wo', 'bo')}
    del _L2_xattn_all

    def _L2_ffn_setup():
        import jax, jax.numpy as jnp
        import numpy as np
        import math
        B, S, D = (2, 256, 128)
        H = 16
        HD = D // H
        FFN = 256
        E = 8
        TOP_K = 2
        CAP_FACTOR = 1.25
        EPS = 1e-06
        BASE = 10000.0
        CAP = max(math.ceil(B * S * TOP_K * CAP_FACTOR / E), 1)

        def _rmsnorm(x, w):
            rms = jax.lax.rsqrt(jnp.mean(x * x, axis=-1, keepdims=True) + EPS)
            return w * x * rms

        def _rope(x, cos, sin):
            xr = x[..., 0::2]
            xi = x[..., 1::2]
            c = cos[None, None]
            s_ = sin[None, None]
            out_r = xr * c - xi * s_
            out_i = xr * s_ + xi * c
            return jnp.stack([out_r, out_i], axis=-1).reshape(x.shape)

        def _mha(x, w_qkv, w_o):
            b, s, d = x.shape
            qkv = x @ w_qkv
            q, k, v = jnp.split(qkv, 3, axis=-1)
            to_heads = lambda z: z.reshape(b, s, H, HD).transpose(0, 2, 1, 3)
            q, k, v = (to_heads(q), to_heads(k), to_heads(v))
            theta = BASE ** (-2.0 * (jnp.arange(HD // 2, dtype=jnp.float32) / HD))
            freqs = jnp.arange(s, dtype=jnp.float32)[:, None] * theta[None, :]
            cos, sin = (jnp.cos(freqs), jnp.sin(freqs))
            q = _rope(q, cos, sin)
            k = _rope(k, cos, sin)
            scores = jnp.einsum('bhqd,bhkd->bhqk', q, k) / jnp.sqrt(jnp.float32(HD))
            causal = jnp.tril(jnp.ones((s, s), dtype=bool))
            scores = jnp.where(causal, scores, -jnp.inf)
            attn = jax.nn.softmax(scores, axis=-1)
            y = jnp.einsum('bhqk,bhkd->bhqd', attn, v)
            y = y.transpose(0, 2, 1, 3).reshape(b, s, d)
            return y @ w_o

        def _moe(x, w_router, w1, w2):
            b, s, d = x.shape
            t = b * s
            xf = x.reshape(t, d)
            logits = xf.astype(jnp.float32) @ w_router.astype(jnp.float32)
            probs = jax.nn.softmax(logits, axis=-1)
            g, eidx = jax.lax.top_k(probs, TOP_K)
            fg = g.reshape(t * TOP_K)
            fe = eidx.reshape(t * TOP_K)
            tok_of = jnp.arange(t * TOP_K) // TOP_K
            masked = jnp.where(fe[None, :] == jnp.arange(E)[:, None], fg[None, :], -jnp.inf)
            vals, idx = jax.lax.top_k(masked, CAP)
            valid = jnp.isfinite(vals)
            gates = jnp.where(valid, vals, 0.0)
            tok = tok_of[idx]
            xe = xf[tok]
            h = jax.nn.relu(jnp.einsum('ecd,edf->ecf', xe, w1))
            ye = jnp.einsum('ecf,efd->ecd', h, w2) * gates[..., None]
            y = jnp.zeros_like(xf).at[tok.reshape(-1)].add(ye.reshape(-1, d))
            return y.reshape(b, s, d)
        key = jax.random.key(seed)
        ks = jax.random.split(key, 6)
        sd = 0.02
        return {'x': jax.random.normal(ks[0], (B, S, D), jnp.float32), 'g1': jnp.ones((D,), jnp.float32), 'w_qkv': jax.random.normal(ks[1], (D, 3 * D), jnp.float32) * sd, 'w_o': jax.random.normal(ks[2], (D, D), jnp.float32) * sd, 'g2': jnp.ones((D,), jnp.float32), 'w_router': jax.random.normal(ks[3], (D, E), jnp.float32) * sd, 'w1': jax.random.normal(ks[4], (E, D, FFN), jnp.float32) * sd, 'w2': jax.random.normal(ks[5], (E, FFN, D), jnp.float32) * sd}
    _L2_ffn_all = _L2_ffn_setup()
    _L2_ffn_in = {k: v for k, v in _L2_ffn_all.items() if k in ('g1', 'w_qkv', 'w_o', 'g2', 'w_router', 'w1', 'w2')}
    del _L2_ffn_all

    def _L3_attn_setup():
        import jax, jax.numpy as jnp
        import numpy as np
        HEADS = 16
        key = jax.random.key(seed)
        k1, k2, k3 = jax.random.split(key, 3)
        B, N, C = (4, 512, 128)
        x = jax.random.normal(k1, (B, N, C), dtype=jnp.float32)
        w_qkv = jax.random.normal(k2, (3 * C, C), dtype=jnp.float32) * C ** (-0.5)
        w_proj = jax.random.normal(k3, (C, C), dtype=jnp.float32) * C ** (-0.5)
        b_proj = jnp.zeros((C,), dtype=jnp.float32)
        return {'x': x, 'w_qkv': w_qkv, 'w_proj': w_proj, 'b_proj': b_proj}
    _L3_attn_all = _L3_attn_setup()
    _L3_attn_in = {k: v for k, v in _L3_attn_all.items() if k in ('w_qkv', 'w_proj', 'b_proj')}
    del _L3_attn_all

    def _L3_xattn_setup():
        import jax, jax.numpy as jnp
        import numpy as np
        NUM_HEADS = 16
        HEAD_DIM = 64
        Q_DIM = 128
        KV_DIM = 64
        INNER = NUM_HEADS * HEAD_DIM
        key = jax.random.key(seed)
        ks = jax.random.split(key, 7)
        B, N, M = (32, 128, 256)
        q = jax.random.normal(ks[0], (B, N, Q_DIM), dtype=jnp.float32)
        kv = jax.random.normal(ks[1], (B, M, KV_DIM), dtype=jnp.float32)
        Wq = jax.random.normal(ks[2], (Q_DIM, INNER), dtype=jnp.float32) / np.sqrt(Q_DIM)
        Wk = jax.random.normal(ks[3], (KV_DIM, INNER), dtype=jnp.float32) / np.sqrt(KV_DIM)
        Wv = jax.random.normal(ks[4], (KV_DIM, INNER), dtype=jnp.float32) / np.sqrt(KV_DIM)
        Wo = jax.random.normal(ks[5], (INNER, Q_DIM), dtype=jnp.float32) / np.sqrt(INNER)
        bo = jax.random.normal(ks[6], (Q_DIM,), dtype=jnp.float32) * 0.01
        return {'q': q, 'kv': kv, 'Wq': Wq, 'Wk': Wk, 'Wv': Wv, 'Wo': Wo, 'bo': bo}
    _L3_xattn_all = _L3_xattn_setup()
    _L3_xattn_in = {k: v for k, v in _L3_xattn_all.items() if k in ('Wq', 'Wk', 'Wv', 'Wo', 'bo')}
    del _L3_xattn_all

    def _L3_ffn_setup():
        import jax, jax.numpy as jnp
        import numpy as np
        B, L, D = (4, 64, 128)
        E, TOP_K = (16, 4)
        F = 4 * D
        key = jax.random.key(seed)
        ks = jax.random.split(key, 6)
        scale = 0.02
        return {'x': jax.random.normal(ks[0], (B, L, D), jnp.float32), 'keys': jax.random.normal(ks[1], (E, D), jnp.float32), 'w1': jax.random.normal(ks[2], (E, F, D), jnp.float32) * scale, 'b1': jnp.zeros((E, F), jnp.float32), 'w2': jax.random.normal(ks[3], (E, D, F), jnp.float32) * scale, 'b2': jnp.zeros((E, D), jnp.float32), 'rw': jax.random.normal(ks[4], (E, D), jnp.float32) * scale, 'rb': jnp.zeros((E,), jnp.float32)}
    _L3_ffn_all = _L3_ffn_setup()
    _L3_ffn_in = {k: v for k, v in _L3_ffn_all.items() if k in ('keys', 'w1', 'b1', 'w2', 'b2', 'rw', 'rb')}
    del _L3_ffn_all
    return {'x': x, 'ctx_512': ctx_512, 'L0_attn_qkv_w': _L0_attn_in['qkv_w'], 'L0_attn_qkv_b': _L0_attn_in['qkv_b'], 'L0_attn_out_w': _L0_attn_in['out_w'], 'L0_attn_out_b': _L0_attn_in['out_b'], 'L0_xattn_Wk': _L0_xattn_in['Wk'], 'L0_xattn_bk': _L0_xattn_in['bk'], 'L0_xattn_Wq': _L0_xattn_in['Wq'], 'L0_xattn_bq': _L0_xattn_in['bq'], 'L0_xattn_Wv': _L0_xattn_in['Wv'], 'L0_xattn_bv': _L0_xattn_in['bv'], 'L0_xattn_Wck': _L0_xattn_in['Wck'], 'L0_xattn_bck': _L0_xattn_in['bck'], 'L0_xattn_Wcq': _L0_xattn_in['Wcq'], 'L0_xattn_bcq': _L0_xattn_in['bcq'], 'L0_xattn_Wcv': _L0_xattn_in['Wcv'], 'L0_xattn_bcv': _L0_xattn_in['bcv'], 'L0_xattn_Wp': _L0_xattn_in['Wp'], 'L0_xattn_bp': _L0_xattn_in['bp'], 'L0_ffn_gate_w': _L0_ffn_in['gate_w'], 'L0_ffn_gate_b': _L0_ffn_in['gate_b'], 'L0_ffn_dp_w1': _L0_ffn_in['dp_w1'], 'L0_ffn_dp_b1': _L0_ffn_in['dp_b1'], 'L0_ffn_dp_w2': _L0_ffn_in['dp_w2'], 'L0_ffn_dp_b2': _L0_ffn_in['dp_b2'], 'L0_ffn_ew1': _L0_ffn_in['ew1'], 'L0_ffn_eb1': _L0_ffn_in['eb1'], 'L0_ffn_ew2': _L0_ffn_in['ew2'], 'L0_ffn_eb2': _L0_ffn_in['eb2'], 'L1_attn_Wqkv': _L1_attn_in['Wqkv'], 'L1_attn_bqkv': _L1_attn_in['bqkv'], 'L1_attn_Wgate': _L1_attn_in['Wgate'], 'L1_attn_bgate': _L1_attn_in['bgate'], 'L1_attn_Wout': _L1_attn_in['Wout'], 'L1_attn_bout': _L1_attn_in['bout'], 'L1_attn_pos_bias': _L1_attn_in['pos_bias'], 'L1_attn_offsets': _L1_attn_in['offsets'], 'L1_xattn_Wq': _L1_xattn_in['Wq'], 'L1_xattn_Wkv': _L1_xattn_in['Wkv'], 'L1_xattn_Wo': _L1_xattn_in['Wo'], 'L1_ffn_Wg': _L1_ffn_in['Wg'], 'L1_ffn_gamma': _L1_ffn_in['gamma'], 'L1_ffn_beta': _L1_ffn_in['beta'], 'L1_ffn_W1': _L1_ffn_in['W1'], 'L1_ffn_b1': _L1_ffn_in['b1'], 'L1_ffn_W2': _L1_ffn_in['W2'], 'L1_ffn_b2': _L1_ffn_in['b2'], 'L2_attn_Wqkv_w': _L2_attn_in['Wqkv_w'], 'L2_attn_Wqkv_b': _L2_attn_in['Wqkv_b'], 'L2_attn_out_w': _L2_attn_in['out_w'], 'L2_attn_out_b': _L2_attn_in['out_b'], 'L2_xattn_Wq': _L2_xattn_in['Wq'], 'L2_xattn_bq': _L2_xattn_in['bq'], 'L2_xattn_Wk': _L2_xattn_in['Wk'], 'L2_xattn_bk': _L2_xattn_in['bk'], 'L2_xattn_Wv': _L2_xattn_in['Wv'], 'L2_xattn_bv': _L2_xattn_in['bv'], 'L2_xattn_Wo': _L2_xattn_in['Wo'], 'L2_xattn_bo': _L2_xattn_in['bo'], 'L2_ffn_g1': _L2_ffn_in['g1'], 'L2_ffn_w_qkv': _L2_ffn_in['w_qkv'], 'L2_ffn_w_o': _L2_ffn_in['w_o'], 'L2_ffn_g2': _L2_ffn_in['g2'], 'L2_ffn_w_router': _L2_ffn_in['w_router'], 'L2_ffn_w1': _L2_ffn_in['w1'], 'L2_ffn_w2': _L2_ffn_in['w2'], 'L3_attn_w_qkv': _L3_attn_in['w_qkv'], 'L3_attn_w_proj': _L3_attn_in['w_proj'], 'L3_attn_b_proj': _L3_attn_in['b_proj'], 'L3_xattn_Wq': _L3_xattn_in['Wq'], 'L3_xattn_Wk': _L3_xattn_in['Wk'], 'L3_xattn_Wv': _L3_xattn_in['Wv'], 'L3_xattn_Wo': _L3_xattn_in['Wo'], 'L3_xattn_bo': _L3_xattn_in['bo'], 'L3_ffn_keys': _L3_ffn_in['keys'], 'L3_ffn_w1': _L3_ffn_in['w1'], 'L3_ffn_b1': _L3_ffn_in['b1'], 'L3_ffn_w2': _L3_ffn_in['w2'], 'L3_ffn_b2': _L3_ffn_in['b2'], 'L3_ffn_rw': _L3_ffn_in['rw'], 'L3_ffn_rb': _L3_ffn_in['rb']}

def reference(x, ctx_512, L0_attn_qkv_w, L0_attn_qkv_b, L0_attn_out_w, L0_attn_out_b, L0_xattn_Wk, L0_xattn_bk, L0_xattn_Wq, L0_xattn_bq, L0_xattn_Wv, L0_xattn_bv, L0_xattn_Wck, L0_xattn_bck, L0_xattn_Wcq, L0_xattn_bcq, L0_xattn_Wcv, L0_xattn_bcv, L0_xattn_Wp, L0_xattn_bp, L0_ffn_gate_w, L0_ffn_gate_b, L0_ffn_dp_w1, L0_ffn_dp_b1, L0_ffn_dp_w2, L0_ffn_dp_b2, L0_ffn_ew1, L0_ffn_eb1, L0_ffn_ew2, L0_ffn_eb2, L1_attn_Wqkv, L1_attn_bqkv, L1_attn_Wgate, L1_attn_bgate, L1_attn_Wout, L1_attn_bout, L1_attn_pos_bias, L1_attn_offsets, L1_xattn_Wq, L1_xattn_Wkv, L1_xattn_Wo, L1_ffn_Wg, L1_ffn_gamma, L1_ffn_beta, L1_ffn_W1, L1_ffn_b1, L1_ffn_W2, L1_ffn_b2, L2_attn_Wqkv_w, L2_attn_Wqkv_b, L2_attn_out_w, L2_attn_out_b, L2_xattn_Wq, L2_xattn_bq, L2_xattn_Wk, L2_xattn_bk, L2_xattn_Wv, L2_xattn_bv, L2_xattn_Wo, L2_xattn_bo, L2_ffn_g1, L2_ffn_w_qkv, L2_ffn_w_o, L2_ffn_g2, L2_ffn_w_router, L2_ffn_w1, L2_ffn_w2, L3_attn_w_qkv, L3_attn_w_proj, L3_attn_b_proj, L3_xattn_Wq, L3_xattn_Wk, L3_xattn_Wv, L3_xattn_Wo, L3_xattn_bo, L3_ffn_keys, L3_ffn_w1, L3_ffn_b1, L3_ffn_w2, L3_ffn_b2, L3_ffn_rw, L3_ffn_rb):
    import jax
    import jax.numpy as jnp

    def _L0_attn_ref(x, qkv_w, qkv_b, out_w, out_b):
        import jax, jax.numpy as jnp
        import numpy as np
        D_MODEL = 128
        N_HEADS = 16
        HEAD_DIM = D_MODEL // N_HEADS
        SCALE = HEAD_DIM ** (-0.5)

        def apply_rotary(x):
            seq_len = x.shape[-2]
            freqs = 10000.0 ** (jnp.arange(0, HEAD_DIM, 2.0, dtype=jnp.float32) / HEAD_DIM)
            t = jnp.arange(seq_len, dtype=jnp.float32)
            angles = t[:, None] * freqs[None, :]
            sin = jnp.sin(angles)[None, None]
            cos = jnp.cos(angles)[None, None]
            x1, x2 = (x[..., ::2], x[..., 1::2])
            return jnp.concatenate([x1 * cos - x2 * sin, x2 * cos + x1 * sin], axis=-1)
        B, T, D = x.shape
        qkv = x @ qkv_w + qkv_b
        q, k, v = jnp.split(qkv, 3, axis=-1)

        def to_heads(a):
            return a.reshape(B, T, N_HEADS, HEAD_DIM).transpose(0, 2, 1, 3)
        q, k, v = (to_heads(q), to_heads(k), to_heads(v))
        q = apply_rotary(q)
        k = apply_rotary(k)
        scores = jnp.einsum('bhqd,bhkd->bhqk', q, k) * SCALE
        weights = jax.nn.softmax(scores, axis=-1)
        attn = jnp.einsum('bhqk,bhkd->bhqd', weights, v)
        attn = attn.transpose(0, 2, 1, 3).reshape(B, T, D)
        return attn @ out_w + out_b

    def _L0_xattn_ref(x, cross_input, Wk, bk, Wq, bq, Wv, bv, Wck, bck, Wcq, bcq, Wcv, bcv, Wp, bp):
        import jax, jax.numpy as jnp
        import numpy as np
        B, T, TC, C, CC, H = (2, 256, 64, 128, 64, 16)
        D = C // H

        def _heads(t):
            b, l, _ = t.shape
            return t.reshape(b, l, H, D).transpose(0, 2, 1, 3)
        scale = np.float32(1.0 / np.sqrt(D))
        q = _heads(x @ Wq + bq)
        k = _heads(x @ Wk + bk)
        v = _heads(x @ Wv + bv)
        att = jnp.einsum('bhqd,bhkd->bhqk', q, k) * scale
        causal = jnp.tril(jnp.ones((T, T), bool))
        att = jnp.where(causal[None, None], att, -jnp.inf)
        y = jnp.einsum('bhqk,bhkd->bhqd', jax.nn.softmax(att, axis=-1), v)
        qc = _heads(x @ Wcq + bcq)
        kc = _heads(cross_input @ Wck + bck)
        vc = _heads(cross_input @ Wcv + bcv)
        attc = jnp.einsum('bhqd,bhkd->bhqk', qc, kc) * scale
        y = y + jnp.einsum('bhqk,bhkd->bhqd', jax.nn.softmax(attc, axis=-1), vc)
        y = y.transpose(0, 2, 1, 3).reshape(x.shape[0], T, C)
        return y @ Wp + bp

    def _L0_ffn_ref(x, gate_w, gate_b, dp_w1, dp_b1, dp_w2, dp_b2, ew1, eb1, ew2, eb2):
        import jax, jax.numpy as jnp
        import numpy as np
        D_MODEL = 128
        E = 4
        MIN_E = 1
        TH_LO = 0.5
        TH_HI = 2.0
        B, N, D = x.shape
        xf = x.reshape(B * N, D)
        T = B * N
        h = jax.nn.relu(xf @ dp_w1 + dp_b1)
        entropy = jax.nn.softplus(h @ dp_w2 + dp_b2)[:, 0]
        norm = jnp.clip((entropy - TH_LO) / (TH_HI - TH_LO), 0.0, 1.0)
        k_tok = jnp.clip(jnp.round(MIN_E + norm * (E - MIN_E)).astype(jnp.int32), MIN_E, E)
        logits = xf @ gate_w + gate_b
        top_logits, top_idx = jax.lax.top_k(logits, E)
        pos = jnp.arange(E)
        sel = pos[None, :] < k_tok[:, None]
        masked = jnp.where(sel, top_logits, -jnp.inf)
        w_top = jax.nn.softmax(masked, axis=-1)
        dense_w = jnp.zeros((T, E), dtype=xf.dtype).at[jnp.arange(T)[:, None], top_idx].set(w_top)
        hid = jax.nn.relu(jnp.einsum('td,edh->teh', xf, ew1) + eb1[None, :, :])
        y = jnp.einsum('teh,ehd->ted', hid, ew2) + eb2[None, :, :]
        out = jnp.einsum('te,ted->td', dense_w, y)
        return out.reshape(B, N, D)

    def _L1_attn_ref(x, Wqkv, bqkv, Wgate, bgate, Wout, bout, pos_bias, offsets):
        import jax, jax.numpy as jnp
        import numpy as np
        import math
        _DENSE_LOCAL_W = 64
        _DYADIC = [96, 128, 192, 32, 48, 64, 96, 128, 192]
        OFFSETS = sorted(set(range(0, _DENSE_LOCAL_W + 1)) | set(_DYADIC))
        B, N, D, H = (1, 256, 128, 16)
        HD = D // H
        Bx, Nx, Dx = x.shape
        qkv = x @ Wqkv.T + bqkv
        q, k, v = jnp.split(qkv, 3, axis=-1)
        q = q.reshape(Bx, Nx, H, HD).transpose(0, 2, 1, 3)
        k = k.reshape(Bx, Nx, H, HD).transpose(0, 2, 1, 3)
        v = v.reshape(Bx, Nx, H, HD).transpose(0, 2, 1, 3)
        scale = HD ** (-0.5)
        n_idx = jnp.arange(Nx, dtype=jnp.int32)[:, None]
        idx = n_idx - offsets[None, :]
        valid = idx >= 0
        idx_c = jnp.clip(idx, 0, Nx - 1)
        K_all = k[:, :, idx_c, :]
        V_all = v[:, :, idx_c, :]
        scores = jnp.einsum('bhnd,bhnod->bhno', q, K_all) * scale
        scores = scores + pos_bias.T[None, :, None, :]
        scores = jnp.where(valid[None, None], scores, -jnp.inf)
        alpha = jax.nn.softmax(scores, axis=-1)
        out = jnp.einsum('bhno,bhnod->bhnd', alpha, V_all)
        flat = out.transpose(0, 2, 1, 3).reshape(Bx, Nx, Dx)
        gate = jax.nn.sigmoid(x @ Wgate.T + bgate)
        return flat * gate @ Wout.T + bout

    def _L1_xattn_ref(x, z, Wq, Wkv, Wo):
        import jax, jax.numpy as jnp
        import numpy as np
        DIM = 128
        LATENT_DIM = 64
        NUM_HEADS = 16
        HEAD_DIM = DIM // NUM_HEADS
        SCALE = HEAD_DIM ** (-0.5)
        B, xN, _ = x.shape
        _, zN, _ = z.shape
        Q = (x @ Wq.T).reshape(B, xN, NUM_HEADS, HEAD_DIM)
        KV = (z @ Wkv.T).reshape(B, zN, 2, NUM_HEADS, HEAD_DIM)
        K = KV[:, :, 0]
        V = KV[:, :, 1]
        attn = jnp.einsum('bqhd,bkhd->bhqk', Q, K) * SCALE
        attn = jax.nn.softmax(attn, axis=-1)
        O = jnp.einsum('bhqk,bkhd->bqhd', attn, V).reshape(B, xN, DIM)
        return O @ Wo.T

    def _L1_ffn_ref(x, Wg, gamma, beta, W1, b1, W2, b2):
        import jax, jax.numpy as jnp
        import numpy as np
        E, K, D, F = (8, 2, 128, 512)
        EPS = 1e-06
        B, S = (2, 128)
        orig_shape = x.shape
        xf = x.reshape(-1, orig_shape[-1])
        scores = xf @ Wg
        w, idx = jax.lax.top_k(scores, K)
        w = jax.nn.softmax(w, axis=-1)
        mu = jnp.mean(xf, axis=-1, keepdims=True)
        var = jnp.var(xf, axis=-1, keepdims=True)
        xhat = (xf - mu) * jax.lax.rsqrt(var + EPS)
        normed = xhat[None, :, :] * gamma[:, None, :] + beta[:, None, :]
        h = jax.nn.relu(jnp.einsum('end,edf->enf', normed, W1) + b1[:, None, :])
        out = jnp.einsum('enf,efd->end', h, W2) + b2[:, None, :] + xf[None, :, :]
        cw = jnp.sum(w[..., None] * jax.nn.one_hot(idx, E, dtype=w.dtype), axis=1)
        y = jnp.einsum('ne,end->nd', cw, out)
        return y.reshape(orig_shape)

    def _L2_attn_ref(x, Wqkv_w, Wqkv_b, out_w, out_b):
        import jax, jax.numpy as jnp
        import numpy as np
        import math
        D_MODEL = 128
        NUM_HEADS = 16
        HEAD_DIM = D_MODEL // NUM_HEADS
        REPETITIONS = 3
        NEG = -10000.0

        def _self_attention(q, k, v, mask):
            scale = 1.0 / math.sqrt(q.shape[-1])
            scores = jnp.einsum('bthd,bshd->bhts', q, k * scale) + mask
            attn = jax.nn.softmax(scores, axis=-1)
            return jnp.einsum('bhts,bshd->bthd', attn, v)
        B, S, _ = x.shape
        qkv = x @ Wqkv_w.T + Wqkv_b
        qkv = qkv.reshape(B, S, 3, NUM_HEADS, HEAD_DIM)
        q, k, v = (qkv[:, :, 0], qkv[:, :, 1], qkv[:, :, 2])
        mask = jnp.triu(jnp.full((S, S), NEG, dtype=x.dtype), 1)
        context = _self_attention(q, k, v, mask)
        for _ in range(REPETITIONS - 1):
            context = _self_attention(context, k, v, mask)
        out = context.reshape(B, S, D_MODEL) @ out_w.T + out_b
        return out

    def _L2_xattn_ref(q, k, v, Wq, bq, Wk, bk, Wv, bv, Wo, bo):
        import jax, jax.numpy as jnp
        import numpy as np
        HEADS = 16
        D_MODEL = 128
        IMG_MODEL = 64
        D_K = D_MODEL // HEADS
        B, LQ, _ = q.shape
        LKV = k.shape[1]
        qh = (q @ Wq + bq).reshape(B, LQ, HEADS, D_K).transpose(0, 2, 1, 3)
        kh = (k @ Wk + bk).reshape(B, LKV, HEADS, D_K).transpose(0, 2, 1, 3)
        vh = (v @ Wv + bv).reshape(B, LKV, HEADS, D_K).transpose(0, 2, 1, 3)
        scale = 1.0 / np.sqrt(D_K)
        scores = jnp.einsum('bhqd,bhkd->bhqk', qh, kh) * scale
        attn = jax.nn.softmax(scores, axis=-1)
        out = jnp.einsum('bhqk,bhkd->bhqd', attn, vh)
        concat = out.transpose(0, 2, 1, 3).reshape(B, LQ, D_MODEL)
        return concat @ Wo + bo

    def _L2_ffn_ref(x, g1, w_qkv, w_o, g2, w_router, w1, w2):
        import jax, jax.numpy as jnp
        import numpy as np
        import math
        B, S, D = (2, 256, 128)
        H = 16
        HD = D // H
        FFN = 256
        E = 8
        TOP_K = 2
        CAP_FACTOR = 1.25
        EPS = 1e-06
        BASE = 10000.0
        CAP = max(math.ceil(B * S * TOP_K * CAP_FACTOR / E), 1)

        def _rmsnorm(x, w):
            rms = jax.lax.rsqrt(jnp.mean(x * x, axis=-1, keepdims=True) + EPS)
            return w * x * rms

        def _rope(x, cos, sin):
            xr = x[..., 0::2]
            xi = x[..., 1::2]
            c = cos[None, None]
            s_ = sin[None, None]
            out_r = xr * c - xi * s_
            out_i = xr * s_ + xi * c
            return jnp.stack([out_r, out_i], axis=-1).reshape(x.shape)

        def _mha(x, w_qkv, w_o):
            b, s, d = x.shape
            qkv = x @ w_qkv
            q, k, v = jnp.split(qkv, 3, axis=-1)
            to_heads = lambda z: z.reshape(b, s, H, HD).transpose(0, 2, 1, 3)
            q, k, v = (to_heads(q), to_heads(k), to_heads(v))
            theta = BASE ** (-2.0 * (jnp.arange(HD // 2, dtype=jnp.float32) / HD))
            freqs = jnp.arange(s, dtype=jnp.float32)[:, None] * theta[None, :]
            cos, sin = (jnp.cos(freqs), jnp.sin(freqs))
            q = _rope(q, cos, sin)
            k = _rope(k, cos, sin)
            scores = jnp.einsum('bhqd,bhkd->bhqk', q, k) / jnp.sqrt(jnp.float32(HD))
            causal = jnp.tril(jnp.ones((s, s), dtype=bool))
            scores = jnp.where(causal, scores, -jnp.inf)
            attn = jax.nn.softmax(scores, axis=-1)
            y = jnp.einsum('bhqk,bhkd->bhqd', attn, v)
            y = y.transpose(0, 2, 1, 3).reshape(b, s, d)
            return y @ w_o

        def _moe(x, w_router, w1, w2):
            b, s, d = x.shape
            t = b * s
            xf = x.reshape(t, d)
            logits = xf.astype(jnp.float32) @ w_router.astype(jnp.float32)
            probs = jax.nn.softmax(logits, axis=-1)
            g, eidx = jax.lax.top_k(probs, TOP_K)
            fg = g.reshape(t * TOP_K)
            fe = eidx.reshape(t * TOP_K)
            tok_of = jnp.arange(t * TOP_K) // TOP_K
            masked = jnp.where(fe[None, :] == jnp.arange(E)[:, None], fg[None, :], -jnp.inf)
            vals, idx = jax.lax.top_k(masked, CAP)
            valid = jnp.isfinite(vals)
            gates = jnp.where(valid, vals, 0.0)
            tok = tok_of[idx]
            xe = xf[tok]
            h = jax.nn.relu(jnp.einsum('ecd,edf->ecf', xe, w1))
            ye = jnp.einsum('ecf,efd->ecd', h, w2) * gates[..., None]
            y = jnp.zeros_like(xf).at[tok.reshape(-1)].add(ye.reshape(-1, d))
            return y.reshape(b, s, d)
        x = x + _mha(_rmsnorm(x, g1), w_qkv, w_o)
        x = x + _moe(_rmsnorm(x, g2), w_router, w1, w2)
        return x

    def _L3_attn_ref(x, w_qkv, w_proj, b_proj):
        import jax, jax.numpy as jnp
        import numpy as np
        HEADS = 16
        B, N, C = x.shape
        H = HEADS
        D = C // H
        qkv = x @ w_qkv.T
        q, k, v = jnp.split(qkv, 3, axis=-1)

        def to_bhdn(t):
            return t.reshape(B, N, H, D).transpose(0, 2, 3, 1)
        q = jax.nn.relu(to_bhdn(q))
        k = jax.nn.relu(to_bhdn(k))
        v = to_bhdn(v)
        eps = jnp.finfo(q.dtype).eps
        ksum = k.sum(axis=-1)
        z = 1.0 / (jnp.einsum('bhd,bhdn->bhn', ksum, q) + eps)
        context = jnp.einsum('bhdn,bhen->bhde', v, k)
        out = jnp.einsum('bhde,bhen->bhdn', context, q)
        out = out * z[:, :, None, :]
        out = out.transpose(0, 3, 1, 2).reshape(B, N, C)
        return out @ w_proj.T + b_proj

    def _L3_xattn_ref(q, kv, Wq, Wk, Wv, Wo, bo):
        import jax, jax.numpy as jnp
        import numpy as np
        NUM_HEADS = 16
        HEAD_DIM = 64
        Q_DIM = 128
        KV_DIM = 64
        INNER = NUM_HEADS * HEAD_DIM
        B, N, _ = q.shape
        M = kv.shape[1]
        scale = HEAD_DIM ** (-0.5)
        qh = (q @ Wq).reshape(B, N, NUM_HEADS, HEAD_DIM).transpose(0, 2, 1, 3)
        kh = (kv @ Wk).reshape(B, M, NUM_HEADS, HEAD_DIM).transpose(0, 2, 1, 3)
        vh = (kv @ Wv).reshape(B, M, NUM_HEADS, HEAD_DIM).transpose(0, 2, 1, 3)
        scores = jnp.einsum('bhnd,bhmd->bhnm', qh, kh) * scale
        attn = jax.nn.softmax(scores, axis=-1)
        out = jnp.einsum('bhnm,bhmd->bhnd', attn, vh)
        out = out.transpose(0, 2, 1, 3).reshape(B, N, INNER)
        return out @ Wo + bo

    def _L3_ffn_ref(x, keys, w1, b1, w2, b2, rw, rb):
        import jax, jax.numpy as jnp
        import numpy as np
        B, L, D = (4, 64, 128)
        E, TOP_K = (16, 4)
        F = 4 * D
        diff = x[:, :, None, :] - keys
        dist2 = jnp.sum(diff * diff, axis=-1)
        logits = -dist2 + jnp.einsum('bld,ed->ble', x, rw) + rb
        topv, topi = jax.lax.top_k(logits, TOP_K)
        w = jax.nn.softmax(topv, axis=-1)
        hidden = jax.nn.gelu(jnp.einsum('bld,efd->blef', x, w1) + b1, approximate=False)
        exp_out = jnp.einsum('blef,edf->bled', hidden, w2) + b2
        sel = jnp.take_along_axis(exp_out, topi[..., None], axis=2)
        fused = jnp.sum(w[..., None] * sel, axis=2)
        return fused
    x = _layernorm(x + _L0_attn_ref(x, L0_attn_qkv_w, L0_attn_qkv_b, L0_attn_out_w, L0_attn_out_b), axis=-1)
    x = _layernorm(x + _L0_xattn_ref(x, ctx_512, L0_xattn_Wk, L0_xattn_bk, L0_xattn_Wq, L0_xattn_bq, L0_xattn_Wv, L0_xattn_bv, L0_xattn_Wck, L0_xattn_bck, L0_xattn_Wcq, L0_xattn_bcq, L0_xattn_Wcv, L0_xattn_bcv, L0_xattn_Wp, L0_xattn_bp), axis=-1)
    x = _layernorm(x + _L0_ffn_ref(x, L0_ffn_gate_w, L0_ffn_gate_b, L0_ffn_dp_w1, L0_ffn_dp_b1, L0_ffn_dp_w2, L0_ffn_dp_b2, L0_ffn_ew1, L0_ffn_eb1, L0_ffn_ew2, L0_ffn_eb2), axis=-1)
    x = _layernorm(x + _L1_attn_ref(x, L1_attn_Wqkv, L1_attn_bqkv, L1_attn_Wgate, L1_attn_bgate, L1_attn_Wout, L1_attn_bout, L1_attn_pos_bias, L1_attn_offsets), axis=-1)
    x = _layernorm(x + _L1_xattn_ref(x, ctx_512, L1_xattn_Wq, L1_xattn_Wkv, L1_xattn_Wo), axis=-1)
    x = _layernorm(x + _L1_ffn_ref(x, L1_ffn_Wg, L1_ffn_gamma, L1_ffn_beta, L1_ffn_W1, L1_ffn_b1, L1_ffn_W2, L1_ffn_b2), axis=-1)
    x = _layernorm(x + _L2_attn_ref(x, L2_attn_Wqkv_w, L2_attn_Wqkv_b, L2_attn_out_w, L2_attn_out_b), axis=-1)
    x = _layernorm(x + _L2_xattn_ref(x, ctx_512, ctx_512, L2_xattn_Wq, L2_xattn_bq, L2_xattn_Wk, L2_xattn_bk, L2_xattn_Wv, L2_xattn_bv, L2_xattn_Wo, L2_xattn_bo), axis=-1)
    x = _layernorm(x + _L2_ffn_ref(x, L2_ffn_g1, L2_ffn_w_qkv, L2_ffn_w_o, L2_ffn_g2, L2_ffn_w_router, L2_ffn_w1, L2_ffn_w2), axis=-1)
    x = _layernorm(x + _L3_attn_ref(x, L3_attn_w_qkv, L3_attn_w_proj, L3_attn_b_proj), axis=-1)
    x = _layernorm(x + _L3_xattn_ref(x, ctx_512, L3_xattn_Wq, L3_xattn_Wk, L3_xattn_Wv, L3_xattn_Wo, L3_xattn_bo), axis=-1)
    x = _layernorm(x + _L3_ffn_ref(x, L3_ffn_keys, L3_ffn_w1, L3_ffn_b1, L3_ffn_w2, L3_ffn_b2, L3_ffn_rw, L3_ffn_rb), axis=-1)
    return x

_drawn_inputs = setup_inputs


def setup_inputs(seed=0):
    import zlib

    import numpy as np

    out = dict(_drawn_inputs(seed))
    spreads = {'L0_attn_qkv_b': (0.0, 0.1),
     'L0_attn_out_b': (0.0, 0.1),
     'L0_xattn_bk': (0.0, 2.0),
     'L0_xattn_bq': (0.0, 0.319),
     'L0_xattn_bv': (0.0, 0.1),
     'L0_xattn_bck': (0.0, 2.0),
     'L0_xattn_bcq': (0.0, 0.268),
     'L0_xattn_bcv': (0.0, 0.1),
     'L0_xattn_bp': (0.0, 0.1),
     'L0_ffn_gate_b': (0.0, 0.1),
     'L0_ffn_dp_b1': (0.0, 0.1),
     'L0_ffn_eb1': (0.0, 0.28),
     'L0_ffn_eb2': (0.0, 0.1),
     'L1_ffn_gamma': (1.0, 0.2),
     'L1_ffn_beta': (0.0, 0.337),
     'L1_ffn_b1': (0.0, 0.327),
     'L1_ffn_b2': (0.0, 0.1),
     'L2_xattn_bq': (0.0, 0.317),
     'L2_xattn_bk': (0.0, 2.0),
     'L2_xattn_bv': (0.0, 0.1),
     'L2_xattn_bo': (0.0, 0.1),
     'L2_ffn_g1': (1.0, 0.6),
     'L2_ffn_g2': (1.0, 0.6),
     'L3_attn_b_proj': (0.0, 0.1),
     'L3_ffn_b1': (0.0, 0.34),
     'L3_ffn_b2': (0.0, 0.1),
     'L3_ffn_rb': (0.0, 2.0)}
    factors = {'L1_attn_bgate': 8.0,
     'L2_attn_Wqkv_b': 2.741,
     'L2_attn_out_b': 2.883,
     'L2_ffn_w_router': 8.0,
     'L2_ffn_w1': 8.0,
     'L2_ffn_w2': 8.0,
     'L3_xattn_bo': 5.41,
     'L3_ffn_rw': 8.0}
    for name, (base, spread) in spreads.items():
        noise = np.random.default_rng([zlib.crc32(name.encode()), seed]).standard_normal(out[name].shape)
        drawn = base * np.exp(spread * noise) if base else spread * noise
        out[name] = jnp.asarray(drawn.astype(out[name].dtype))
    for name, factor in factors.items():
        out[name] = (out[name] * factor).astype(out[name].dtype)
    return out
```

```python
import concourse.bass as bass
from concourse import mybir
from contextlib import ExitStack
import numpy as np

F32 = mybir.dt.float32
BF16 = mybir.dt.bfloat16
I32 = mybir.dt.int32
ALU = mybir.AluOpType
ACT = mybir.ActivationFunctionType
AX = mybir.AxisListType
NCH = 8
START, STOP = 0, 12
RS8 = float(8 ** -0.5)
NEG = -1e30


class Tok:
    def __init__(self, sem=None, val=0):
        self.sem, self.val, self.used = sem, val, False


class Queues:
    def __init__(self, nc, ctx):
        self.nc, self.ctx = nc, ctx
        self.q = {k: [] for k in ("pe", "act", "dve", "pool", "sp")}
        self.nsem = 0
        self.dsems = []
        self.new_phase()

    def sem(self, name):
        self.nsem += 1
        return self.ctx.enter_context(self.nc.semaphore(f"{name}{self.nsem}"))

    def new_phase(self):
        self.sems = {k: self.sem("s_" + k) for k in ("pe", "act", "dve", "pool")}

    def add(self, eng, waits, fn):
        t = Tok(self.sems.get(eng))
        flat = []

        def walk(w):
            if isinstance(w, Tok):
                w.used = True
                flat.append(w)
            elif w is not None:
                for v in w:
                    walk(v)
        walk(waits)
        self.q[eng].append((fn, flat, t))
        return t

    def count(self):
        n = {}
        for eng in ("pe", "act", "dve", "pool"):
            for fn, waits, t in self.q[eng]:
                if t is not None and t.used:
                    n[t.sem.name] = n.get(t.sem.name, 0) + 1
                    t.val = n[t.sem.name]

    def emit(self, eng, e):
        seen = {}
        for fn, waits, t in self.q[eng]:
            need = {}
            for w in waits:
                if seen.get(w.sem.name, 0) < w.val and need.get(w.sem.name, (None, 0))[1] < w.val:
                    need[w.sem.name] = (w.sem, w.val)
            for n, (s, v) in need.items():
                e.wait_ge(s, v)
                seen[n] = v
            ins = fn(e)
            if t is not None and t.used:
                ins.then_inc(t.sem, 1)


class Slot:
    def __init__(self, ap):
        self.ap, self.rel, self.held = ap, [], False

    def take(self):
        assert not self.held
        self.held = True
        return self.rel

    def free(self, *toks):
        self.held = False
        self.rel = list(toks)


class Ring:
    def __init__(self, slots):
        self.slots, self.n = slots, 0

    def take(self):
        s = self.slots[self.n % len(self.slots)]
        self.n += 1
        return s, list(s.take())


class DSem:
    def __init__(self, Q, name):
        self.Q, self.sem, self.n = Q, Q.sem(name), 0
        Q.dsems.append(self)

    def dma(self, waits, out, in_, eng="sp"):
        self.n += 16
        sem = self.sem
        self.Q.add(eng, waits, lambda e: e.dma_start(out, in_).then_inc(sem, 16)).used = False
        t = Tok(self.sem, self.n)
        return t


def run_pipeline(gens, skew):
    live, nxt, t = [], 0, 0
    while live or nxt < len(gens):
        if nxt < len(gens) and t >= nxt * skew:
            live.append(gens[nxt])
            nxt += 1
        for g in list(live):
            try:
                next(g)
            except StopIteration:
                live.remove(g)
        t += 1


def program(nc, A, out, stop=12):
    ctx = ExitStack()
    with ctx:
        Q = Queues(nc, ctx)

        def sb(name, shape, dt=F32):
            return ctx.enter_context(nc.sbuf_tensor(name, shape, dt))

        def mm(w, o, l, r, s=True, t=True):
            return Q.add("pe", w, lambda e: e.matmul(o, l, r, start=s, stop=t))

        def tr(w, o, i, idn):
            return Q.add("pe", w, lambda e: e.transpose(o, i, idn))

        def act(w, o, i, f=ACT.Copy, scale=1.0, bias=0.0):
            return Q.add("act", w, lambda e: e.activation(o, i, f, bias=bias, scale=scale))

        def tt(w, o, a, b, op, eng="dve"):
            return Q.add(eng, w, lambda e: e.tensor_tensor(o, a, b, op))

        def ts(w, o, a, s1, s2, op0, op1=None, eng="dve"):
            if op1 is None:
                return Q.add(eng, w, lambda e: e.tensor_scalar(o, a, s1, None, op0))
            return Q.add(eng, w, lambda e: e.tensor_scalar(o, a, s1, s2, op0, op1))

        def stt(w, o, a, s, b, op0, op1):
            return Q.add("dve", w, lambda e: e.scalar_tensor_tensor(out=o, in0=a, scalar=s, in1=b, op0=op0, op1=op1))

        def red(w, o, i, op):
            return Q.add("dve", w, lambda e: e.tensor_reduce(o, i, axis=AX.X, op=op))

        def cp(w, o, i, eng="dve"):
            return Q.add(eng, w, lambda e: e.tensor_copy(o, i))

        def ms(w, o, v, eng="pool"):
            return Q.add(eng, w, lambda e: e.memset(o, v))

        def rcp(w, o, i):
            return Q.add("dve", w, lambda e: e.reciprocal(o, i))

        X = sb("X", [128, 32, 128])
        XT = sb("XT", [128, 4096])
        xtok = [None] * NCH
        xttok = [None] * NCH
        xtfree = [[] for _ in range(NCH)]
        PS = ctx.enter_context(nc.psum_tensor("ps", [128, 8, 512], F32))
        bank = [Slot(PS[:, i, :]) for i in range(8)]

        class Banks:
            def __init__(self, groups):
                self.groups, self.n = groups, 0

            def take(self):
                g = self.groups[self.n % len(self.groups)]
                self.n += 1
                w = [list(bank[i].take()) for i in g]
                ap = PS[:, g[0]:g[0] + len(g), :]

                class H:
                    pass
                h = H()
                h.ap = ap if len(g) > 1 else PS[:, g[0], :]

                def free(*toks):
                    for i in g:
                        bank[i].free(*toks)
                h.free = free
                return h, w
        MX = Banks([[0], [1]])
        ST = Banks([[2, 3], [4, 5]])
        PV = Banks([[6]])
        PJ = Banks([[7]])
        UP = Banks([[0], [1], [2], [3]])
        DN = Banks([[4], [5]])

        s_const = DSem(Q, "d_const")

        WB = sb("WB", [128, 5376])

        idf = sb("idf", [128, 128])
        idb = sb("idb", [128, 128], BF16)
        mskQ = sb("mskQ", [128, 128], BF16)
        mskK = sb("mskK", [128, 128], BF16)
        ones1 = sb("ones1", [1, 128])
        t = s_const.dma(None, idf[:, :], A["c_ident"])
        t = s_const.dma(None, mskQ[:, :].bitcast(F32), A["c_maskq"])
        t = s_const.dma(None, mskK[:, :].bitcast(F32), A["c_maskk"])
        t_c = s_const.dma(None, ones1[:, :], A["c_ones"][0:1, 0:128])
        pmask = sb("pmask", [128, 2])
        t_c = s_const.dma(None, pmask[:, :], A["c_pmask"])
        t_idb = cp(t_c, idb[:, :], idf[:, :])

        s_x = DSem(Q, "d_x")
        s_xt = DSem(Q, "d_xt")
        xd = s_x.dma(None, X[:, :, :], A["x"].rearrange("b (t p) d -> p (b t) d", p=128))
        xtd = s_xt.dma(None, XT[:, :], A["xT"])
        for c in range(NCH):
            xtok[c], xttok[c] = xd, xtd

        KS = [sb(f"KS{i}", [128, 16, 512], BF16) for i in range(2)]
        QS = [sb(f"QS{i}", [128, 8, 512], BF16) for i in range(2)]
        VA = [sb(f"VA{i}", [128, 64, 9]) for i in range(2)]
        zt = []
        for i in range(2):
            z = ms(None, KS[i][:, :, :].bitcast(I32), 0, eng="pool")
            ks_one = DSem(Q, "d_one")
            o1 = None
            for par in range(2):
                o1 = ks_one.dma(z, KS[i][96 + 2 * par:98 + 2 * par, 8 * par:8 * par + 8, :].bitcast(F32),
                                A["c_one2"].rearrange("p (a b) -> p a b", a=8))
            zq = ms(None, QS[i][96:128, :, :].bitcast(I32), 0, eng="dve")
            zv = ms(None, VA[i][:, :, 8:9], 1.0, eng="dve")
            zt.append([z, o1, zq, zv])
        KSr = Ring([Slot(KS[i]) for i in range(2)])
        QSr = Ring([Slot(QS[i]) for i in range(2)])
        QX = Slot(sb("QX", [128, 8, 512], BF16))
        QX.rel = [ms(None, QX.ap[96:128, :, :].bitcast(I32), 0, eng="dve")]
        QX.ds, QX.dm = DSem(Q, "d_qs"), [DSem(Q, "d_qm"), DSem(Q, "d_qm")]
        VAr = Ring([Slot(VA[i]) for i in range(2)])
        for i in range(2):
            KSr.slots[i].rel = list(zt[i])
            QSr.slots[i].rel = list(zt[i])
            VAr.slots[i].rel = list(zt[i])
            KSr.slots[i].ds = DSem(Q, "d_ks")
            QSr.slots[i].ds = DSem(Q, "d_qs")
            QSr.slots[i].dm = [DSem(Q, "d_qm"), DSem(Q, "d_qm")]

        def ring(name, n, shape, dt=F32):
            return Ring([Slot(sb(f"{name}{i}", shape, dt)) for i in range(n)])
        FF = ring("FF", 2, [128, 512])
        GG = ring("GG", 1, [128, 512])
        HH = ring("HH", 3, [128, 3, 512], BF16)
        M3 = ring("M3", 2, [128, 16, 4])
        MB = ring("MB", 2, [128, 2, 32], BF16)
        MT = ring("MT", 2, [32, 256], BF16)
        PT = ring("PT", 3, [128, 1024])
        RC = ring("RC", 2, [128, 32])
        OO = ring("OO", 2, [128, 2, 128])
        OC = ring("OC", 2, [128, 2, 128])
        OT = ring("OT", 2, [128, 512])
        RR = ring("RR", 2, [128, 4, 128])
        BS = ring("BS", 2, [128, 4, 6])
        MV = ring("MV", 2, [128, 4, 2])
        RSD = ring("RSD", 2, [128, 4])
        BIG = sb("BIG", [128, 10752])

        QSLOT = (0, 0, 0, 1, 1, 2)
        KSLOT = (0, 1, 2, 0, 1, 0)

        def split3(src, ts_, w):
            hh, wh = HH.take()
            t1 = act([ts_, wh], hh.ap[:, 0, 0:w], src[:, 0:w])
            t2 = tt([ts_, t1], src[:, 0:w], src[:, 0:w], hh.ap[:, 0, 0:w], ALU.subtract, eng="pool")
            t3 = act(t2, hh.ap[:, 1, 0:w], src[:, 0:w])
            t4 = tt([t2, t3], hh.ap[:, 2, 0:w], src[:, 0:w], hh.ap[:, 1, 0:w], ALU.subtract, eng="pool")
            return hh, [t1, t3, t4], t4

        def stack_q(hh, ht, slot, wslot):
            t = None
            for par in range(2):
                for s in range(6):
                    t = slot.ds.dma([ht, wslot], slot.ap[48 * par + 8 * s:48 * par + 8 * s + 8, :, :],
                                    hh.ap[64 * par:64 * par + 64, QSLOT[s], :])
            return t

        def stack_k(hh, ht, slot, wslot):
            t = None
            for par in range(2):
                for s in range(6):
                    t = slot.ds.dma([ht, wslot], slot.ap[48 * par + 8 * s:48 * par + 8 * s + 8, 8 * par:8 * par + 8, :],
                                    hh.ap[64 * par:64 * par + 64, KSLOT[s], :])
            return t

        def project(xt, xtt, W, wt, b, rope):
            pj, wp = PJ.take()
            t1 = mm([wp, xtt, wt], pj.ap, W[0], xt)
            ff, wf = FF.take()
            if rope is None:
                if b is None:
                    t2 = act([t1, wf], ff.ap[:, :], pj.ap)
                else:
                    t2 = act([t1, wf, wt], ff.ap[:, :], pj.ap, ACT.Identity, bias=b[0])
                pj.free(t2)
                return ff, t2
            gg, wg = GG.take()
            bias0 = b[0] if b is not None else 0.0
            t2 = stt([t1, wf, rope[2], wt], ff.ap[:, :], pj.ap, bias0, rope[0], ALU.add, ALU.mult)
            pj.free(t2)
            pj, wp = PJ.take()
            t3 = mm([wp], pj.ap, W[1], xt)
            bias1 = b[1] if b is not None else 0.0
            t4 = stt([t3, wg], gg.ap[:, :], pj.ap, bias1, rope[1], ALU.add, ALU.mult)
            pj.free(t4)
            t5 = tt([t2, t4], ff.ap[:, :], ff.ap[:, :], gg.ap[:, :], ALU.add, eng="pool")
            gg.free(t5)
            return ff, t5

        def shift_rows(m, tm, qslot, bb, order):
            mb, wm = MB.take()
            m3 = m.ap[:, :, :]
            for qt in range(2):
                if order == "self":
                    v = m3[:, :, qt:qt + 1].rearrange("p (a b) o -> p a (b o)", a=2)
                else:
                    v = m3[:, :, qt:qt + 1].rearrange("p (b a) o -> p a (b o)", a=2)
                o = mb.ap[:, qt, :].rearrange("p (a s b) -> p a s b", a=2, s=2)
                t1 = ts([tm, wm], o[:, :, 0, :], v, -1.0, None, ALU.mult)
                t2 = stt([t1], o[:, :, 1, :], v, -1.0, o[:, :, 0, :], ALU.mult, ALU.subtract)
            m.free(t2)
            pj, wp = PJ.take()
            pb = pj.ap.bitcast(BF16)
            for qt in range(2):
                t3 = tr([t2, wp, t_idb], pb[0:32, 128 * qt:128 * qt + 128], mb.ap[:, qt, :], idb[:, :])
            mb.free(t3)
            mt, wt = MT.take()
            t4 = cp([t3, wt], mt.ap[:, :], pb[0:32, 0:256])
            pj.free(t4)
            t5 = qslot.dm[bb].dma([t4], qslot.ap[96:100, :, 256 * bb:256 * bb + 256], mt.ap[:, :])
            mt.free(t5)
            return t5

        def normalise(pv, tp, oo, wo, order):
            rc, wr = RC.take()
            v = pv.ap[:, 0:288].rearrange("p (a k) -> p a k", k=9)
            t1 = rcp([tp, wr], rc.ap[:, :], v[:, :, 8:9].rearrange("p a o -> p (a o)"))
            for qt in range(2):
                o = oo.ap[:, qt, :].rearrange("p (h d b) -> p h d b", h=2, d=8)
                o = o.rearrange("p h d b -> p h b d") if order == "self" else o.rearrange("p h d b -> p b h d")
                a = 2 if order == "self" else 8
                i = v[:, 16 * qt:16 * qt + 16, 0:8].rearrange("p (x y) k -> p x y k", x=a)
                r = rc.ap[:, 16 * qt:16 * qt + 16].rearrange("p (x y k) -> p x y k", x=a, k=1)
                r = r.to_broadcast([128, a, 16 // a, 8])
                t2 = tt([t1, wo], o, i, r, ALU.mult)
            pv.free(t2)
            rc.free(t2)
            return t2

        def self_scores(qs, qt_, ks, kt_, va, vt, mode, bias, pt_rope, bb, res):
            causal = mode in ("causal", "bias")
            m3, wm = M3.take()
            for hh in range(16):
                blk = hh % 8
                mx, wx = MX.take()
                q0 = qs.ap[0:96, blk, 256 * bb:256 * bb + 256]
                k0 = ks.ap[0:96, hh, 256 * bb:256 * bb + 256]
                lasts = mode == "none"
                if causal:
                    parts = [(0, 0, 128), (1, 128, 256)]
                else:
                    parts = [(0, 0, 256), (1, 256, 256)]
                for qt, o, n in parts:
                    mm([wx, qt_, kt_], mx.ap[:, o:o + n], q0[:, 128 * qt:128 * qt + 128], k0[:, 0:n], t=lasts)
                    if mode == "bias":
                        off = 256 - n
                        t1 = mm([bias[2]], mx.ap[:, o:o + n], idb[:, :], bias[0][:, hh, off:off + n], s=False)
                    elif mode == "causal":
                        t1 = mm([t_c, t_idb], mx.ap[:, o + n - 128:o + n], idb[:, :], mskQ[:, :], s=False)
                    elif mode == "add":
                        if qt == 0:
                            t1 = mm([bias[4], t_idb], mx.ap[:, o:o + 256], idb[:, :], bias[0][:, 0:256], s=False)
                        else:
                            t1 = mm([bias[4], t_idb], mx.ap[:, o + 128:o + 256], idb[:, :], bias[0][:, 0:128], s=False)
                    else:
                        t1 = None
                last = Q.q["pe"][-1][2]
                if causal:
                    t2 = red([last, wm], m3.ap[:, hh, 0:3], mx.ap[:, 0:384].rearrange("p (a k) -> p a k", a=3), ALU.max)
                else:
                    t2 = red([last, wm], m3.ap[:, hh, 0:2], mx.ap.rearrange("p (a k) -> p a k", a=2), ALU.max)
                mx.free(t2)
                yield
            if causal:
                t2 = tt([t2], m3.ap[:, :, 1], m3.ap[:, :, 1], m3.ap[:, :, 2], ALU.max)
            ds = shift_rows(m3, t2, qs, bb, "self")
            yield
            yield
            yield
            pv, wv = PV.take()
            pvv = pv.ap[:, 0:288].rearrange("p (q h k) -> p q h k", q=2, h=16)
            for hp in range(8):
                st, wst = ST.take()
                pt, wpt = PT.take()
                for par in range(2):
                    hh, blk = 8 * par + hp, hp
                    q1 = qs.ap[0:100, blk, 256 * bb:256 * bb + 256]
                    k1 = ks.ap[0:100, hh, 256 * bb:256 * bb + 256]
                    s_ = st.ap[:, par, :]
                    done = mode == "none"
                    mm([wst, ds], s_[:, 0:256], k1[:, 0:128], q1, t=done)
                    if mode == "bias":
                        mm([bias[3]], s_[:, 0:256], idf[:, :], bias[1][:, hh, 0:256], s=False)
                    elif mode == "causal":
                        mm(None, s_[:, 0:128], idb[:, :], mskK[:, :], s=False)
                    elif mode == "add":
                        mm([bias[4]], s_[:, 0:128], idb[:, :], bias[1], s=False, t=False)
                        mm([bias[4]], s_[:, 0:128], idb[:, :], bias[2], s=False, t=True)
                    if causal:
                        mm(None, s_[:, 256:384], k1[:, 128:256], q1[:, 128:256], t=False)
                        if mode == "bias":
                            t3 = mm(None, s_[:, 256:384], idf[:, :], bias[1][:, hh, 0:128], s=False)
                        else:
                            t3 = mm(None, s_[:, 256:384], idb[:, :], mskK[:, :], s=False)
                    else:
                        t3 = mm(None, s_[:, 256:512], k1[:, 128:256], q1, t=done)
                        if mode == "add":
                            mm(None, s_[:, 256:512], idb[:, :], bias[5], s=False, t=False)
                            t3 = mm(None, s_[:, 256:512], idb[:, :], bias[6], s=False, t=True)
                n = 384 if causal else 512
                pp = pt.ap[:, 0:2 * n].rearrange("p (a k) -> p a k", a=2)
                t4 = act([t3, wpt], pp, st.ap[:, :, 0:n], ACT.Exp, scale=RS8)
                st.free(t4)
                yield
                for par in range(2):
                    hh = 8 * par + hp
                    if causal:
                        seq = [(0, 0, 0, True, True), (1, 0, 128, True, False), (1, 1, 256, False, True)]
                    else:
                        seq = [(0, 0, 0, True, False), (0, 1, 256, False, True),
                               (1, 0, 128, True, False), (1, 1, 384, False, True)]
                    for qt, kt, o, s, e in seq:
                        t5 = mm([t4, wv, vt], pvv[:, qt, hh, :], pp[:, par, o:o + 128],
                                va.ap[:, (2 * bb + kt) * 16 + hh, :], s=s, t=e)
                pt.free(t5)
            oo, wo = OO.take()
            t6 = normalise(pv, t5, oo, wo, "self")
            res.append((oo, t6, t5))
            yield

        def to_ot(oo, to, ot, wot, bb):
            pj, wp = PJ.take()
            for qt in range(2):
                t1 = tr([to, wp, t_c], pj.ap[:, 128 * qt:128 * qt + 128], oo.ap[:, qt, :], idf[:, :])
            oo.free(t1)
            t2 = act([t1, wot], ot.ap[:, 256 * bb:256 * bb + 256], pj.ap[:, 0:256])
            pj.free(t2)
            return t2

        EPS = 1e-5
        NW = ring("NW", 2, [128, 3, 4])

        def rsqrt(w, o, v, eps):
            nw, wn = NW.take()
            a, y, t = (nw.ap[:, i, :] for i in range(3))
            k = ts([w, wn], a, v, eps, None, ALU.add)
            k = ts(k, y.bitcast(I32), a.bitcast(I32), 1, None, ALU.logical_shift_right)
            k = ts(k, y.bitcast(I32), y.bitcast(I32), -1.0, float(0x5F3759DF), ALU.mult, ALU.add)
            for i in range(3):
                k = tt(k, t, y, y, ALU.mult, eng="pool")
                k = tt(k, t, t, a, ALU.mult, eng="pool")
                k = ts(k, t, t, -0.5, 1.5, ALU.mult, ALU.add, eng="pool")
                k = tt(k, y if i < 2 else o, y, t, ALU.mult, eng="pool")
            nw.free(k)
            return k

        def layer_norm(c, r, tr_, eps_out=None, xn=None):
            bs, wb = BS.take()
            mv, wv = MV.take()
            rs, wr = RSD.take()
            for i in range(4):
                t1 = Q.add("dve", [tr_, wb], lambda e, i=i: e.bn_stats(bs.ap[:, i, :], r[:, i, :]))
            for i in range(4):
                t2 = Q.add("dve", [t1, wv], lambda e, i=i: e.bn_aggr(mv.ap[:, i, :], bs.ap[:, i, :]))
            bs.free(t2)
            t3 = rsqrt([t2, wr], rs.ap[:, 0:4], mv.ap[:, :, 1], EPS)
            for i in range(4):
                t4 = ts([t3, xtok[c]], X[:, 4 * c + i, :], r[:, i, :], mv.ap[:, i, 0:1], rs.ap[:, i:i + 1],
                        ALU.subtract, ALU.mult)
            mv.free(t4)
            rs.free(t4)
            xtok[c] = t4
            return t4

        def transpose_x(c, src, t4):
            pj, wp = PJ.take()
            for i in range(4):
                t5 = tr([t4, wp, t_c], pj.ap[:, 128 * i:128 * i + 128], src[:, i, :], idf[:, :])
            t6 = act([t5, xtfree[c]], XT[:, 512 * c:512 * c + 512], pj.ap)
            pj.free(t6)
            xttok[c] = t6
            xtfree[c] = []
            return t5

        def out_proj(c, ot, tot, Wo, wt, bo, readers, last=False, xn=None, keep=None):
            pj, wp = PJ.take()
            t1 = None
            for i in range(4):
                o = pj.ap[:, 128 * i:128 * i + 128]
                t1 = mm([wp, tot, wt], o, ot.ap[:, 128 * i:128 * i + 128], Wo, t=bo is None)
                if bo is not None:
                    t1 = mm([t_c], o, ones1[:, :], bo, s=False)
            ot.free(t1)
            rr, wr = RR.take()
            t2 = tt([t1, wr, xtok[c]], rr.ap[:, :, :], pj.ap.rearrange("p (a b) -> p a b", a=4),
                    X[:, 4 * c:4 * c + 4, :], ALU.add)
            pj.free(t2)
            yield
            if keep is not None:
                xtfree[c] = readers
                x = X[:, 4 * c:4 * c + 4, :]
                xtok[c] = tt(t2, x, x, rr.ap[:, :, :], ALU.add, eng="pool")
                yield from keep(c, t2, rr.ap[:, :, :])
                rr.free(xtok[c], xttok[c])
                return
            t4 = layer_norm(c, rr.ap, t2)
            rr.free(t4)
            yield
            xtfree[c] = readers
            if xn is None:
                transpose_x(c, X[:, 4 * c:4 * c + 4, :], t4)
            else:
                yield from xn(c, t4)
            yield

        def values(c, xt, xtt, Wv, wt, bv):
            va, wv = VAr.take()
            pj, wp = PJ.take()
            for i in range(4):
                o = pj.ap[:, 128 * i:128 * i + 128]
                t1 = mm([wp, xtt, wt], o, xt[:, 128 * i:128 * i + 128], Wv, t=bv is None)
                if bv is not None:
                    t1 = mm([t_c], o, ones1[:, :], bv, s=False)
            t2 = act([t1, wv], va.ap[:, :, 0:8], pj.ap.rearrange("p (a k) -> p a k", k=8))
            pj.free(t2)
            return va, t2, t1

        def self_attention(c, Wd, mode, rope=None, bias=None, reps=1, gate=None, cross=None, last=False, xn=None, keep=None):
            xt, xtt = XT[:, 512 * c:512 * c + 512], xttok[c]
            wt = Wd["t"]
            rp = None
            if rope is not None:
                rp = rope
            qs, wq = QSr.take()
            ks, wk = KSr.take()
            ff, tf = project(xt, xtt, Wd["q"], wt, Wd["qb"], rp)
            yield
            hq, hqt, fr = split3(ff.ap, tf, 512)
            ff.free(fr)
            yield
            qd = stack_q(hq, hqt, qs, wq)
            hq.free(qd)
            ff, tf = project(xt, xtt, Wd["k"], wt, Wd["kb"], rp)
            yield
            hk, hkt, fr = split3(ff.ap, tf, 512)
            ff.free(fr)
            yield
            kd = stack_k(hk, hkt, ks, wk)
            hk.free(kd)
            va, vt, rd = values(c, xt, xtt, Wd["v"], wt, Wd["vb"])
            yield
            yield
            yield
            for rep in range(reps):
                ot, wot = OT.take()
                for bb in range(2):
                    res = []
                    yield from self_scores(qs, qd, ks, kd, va, vt, mode, bias, None, bb, res)
                    oo, to, tpv = res[0]
                    if cross is not None:
                        oc, tc = yield from cross(c, bb)
                        to = tt([to, tc], oo.ap[:, :, :], oo.ap[:, :, :], oc.ap[:, :, :], ALU.add, eng="pool")
                        oc.free(to)
                    if gate is not None:
                        to, rd = yield from gate(c, bb, oo, to)
                    tot = to_ot(oo, to, ot, wot, bb)
                    yield
                if rep < reps - 1:
                    hq, hqt, fr = split3(ot.ap, tot, 512)
                    ot.free(fr)
                    qd = stack_q(hq, hqt, qs, [tpv])
                    hq.free(qd)
                    yield
                    yield
            qs.free(tpv)
            ks.free(tpv)
            va.free(tpv)
            yield from out_proj(c, ot, tot, Wd["o"], wt, Wd["ob"], [rd, tpv], xn=xn, keep=keep)

        def ends(*engs):
            return [Q.q[k][-1][2] for k in (engs or ("pe", "act", "dve", "pool"))]

        class WL:
            turn = 0
            done = [[], []]

        def load_weights(names):
            Q_ = {}
            ds = DSem(Q, "d_w")
            half = WL.turn % 2
            WL.turn += 1
            base = half * 2688
            pos = base
            t = None
            w = WL.done[half]
            for key, name in names:
                ap = A[name]
                k, n = ap.shape
                dst = WB[0:k, pos:pos + n]
                if ap.dtype != F32:
                    ap = ap.bitcast(F32)
                pos += n
                assert pos <= base + 2688, name
                Q_[key] = dst
                t = ds.dma(w, dst, ap)
            Q_["t"] = t
            Q_["half"] = half
            return Q_

        def weights_done(wd):
            WL.done[wd["half"]] = ends()

        SELF = [("q0", "wq"), ("q1", "wqs"), ("k0", "wk"), ("k1", "wks"), ("v", "wv"), ("o", "wo"),
                ("qb0", "bq"), ("qb1", "bqs"), ("kb0", "bk"), ("kb1", "bks"), ("vb", "bv"), ("ob", "bo")]

        def self_weights(pre, extra=()):
            names = [(k, f"{pre}_{n}") for k, n in SELF if f"{pre}_{n}" in A] + list(extra)
            w = load_weights(names)
            w["q"] = (w["q0"], w.get("q1"))
            w["k"] = (w["k0"], w.get("k1"))
            w["qb"] = (w["qb0"], w.get("qb1")) if "qb0" in w else None
            w["kb"] = (w["kb0"], w.get("kb1")) if "kb0" in w else None
            w.setdefault("vb", None)
            w.setdefault("ob", None)
            return w

        def rope_tables(name, after):
            ds = DSem(Q, "d_rope")
            C, S = BIG[:, 0:512], BIG[:, 512:1024]
            ds.dma(after, C, A[name + "_c"])
            t = ds.dma(after, S, A[name + "_s"])
            return (C, S, t)

        CT = sb("CT", [64, 2048])
        ct_t = DSem(Q, "d_ct").dma(None, CT[:, :], A["ctxT"])
        KC = BIG[:, 0:8192].bitcast(BF16).rearrange("p (a b q k) -> p a b q k", a=8, b=16, q=2)
        VB = BIG[:, 8192:8192 + 2304].rearrange("p (b a k) -> p b a k", b=16, a=8)

        class BigMem:
            free = None

        def cross_setup(Wk, bk, Wv, bv, wt):
            z2 = ms(BigMem.free, BIG[:, 8192:8192 + 2304], 0.0, eng="dve")
            ds = DSem(Q, "d_kc")
            kone = ds.dma(BigMem.free, BIG[96:100, 0:8192], A["c_kc"])
            v1 = ms(z2, VB[0:64, :, :, 8:9], 1.0, eng="dve")
            v2 = ms(z2, VB[64:128, :, :, 17:18], 1.0, eng="dve")
            kt = None
            for n in range(2):
                pj, wp = PJ.take()
                t1 = mm([wp, ct_t, wt], pj.ap.rearrange("p (a b) -> p a b", a=8), Wk,
                        CT[:, 1024 * n:1024 * n + 1024].rearrange("p (a q b) -> p a q b", a=8, q=2)[:, :, 0, :])
                ff, wf = FF.take()
                if bk is None:
                    t2 = act([t1, wf], ff.ap[:, :], pj.ap)
                else:
                    t2 = act([t1, wf], ff.ap[:, :], pj.ap, ACT.Identity, bias=bk)
                pj.free(t2)
                hk, hkt, fr = split3(ff.ap, t2, 512)
                ff.free(fr)
                qs, wq = QSr.take()
                for par in range(2):
                    for s in range(6):
                        kd = qs.ds.dma([hkt, wq], qs.ap[48 * par + 8 * s:48 * par + 8 * s + 8, :, :],
                                       hk.ap[64 * par:64 * par + 64, KSLOT[s], :])
                hk.free(kd)
                sv = qs.ap[0:96, :, :].rearrange("p a (b k) -> p a b k", b=8)
                k1 = act([kd, BigMem.free, t_c], KC[0:96, :, 8 * n:8 * n + 8, 0, :], sv, ACT.Copy,
                         scale=pmask[0:96, 0:1])
                k2 = ts([kd, BigMem.free, t_c], KC[0:96, :, 8 * n:8 * n + 8, 1, :], sv, pmask[0:96, 1:2], None,
                        ALU.mult)
                qs.free(k1, k2)
                kt = [k1, k2, kone]
            for r in range(4):
                pj, wp = PJ.take()
                for i in range(4):
                    b = 4 * r + i
                    l = CT[:, 128 * b:128 * b + 128]
                    o = pj.ap[:, 128 * i:128 * i + 128]
                    t1 = mm([wp, ct_t, wt], o, l, Wv, t=bv is None)
                    if bv is not None:
                        t1 = mm([t_c], o, ones1[:, :], bv, s=False)
                v = pj.ap.rearrange("p (i q k) -> p i q k", i=4, q=16)
                t2 = act([t1, z2], VB[0:64, 4 * r:4 * r + 4, :, 0:8], v[0:64, :, 0:8, :])
                t3 = act([t1, z2], VB[64:128, 4 * r:4 * r + 4, :, 9:17], v[64:128, :, 8:16, :])
                pj.free(t2, t3)
            return kt, [t2, t3, v1, v2]

        def cross_scores(qs, qd, kct, vbt, b, bb):
            m3, wm = M3.take()
            for qt in range(2):
                for half in range(2):
                    mx, wx = MX.take()
                    for i in range(4):
                        blk = 4 * half + i
                        t1 = mm([wx, qd, kct], mx.ap[:, 128 * i:128 * i + 128],
                                qs.ap[0:96, blk, 256 * bb + 128 * qt:256 * bb + 128 * qt + 128],
                                KC[0:96, blk, b, :, :].rearrange("p a k -> p (a k)"))
                    t2 = red([t1, wm], m3.ap[:, 8 * half:8 * half + 8, qt],
                             mx.ap.rearrange("p (a k) -> p a k", a=8), ALU.max)
                    mx.free(t2)
                yield
            dm = shift_rows(m3, t2, qs, bb, "cross")
            yield
            yield
            yield
            yield
            pv, wv = PV.take()
            pvv = pv.ap[:, 0:288].rearrange("p (q h k) -> p q h k", q=2, h=8)
            for half in range(2):
                st, wst = ST.take()
                sv = st.ap.rearrange("p a (b k) -> p (a b) k", b=2)
                for i in range(4):
                    blk = 4 * half + i
                    t3 = mm([wst, dm], sv[:, i, :], KC[0:100, blk, b, :, :].rearrange("p a k -> p (a k)"),
                            qs.ap[0:100, blk, 256 * bb:256 * bb + 256])
                pt, wpt = PT.take()
                t4 = act([t3, wpt], pt.ap.rearrange("p (a k) -> p a k", a=2), st.ap, ACT.Exp, scale=RS8)
                st.free(t4)
                yield
                for i in range(4):
                    for qt in range(2):
                        t5 = mm([t4, wv, vbt], pvv[:, qt, 4 * half + i, :],
                                pt.ap[:, 256 * i + 128 * qt:256 * i + 128 * qt + 128], VB[:, b, 4 * half + i, :])
                pt.free(t5)
            oo, wo = OC.take()
            t6 = normalise(pv, t5, oo, wo, "cross")
            yield
            return oo, t6, t5

        def cross_attention(c, Wd, kct, vbt, xn=None):
            xt, xtt = XT[:, 512 * c:512 * c + 512], xttok[c]
            qs, wq = QSr.take()
            ff, tf = project(xt, xtt, Wd["q"], Wd["t"], Wd["qb"], None)
            rd = Q.q["pe"][-1][2]
            yield
            hq, hqt, fr = split3(ff.ap, tf, 512)
            ff.free(fr)
            qd = stack_q(hq, hqt, qs, wq)
            hq.free(qd)
            for _ in range(4):
                yield
            ot, wot = OT.take()
            for bb in range(2):
                oo, to, tpv = yield from cross_scores(qs, qd, kct, vbt, 2 * c + bb, bb)
                tot = to_ot(oo, to, ot, wot, bb)
                yield
            qs.free(tpv)
            yield from out_proj(c, ot, tot, Wd["o"], Wd["t"], Wd["ob"], [rd], xn=xn)

        ATT_SKEW = 40
        CRS_SKEW = 14

        def rms_input(g, tg):
            def f(c, t4, own=False):
                rr, wr = RR.take()
                t5 = rms_scale(c, t4, rr, wr, own)
                yield
                pj, wp = PJ.take()
                for i in range(4):
                    t6 = tr([t5, wp], pj.ap[:, 128 * i:128 * i + 128], rr.ap[:, i, :], idf[:, :])
                rr.free(t6)
                t7 = act([t6, xtfree[c], tg], XT[:, 512 * c:512 * c + 512], pj.ap, ACT.Copy, scale=g)
                pj.free(t7)
                xttok[c] = t7
                xtfree[c] = []
            return f

        def rms_scale(c, t4, rr, wr, own=False):
            rs, wrs = RSD.take()
            bs, wb = BS.take()
            x = own if own else X[:, 4 * c:4 * c + 4, :]
            k = tt([t4, wr], rr.ap[:, :, :], x, x, ALU.mult, eng="pool")
            k = red([k, wb], bs.ap[:, :, 0], rr.ap[:, :, :], ALU.add)
            k = ts(k, bs.ap[:, :, 1], bs.ap[:, :, 0], 1.0 / 128, None, ALU.mult)
            k = rsqrt([k, wrs], rs.ap[:, 0:4], bs.ap[:, :, 1], 1e-6)
            bs.free(k)
            for i in range(4):
                k = ts(k, rr.ap[:, i, :], x[:, i, :], rs.ap[:, i:i + 1], None, ALU.mult)
            rs.free(k)
            return k

        def sub(n):
            on = START <= n < STOP
            if on:
                Q.new_phase()
            return on

        if sub(0):
            w = self_weights("L0a")
            rope = rope_tables("rope0", None)
            run_pipeline([self_attention(c, w, "none", rope=rope) for c in range(NCH)], ATT_SKEW)
            weights_done(w)
            BigMem.free = ends("dve")

        if sub(1):
            w = self_weights("L0x", [("cq", "L0x_wcq"), ("ck", "L0x_wck"), ("cv", "L0x_wcv"),
                                     ("cqb", "L0x_bcq"), ("ckb", "L0x_bck"), ("cvb", "L0x_bcv")])
            kct, vbt = cross_setup(w["ck"], w["ckb"], w["cv"], w["cvb"], w["t"])

            class CrossQ:
                cur = {}

            def cross0(c, bb):
                if bb == 0:
                    xt = XT[:, 512 * c:512 * c + 512]
                    wq = list(QX.take())
                    ff, tf = project(xt, xttok[c], (w["cq"],), w["t"], (w["cqb"],), None)
                    yield
                    hq, hqt, fr = split3(ff.ap, tf, 512)
                    ff.free(fr)
                    qd = stack_q(hq, hqt, QX, wq)
                    hq.free(qd)
                    CrossQ.cur[c] = qd
                    for _ in range(4):
                        yield
                oc, tc, tpv = yield from cross_scores(QX, CrossQ.cur[c], kct, vbt, 2 * c + bb, bb)
                if bb == 1:
                    QX.free(tpv)
                return oc, tc
            run_pipeline([self_attention(c, w, "causal", cross=cross0) for c in range(NCH)], 66)
            weights_done(w)
            BigMem.free = ends("pe")

        WE = [BIG[:, 1032 * i:1032 * i + 1028] for i in range(3)]
        HB = [Slot(BIG[:, 3096 + 2048 * i:3096 + 2048 * i + 2048].rearrange("p (a b) -> p a b", a=4)) for i in range(3)]
        GW = BIG[:, 9240:9752].rearrange("p (t e) -> p t e", e=16)
        GS = [Slot(BIG[:, 9752 + 384 * i:9752 + 384 * i + 384].rearrange("p (a t e) -> p a t e", a=6, t=4))
              for i in range(2)]

        def bc(ap, shape, pat, **kw):
            return ap.rearrange(pat, **kw).to_broadcast(shape)

        def ranks(k, o, v, E, tri):
            a, wa = PT.take()
            b, wb = PT.take()
            sh = [128, 4, E, E]
            va = a.ap[:, 0:4 * E * E].rearrange("p (t x y) -> p t x y", t=4, x=E)
            vb = b.ap[:, 0:4 * E * E].rearrange("p (t x y) -> p t x y", t=4, x=E)
            oth = bc(v, sh, "p t (o e) -> p t o e", o=1)
            own = bc(v, sh, "p t (e o) -> p t e o", o=1)
            k1 = tt([k, wa], va, oth, own, ALU.is_gt)
            k2 = tt([k, wb], vb, oth, own, ALU.is_equal)
            for t in range(4):
                k3 = tt(k2, vb[:, t], vb[:, t], tri.rearrange("p (x y) -> p x y", x=16)[:, 0:E, 0:E], ALU.mult, eng="pool")
            k4 = tt([k1, k3], va, va, vb, ALU.add, eng="pool")
            k5 = red(k4, o, va, ALU.add)
            a.free(k5)
            b.free(k4)
            return k5

        def gate_unit(c, E, w, gw, gb, kind, res):
            xt, xtt = XT[:, 512 * c:512 * c + 512], xttok[c]
            gs, wg = GS[c % 2], list(GS[c % 2].take())
            lg, rk, ex, sm, mx = (gs.ap[:, i, :, 0:E] for i in range(5))
            pj, wp = PJ.take()
            for i in range(4):
                o = pj.ap[:, 16 * i:16 * i + E]
                k = mm([wp, xtt, w["t"], gw[1]], o, xt[:, 128 * i:128 * i + 128], gw[0], t=gb is None)
                if gb is not None:
                    k = mm([gw[1]], o, ones1[:, :], gb, s=False)
            rd = k
            k = cp([k, wg], lg, pj.ap[:, 0:64].rearrange("p (t e) -> p t e", t=4)[:, :, 0:E])
            pj.free(k)
            kt = None
            if kind == "L0":
                pj, wp = PJ.take()
                k1 = mm(wp, pj.ap[0:64, :], w["dw1"], xt)
                ff, wf = FF.take()
                k1 = act([k1, wf], ff.ap[0:64, :], pj.ap[0:64, :], ACT.Relu, bias=w["db1"])
                pj.free(k1)
                yield
                pj, wp = PJ.take()
                for i in range(4):
                    mm([wp, k1], pj.ap[:, i:i + 1], ff.ap[0:64, 128 * i:128 * i + 128], w["dw2"], t=False)
                    k1 = mm(None, pj.ap[:, i:i + 1], ones1[:, :], w["db2"], s=False)
                ff.free(k1)
                z, a, e = (gs.ap[:, 5, i, 0:4] for i in range(3))
                k1 = cp(k1, z, pj.ap[:, 0:4])
                pj.free(k1)
                k1 = act(k1, a, z, ACT.Abs)
                k1 = act(k1, a, a, ACT.Exp, scale=-1.0)
                k1 = ts(k1, a, a, 1.0, None, ALU.add)
                k1 = act(k1, a, a, ACT.Ln)
                k1 = stt(k1, z, z, 0.0, a, ALU.max, ALU.add)
                k1 = ts(k1, z, z, -0.5, 1.0 / 1.5, ALU.add, ALU.mult)
                k1 = ts(k1, z, z, 0.0, 1.0, ALU.max, ALU.min)
                k1 = ts(k1, z, z, 3.0, 1.0, ALU.mult, ALU.add)
                ka = ts(k1, a, z, 1.5, 1.0, ALU.is_ge, ALU.add)
                ka = stt(ka, e, z, 2.5, a, ALU.is_gt, ALU.add)
                kt = stt(ka, a, z, 3.5, e, ALU.is_ge, ALU.add)
            yield
            if kind != "L2":
                kr = ranks(k, rk, lg, E, w["tri"])
                if kind == "L0":
                    kr = tt([kr, kt], rk, rk, bc(a, [128, 4, E], "p (t o) -> p t o", o=1), ALU.is_lt)
                else:
                    kr = ts(kr, rk, rk, 1.5 if kind == "L1" else 3.5, None, ALU.is_lt)
            yield
            k1 = red(k, sm[:, :, 0:1], lg, ALU.max)
            k1 = tt(k1, ex, lg, bc(sm[:, :, 0:1], [128, 4, E], "p t o -> p t o"), ALU.subtract)
            k1 = act(k1, ex, ex, ACT.Exp)
            if kind != "L2":
                k1 = tt([k1, kr], ex, ex, rk, ALU.mult)
            k1 = red(k1, sm[:, :, 0:1], ex, ALU.add)
            k1 = rcp(k1, sm[:, :, 1:2], sm[:, :, 0:1])
            g = GW[:, 4 * c:4 * c + 4, 0:E]
            k1 = tt([k1, BigMem.free], g, ex, bc(sm[:, :, 1:2], [128, 4, E], "p t o -> p t o"), ALU.mult)
            yield
            if kind == "L2":
                kr = ranks(k1, rk, g, E, w["tri"])
                k1 = stt(kr, g, rk, 1.5, g, ALU.is_lt, ALU.mult)
                gs.free(k1)
                res[c] = k1
                return
            res[c] = k1
            if kind == "L1":
                k2 = red(k1, sm[:, :, 2:3], g, ALU.add)
                for i in range(4):
                    x = X[:, 4 * c + i, :]
                    xtok[c] = stt([k2, xtok[c]], x, x, sm[:, i, 2:3], x, ALU.mult, ALU.add)
            gs.free(k1, xtok[c])
            pj, wp = PJ.take()
            for i in range(4):
                k2 = tr([k1, wp], pj.ap[0:E, 128 * i:128 * i + 128], g[:, i, :], idf[:, :])
            ff, wf = FF.take()
            k2 = cp([k2, wf], ff.ap[0:E, :], pj.ap[0:E, :])
            pj.free(k2)
            yield
            pj, wp = PJ.take()
            for i in range(4):
                k3 = mm([k2, wp], pj.ap[:, 128 * i:128 * i + 128], ff.ap[0:E, 128 * i:128 * i + 128], w["b2"])
            ff.free(k3)
            x = X[:, 4 * c:4 * c + 4, :]
            xtok[c] = tt([k3, xtok[c]], x, x, pj.ap.rearrange("p (a b) -> p a b", a=4), ALU.add)
            pj.free(xtok[c])
            yield

        def experts(E, F, w1, w2, b1, func, gates, kind=None, w=None, xn=None, done=None):
            nh = F // 128
            ds = [DSem(Q, "d_we") for _ in range(3)]
            wtok = {}
            last = {}
            slotfree = [BigMem.free] * 3

            def load(e):
                i = e % 3
                ds[i].dma(slotfree[i], WE[i][:, 0:F], A[w1][e])
                if b1:
                    ds[i].dma(slotfree[i], WE[i][:, 1024:1024 + nh], A[b1][e])
                wtok[e] = ds[i].dma(slotfree[i], WE[i][:, 512:512 + nh * 128], A[w2][e])
            load(0)
            load(1)
            for h in HB:
                h.rel = BigMem.free or []

            def unit(e, c):
                if c == 0 and e + 2 < E:
                    load(e + 2)
                we = WE[e % 3]
                xin, xtt = XT[:, 512 * c:512 * c + 512], xttok[c]
                nx = None
                if kind == "L1":
                    nx, wn = FF.take()
                    xtt = ts([xtt, wn, w["t"]], nx.ap[:, :], xin, w["ga"][:, e:e + 1], w["be"][:, e:e + 1], ALU.mult, ALU.add,
                             eng="pool")
                    xin = nx.ap[:, :]
                hb = HB[(e * NCH + c) % 3]
                wh = list(hb.take())
                for hc in range(nh):
                    up, wu = UP.take()
                    k1 = mm([wu, xtt, wtok[e]], up.ap, we[:, 128 * hc:128 * hc + 128], xin)
                    if func is ACT.Relu and hc % 2:
                        if b1:
                            k2 = ts([k1, wh], hb.ap[:, hc, :], up.ap, we[:, 1024 + hc:1025 + hc], 0.0, ALU.add, ALU.max)
                        else:
                            k2 = ts([k1, wh], hb.ap[:, hc, :], up.ap, 0.0, None, ALU.max)
                    elif b1:
                        k2 = act([k1, wh], hb.ap[:, hc, :], up.ap, func, bias=we[:, 1024 + hc:1025 + hc])
                    else:
                        k2 = act([k1, wh], hb.ap[:, hc, :], up.ap, func)
                    up.free(k2)
                    if hc == nh - 2:
                        k0 = k2
                if nx is not None:
                    nx.free(k1)
                yield
                dn, wd = DN.take()
                for i in range(4):
                    for hc in range(nh):
                        k3 = mm([wd, k2, k0], dn.ap[:, 128 * i:128 * i + 128], hb.ap[:, hc, 128 * i:128 * i + 128],
                                we[:, 512 + 128 * hc:640 + 128 * hc], s=hc == 0, t=hc == nh - 1)
                hb.free(k3)
                for i in range(4):
                    x = X[:, 4 * c + i, :]
                    xtok[c] = stt([k3, xtok[c], gates[c]], x, dn.ap[:, 128 * i:128 * i + 128],
                                  GW[:, 4 * c + i, e:e + 1], x, ALU.mult, ALU.add)
                dn.free(xtok[c])
                if c == NCH - 1:
                    slotfree[e % 3] = k3
                if e == E - 1:
                    yield
                    x = X[:, 4 * c:4 * c + 4, :]
                    t4 = layer_norm(c, x, xtok[c])
                    yield
                    xtfree[c] = [k1]
                    if done is None:
                        transpose_x(c, x, t4)
                    yield
            run_pipeline([unit(e, c) for e in range(E) for c in range(NCH)], 1)
            BigMem.free = ends("pe", "dve")

        def gates_of(E, w, gw, gb, kind):
            res = {}
            for s_ in GS:
                s_.rel = BigMem.free or []
            run_pipeline([gate_unit(c, E, w, gw, gb, kind, res) for c in range(NCH)], 3)
            return res

        if sub(2):
            w = load_weights([("gw", "L0f_gw"), ("gb", "L0f_gb"), ("tri", "c_tri"), ("dw1", "L0f_dw1"), ("db1", "L0f_db1"),
                              ("dw2", "L0f_dw2"), ("db2", "L0f_db2"), ("b2", "L0f_b2")])
            g = gates_of(4, w, (w["gw"], None), w["gb"], "L0")
            experts(4, 256, "L0f_w1", "L0f_w2", "L0f_b1", ACT.Relu, g)
            weights_done(w)

        if sub(3):
            w = self_weights("L1a", [("g", "L1a_wg"), ("gb", "L1a_bg"), ("pb", "L1a_pb"), ("off", "L1a_offc"),
                                     ("it", "c_iota"), ("itc", "c_iotac"),
                                     ("anti", "c_anti")])
            KB = BIG[:, 0:4096].rearrange("p (h k) -> p h k", h=16)
            TMP = BIG[:, 4096:8192].rearrange("p (h k) -> p h k", h=16)
            QB = BIG[:, 8192:10240].bitcast(BF16).rearrange("p (h k) -> p h k", h=16)
            ds = DSem(Q, "d_tab")
            sc, wsc = PT.take()
            sd, wsd = PT.take()
            se, wse = PT.take()
            OH, OHT = sc.ap[0:68, 0:512], sc.ap[:, 512:648].rearrange("p (n o) -> p n o", n=2)
            OFR = sc.ap[:, 648:716]
            PMS = sd.ap[:, 0:32].rearrange("p (n h) -> p n h", n=2)
            CN = sd.ap[:, 32:34]
            OFRI = sd.ap[:, 100:168].bitcast(I32)
            OFCI = w["off"]
            OFC = sd.ap[0:68, 170:171]
            EO = sd.ap[0:68, 180:196]
            PM2 = se.ap[0:16, 0:512]
            EX2 = se.ap[0:16, 512:1024]
            TB = [BIG[0:16, 0:640], BIG[0:16, 640:1280]]
            td = ds.dma([wsd], OFRI, A["L1a_offr"].partition_broadcast(128))
            k = cp([td, wsc], OFR, OFRI)
            k = cp([w["t"], wsd], OFC, OFCI.bitcast(I32))
            k1 = ts([k], OH, w["it"], OFC, None, ALU.is_equal)
            for n in range(2):
                k2 = ts(None, OHT[:, n, :], OFR, w["itc"][:, n:n + 1], None, ALU.is_equal)
            pj, wp = PJ.take()
            pbt = w["pb"]
            onec = w["itc"][0:68, 2:3]
            for n in range(2):
                mm([wp, k1], pj.ap[:, 32 * n:32 * n + 16], OH[:, 128 * n:128 * n + 128], pbt)
                k3 = mm(None, pj.ap[:, 32 * n + 16:32 * n + 17], OH[:, 128 * n:128 * n + 128], onec)
            pv = pj.ap[:, 0:64].rearrange("p (n h) -> p n h", n=2)
            k4 = ts([k3], CN, pv[:, :, 16], 1.0, None, ALU.max)
            k4 = rcp(k4, CN, CN)
            for n in range(2):
                k5 = ts(k4, PMS[:, n, :], pv[:, n, 0:16], CN[:, n:n + 1], None, ALU.mult)
            pj.free(k5)
            pj, wp = PJ.take()
            for n in range(2):
                k6 = mm([wp, k5, k2], pj.ap[0:68, 0:16], OHT[:, n, :], PMS[:, n, :], s=n == 0, t=n == 1)
            k7 = tt(k6, EO, pbt, pj.ap[0:68, 0:16], ALU.subtract)
            pj.free(k7)
            k7 = act(k7, EO, EO, ACT.Exp)
            pj, wp = PJ.take()
            onem = w["itc"][0:68, 2:18]
            k8 = mm([wp], pj.ap[0:16, :], onem, OH)
            ms_ = FF.take()
            cnt = ms_[0].ap[0:16, :]
            k9 = cp([k8, ms_[1]], cnt, pj.ap[0:16, :])
            pj.free(k9)
            k10 = ts([k9, wse], PM2, cnt, 1.0, None, ALU.max)
            k10 = rcp(k10, PM2, PM2)
            pj, wp = PJ.take()
            k11 = mm([wp], pj.ap[0:16, :], pbt, OH)
            k12 = tt([k10, k11], PM2, PM2, pj.ap[0:16, :], ALU.mult)
            pj.free(k12)
            pj, wp = PJ.take()
            k13 = mm([wp, k7], pj.ap[0:16, :], EO, OH)
            k14 = ts([k13, wse], EX2, pj.ap[0:16, :], 1e-30, None, ALU.max)
            pj.free(k14)
            k14 = act(k14, EX2, EX2, ACT.Ln)
            k15 = tt([k14, k12], PM2, PM2, EX2, ALU.add)
            k15 = ts(k15, PM2, PM2, float(8 ** 0.5), None, ALU.mult)
            k16 = ts([k9], cnt, cnt, 0.0, NEG, ALU.is_equal, ALU.mult)
            k17 = None
            for n in range(2):
                k17 = ms(BigMem.free, TB[n], NEG, eng="dve")
            k18 = tt([k17, k16, k15], TB[0][:, 256:512], PM2[:, 0:256], cnt[:, 0:256], ALU.add)
            k19 = tt([k17, k16, k15], TB[1][:, 1:257], PM2[:, 256:512], cnt[:, 256:512], ALU.add)
            ms_[0].free(k19)
            sc.free(k13)
            sd.free(k13)
            se.free(k19)
            tab = A["scratch"]
            td = ds.dma([k18, k19], tab.rearrange("(n h) k -> h n k", n=2),
                        BIG[0:16, 0:1280].rearrange("p (n k) -> p n k", n=2))
            tb = tab.tensor
            td3 = ds.dma([td], TMP, bass.AP(tb, 129, [[1, 128], [640, 16], [1, 256]]))

            def turn(kd, dst):
                for i in range(8):
                    pj, wp = PJ.take()
                    k1 = mm([kd, wp], pj.ap, w["anti"], TMP[:, 2 * i:2 * i + 2, :])
                    k2 = act([k1, BigMem.free], dst[:, 2 * i:2 * i + 2, :], pj.ap.rearrange("p (h k) -> p h k", h=2))
                    pj.free(k2)
                return k1, k2
            k1, td2 = turn(td3, KB)
            td3 = ds.dma([k1], TMP, bass.AP(tb, 16 * 640 + 1, [[1, 128], [640, 16], [1, 256]]))
            k1, kq = turn(td3, QB)

            def gate1(c, bb, oo, to):
                xt = XT[:, 512 * c + 256 * bb:512 * c + 256 * bb + 256]
                pj, wp = PJ.take()
                for i in range(2):
                    mm([wp], pj.ap[:, 128 * i:128 * i + 128], xt[:, 128 * i:128 * i + 128], w["g"], t=False)
                    k1 = mm(None, pj.ap[:, 128 * i:128 * i + 128], ones1[:, :], w["gb"], s=False)
                oc, wo = OC.take()
                o2 = oc.ap.rearrange("p a b -> p (a b)")
                k2 = act([k1, wo], o2, pj.ap[:, 0:256], ACT.Exp, scale=-1.0)
                pj.free(k2)
                k3 = ts(k2, o2, o2, 1.0, None, ALU.add)
                k3 = rcp(k3, o2, o2)
                k4 = tt([k3, to], oo.ap[:, :, :], oo.ap[:, :, :], oc.ap[:, :, :], ALU.mult, eng="pool")
                oc.free(k4)
                yield
                return k4, k1
            bias = (QB, KB, kq, td2)
            run_pipeline([self_attention(c, w, "bias", bias=bias, gate=gate1) for c in range(NCH)], ATT_SKEW)
            weights_done(w)
            BigMem.free = ends("pe")

        if sub(4):
            w = self_weights("L1x", [("ck", "L1x_wck"), ("cv", "L1x_wcv")])
            kct, vbt = cross_setup(w["ck"], None, w["cv"], None, w["t"])
            run_pipeline([cross_attention(c, w, kct, vbt) for c in range(NCH)], CRS_SKEW)
            weights_done(w)
            BigMem.free = ends("pe")

        if sub(5):
            w = load_weights([("gw", "L1f_gw"), ("tri", "c_tri"), ("b2", "L1f_b2"), ("ga", "L1f_ga"), ("be", "L1f_be")])
            g = gates_of(8, w, (w["gw"], None), None, "L1")

            def xhat(c):
                rr, wr = RR.take()
                bs, wb = BS.take()
                mv, wv = MV.take()
                rs, wrs = RSD.take()
                k = xtok[c]
                pj, wp = PJ.take()
                for i in range(4):
                    k = tr([xttok[c], wp], pj.ap[:, 128 * i:128 * i + 128], XT[:, 512 * c + 128 * i:512 * c + 128 * i + 128],
                           idf[:, :])
                kx = act([k, wr], rr.ap.rearrange("p a b -> p (a b)"), pj.ap)
                pj.free(kx)
                for i in range(4):
                    k1 = Q.add("dve", [kx, wb], lambda e, i=i: e.bn_stats(bs.ap[:, i, :], rr.ap[:, i, :]))
                for i in range(4):
                    k2 = Q.add("dve", [k1, wv], lambda e, i=i: e.bn_aggr(mv.ap[:, i, :], bs.ap[:, i, :]))
                bs.free(k2)
                yield
                k3 = rsqrt([k2, wrs], rs.ap[:, 0:4], mv.ap[:, :, 1], 1e-6)
                for i in range(4):
                    k4 = ts([k3], rr.ap[:, i, :], rr.ap[:, i, :], mv.ap[:, i, 0:1], rs.ap[:, i:i + 1],
                            ALU.subtract, ALU.mult)
                mv.free(k4)
                rs.free(k4)
                yield
                xtfree[c] = [k]
                t5 = transpose_x(c, rr.ap, k4)
                rr.free(t5)
            run_pipeline([xhat(c) for c in range(NCH)], 1)
            experts(8, 512, "L1f_w1", "L1f_w2", "L1f_b1", ACT.Relu, g, kind="L1", w=w)
            weights_done(w)

        if sub(6):
            w = self_weights("L2a")
            MM = BIG[:, 0:512].bitcast(BF16)
            dm = DSem(Q, "d_mask").dma(BigMem.free, BIG[:, 0:512], A["c_addm"])
            bias = (MM[:, 0:256], MM[:, 256:384], MM[:, 384:512], None, dm, MM[:, 512:768], MM[:, 768:1024])
            run_pipeline([self_attention(c, w, "add", bias=bias, reps=3) for c in range(NCH)], 110)
            weights_done(w)
            BigMem.free = ends("pe")

        pre8 = None
        g8 = None
        if START <= 8 < STOP:
            g8 = sb("g8", [128, 2])
            tg8 = DSem(Q, "d_g").dma(None, g8[:, :], A["L2f_g"])
            pre8 = rms_input(g8[:, 0:1], tg8)
        if sub(7):
            w = self_weights("L2x", [("ck", "L2x_wck"), ("cv", "L2x_wcv"), ("ckb", "L2x_bck"), ("cvb", "L2x_bcv")])
            kct, vbt = cross_setup(w["ck"], w["ckb"], w["cv"], w["cvb"], w["t"])
            run_pipeline([cross_attention(c, w, kct, vbt, xn=pre8) for c in range(NCH)], CRS_SKEW)
            weights_done(w)
            BigMem.free = ends("pe")

        if sub(8):
            if START == 8:
                def first(c):
                    yield from pre8(c, xtok[c])
                run_pipeline([first(c) for c in range(NCH)], 2)
            w = self_weights("L2f")
            rope = rope_tables("rope2", BigMem.free)
            run_pipeline([self_attention(c, w, "causal", rope=rope, keep=rms_input(g8[:, 1:2], tg8)) for c in range(NCH)],
                         ATT_SKEW)
            weights_done(w)
            BigMem.free = ends("pe", "dve")
            w = load_weights([("gw", "L2f_gw"), ("tri", "c_tri"), ("triu", "c_triu"), ("one", "c_ones128")])
            g = gates_of(8, w, (w["gw"], None), None, "L2")
            cur, wc = RC.take()
            cand, tmp, cn = (cur.ap[:, 8 * i:8 * i + 8] for i in (1, 2, 3))
            cu = cur.ap[:, 0:8]
            big, wb = PT.take()
            eqs, we_ = PT.take()
            gv = GW[:, :, 0:8].rearrange("p t e -> p e t")
            cmp_ = big.ap[:, 0:256].rearrange("p (e t) -> p e t", e=8)
            ex8 = [128, 8, 32]

            def b8(v):
                return bc(v, ex8, "p (e o) -> p e o", o=1)

            def total(k):
                pj, wp = PJ.take()
                k = mm([k, wp, w["t"]], pj.ap[:, 0:8], w["one"], cn)
                return pj, k
            k = ms([list(g.values()), wc, wb, we_], cu, 0.0, eng="dve")
            for bit in range(29, -1, -1):
                k = ts(k, cand.bitcast(I32), cu.bitcast(I32), 1 << bit, None, ALU.bitwise_or)
                k = tt(k, cmp_, gv, b8(cand), ALU.is_ge)
                k = red(k, cn, cmp_, ALU.add)
                pj, k = total(k)
                k = stt(k, tmp, pj.ap[:, 0:8], 159.5, cand, ALU.is_gt, ALU.mult)
                pj.free(k)
                k = tt(k, cu, cu, tmp, ALU.max)
            k = tt(k, cmp_, gv, b8(cu), ALU.is_gt)
            k = red(k, cn, cmp_, ALU.add)
            eq = eqs.ap[:, 0:256]
            ke = tt(k, eq.rearrange("p (e t) -> p e t", e=8), gv, b8(cu), ALU.is_equal)
            pj, k = total(k)
            k = ts(k, tmp, pj.ap[:, 0:8], -1.0, 160.0, ALU.mult, ALU.add)
            pj.free(k)
            pj, wp = PJ.take()
            mm([wp, ke], pj.ap[:, 0:256], w["triu"], eq)
            k2 = mm(None, pj.ap[:, 256:512], w["one"], eq)
            tot_, run_ = eqs.ap[:, 256:512], eqs.ap[:, 512:768]
            k2 = cp(k2, tot_, pj.ap[:, 256:512])
            zero = eqs.ap[:, 768:800]
            kz = ms(we_, zero, 0.0, eng="dve")
            for e_ in range(8):
                k3 = Q.add("dve", [k2, kz], lambda e, e_=e_: e.tensor_tensor_scan(
                    run_[:, 32 * e_:32 * e_ + 32], tot_[:, 32 * e_:32 * e_ + 32], zero, 0.0, ALU.add, ALU.add))
            k3 = tt(k3, run_, run_, tot_, ALU.subtract)
            k3 = tt(k3, run_, run_, pj.ap[:, 0:256], ALU.add)
            pj.free(k3)
            r3 = run_.rearrange("p (e t) -> p e t", e=8)
            k3 = tt([k3, k], r3, r3, b8(tmp), ALU.is_lt)
            k3 = tt(k3, run_, run_, eq, ALU.mult)
            k3 = tt(k3, cmp_, cmp_, r3, ALU.add)
            k3 = tt(k3, gv, gv, cmp_, ALU.mult)
            cur.free(k3)
            big.free(k3)
            eqs.free(k3)
            experts(8, 256, "L2f_w1", "L2f_w2", None, ACT.Relu, {c: k3 for c in range(NCH)})
            weights_done(w)

        def linear_attention(c, w):
            xt, xtt = XT[:, 512 * c:512 * c + 512], xttok[c]
            pj, wp = PJ.take()
            k = mm([wp, xtt, w["t"]], pj.ap, w["q"], xt)
            ff, wf = FF.take()
            kq = act([k, wf], ff.ap[:, :], pj.ap, ACT.Relu)
            pj.free(kq)
            yield
            ot, wot = OT.take()
            for bb in range(2):
                pj, wp = PJ.take()
                for i in range(2):
                    rd = mm([wp], pj.ap[:, 256 * i:256 * i + 256], xt[:, 256 * bb + 128 * i:256 * bb + 128 * i + 128],
                            w["kv"])
                kv, wkv = PT.take()
                v = pj.ap.rearrange("p (i k) -> p i k", i=2)
                kr = kv.ap[:, 0:256].rearrange("p (i k) -> p i k", i=2)
                vr = kv.ap[:, 256:256 + 258].rearrange("p (i k) -> p i k", i=2)
                bd = kv.ap[:, 600:744]
                zz = kv.ap[:, 760:792].rearrange("p (i k) -> p i k", i=2)
                k1 = act([rd, wkv], kr, v[:, :, 0:128], ACT.Relu)
                k2 = act([rd, wkv], vr[:, :, 0:128], v[:, :, 128:256])
                k3 = ms(wkv, vr[:, :, 128:129], 1.0, eng="pool")
                pj.free(k1, k2)
                yield
                pj, wp = PJ.take()
                for i in range(2):
                    k4 = mm([wp, k1, k2, k3], pj.ap[:, 0:129], kr[:, i, :], vr[:, i, :], s=i == 0, t=i == 1)
                k5 = tt([k4], bd[:, 0:128].rearrange("p (h d) -> p h d", h=16),
                        pj.ap[:, 0:128].rearrange("p (h d) -> p h d", h=16),
                        bc(w["hm"], [128, 16, 8], "p (h o) -> p h o", o=1), ALU.mult)
                k6 = tt([k4], bd[:, 128:144], w["hm"], pj.ap[:, 128:129].to_broadcast([128, 16]), ALU.mult)
                pj.free(k6)
                yield
                pj, wp = PJ.take()
                o = pj.ap[:, 0:288].rearrange("p (i k) -> p i k", i=2)
                for i in range(2):
                    k7 = mm([wp, k6, k5, kq], o[:, i, :], ff.ap[:, 256 * bb + 128 * i:256 * bb + 128 * i + 128], bd)
                k8 = ts([k7], zz, o[:, :, 128:144], float(np.finfo(np.float32).eps), None, ALU.add)
                k8 = rcp(k8, zz, zz)
                oo, wo = OO.take()
                for i in range(2):
                    k9 = tt([k8, wo], oo.ap[:, i, :].rearrange("p (h d) -> p h d", h=16),
                            o[:, i, 0:128].rearrange("p (h d) -> p h d", h=16),
                            bc(zz[:, i, :], [128, 16, 8], "p (h o) -> p h o", o=1), ALU.mult)
                pj.free(k9)
                kv.free(k9, k7)
                yield
                tot = to_ot(oo, k9, ot, wot, bb)
                if bb == 1:
                    ff.free(k7)
                yield
            yield from out_proj(c, ot, tot, w["o"], w["t"], w["ob"], [rd])

        if sub(9):
            w = load_weights([("q", "L3a_wq"), ("kv", "L3a_wkv"), ("o", "L3a_wo"), ("ob", "L3a_bo"), ("hm", "c_hm")])
            run_pipeline([linear_attention(c, w) for c in range(NCH)], 7)
            weights_done(w)
            BigMem.free = ends("pe", "dve")

        if sub(10):
            dw = DSem(Q, "d_w")
            pos = 0
            w = {}
            for key, name in (("q", "L3x_wq"), ("k", "L3x_wk"), ("v", "L3x_wv"), ("o", "L3x_wo"), ("sel", "c_sel"),
                              ("ob64", "c_ob64"), ("bo", "L3x_bo")):
                k_, n_ = A[name].shape
                w[key] = WB[0:k_, pos:pos + n_]
                pos += n_
                assert pos <= 5376
                wtk = dw.dma(WL.done, w[key], A[name])
            sel = w["sel"].bitcast(BF16)
            KB2 = [Slot(BIG[:, 2048 * i:2048 * i + 2048].rearrange("p (a b k) -> p a b k", a=8, b=2)) for i in range(2)]
            VB2 = [Slot(BIG[:, 4096 + 2048 * i:6144 + 2048 * i].rearrange("p (a b k) -> p a b k", a=8, b=2)) for i in range(2)]
            R2 = [Slot(BIG[:, 8192 + 256 * i:8448 + 256 * i]) for i in range(2)]
            z = ms(BigMem.free, BIG[:, 0:8192], 0.0, eng="dve")
            for s_ in KB2 + VB2 + R2:
                s_.rel = [z]
            QT2 = Ring([Slot(KS[i][:, :, :].bitcast(F32).rearrange("p a b -> p (a b)").rearrange("p (a b) -> p a b", a=8))
                        for i in range(2)])
            for i in range(2):
                QT2.slots[i].rel = KSr.slots[i].rel
            KB2, VB2, R2 = Ring(KB2), Ring(VB2), Ring(R2)

            def wide(c):
                xt, xtt = XT[:, 512 * c:512 * c + 512], xttok[c]
                qt_, wq = QT2.take()
                kb, wk = KB2.take()
                vb, wv = VB2.take()
                for blk in range(8):
                    pj, wp = PJ.take()
                    rd = mm([wp, xtt, wtk], pj.ap, w["q"][:, 128 * blk:128 * blk + 128], xt)
                    kq = act([rd, wq], qt_.ap[:, blk, :], pj.ap)
                    pj.free(kq)
                    yield
                for half in range(2):
                    pj, wp = PJ.take()
                    for i in range(4):
                        k1 = mm([wp, ct_t], pj.ap[:, 128 * i:128 * i + 128].rearrange("p (a k) -> p a k", a=2),
                                w["k"][:, 512 * half + 128 * i:512 * half + 128 * i + 128],
                                CT[:, 256 * c:256 * c + 256].rearrange("p (a q k) -> p a q k", a=2, q=2)[:, :, 0, :])
                    v = pj.ap.rearrange("p (i a k) -> p i a k", i=4, a=2)
                    k2 = act([k1, wk], kb.ap[0:64, 4 * half:4 * half + 4, :, 0:64], v[0:64])
                    k3 = cp([k1, wk], kb.ap[64:128, 4 * half:4 * half + 4, :, 64:128], v[64:128])
                    pj.free(k2, k3)
                    kk = [k2, k3] if half == 0 else kk + [k2, k3]
                    yield
                kv = []
                for bb in range(2):
                    for half in range(2):
                        pj, wp = PJ.take()
                        k1 = mm([wp], pj.ap, CT[:, 256 * c + 128 * bb:256 * c + 128 * bb + 128],
                                w["v"][:, 512 * half:512 * half + 512])
                        v = pj.ap.rearrange("p (i a k) -> p i a k", i=4, a=2)
                        k2 = act([k1, wv], vb.ap[0:64, 4 * half:4 * half + 4, bb, 0:64], v[0:64, :, 0, :])
                        k3 = cp([k1, wv], vb.ap[64:128, 4 * half:4 * half + 4, bb, 64:128], v[64:128, :, 1, :])
                        pj.free(k2, k3)
                        kv += [k2, k3]
                        yield
                outs = []
                for bb in range(2):
                    m3, wm = M3.take()
                    for qt in range(2):
                        for half in range(2):
                            mx, wx = MX.take()
                            for i in range(4):
                                blk = 4 * half + i
                                k4 = mm([wx, kk, kq], mx.ap[:, 128 * i:128 * i + 128],
                                        qt_.ap[:, blk, 256 * bb + 128 * qt:256 * bb + 128 * qt + 128], kb.ap[:, blk, bb, :])
                            k5 = red([k4, wm], m3.ap[:, 8 * half:8 * half + 8, qt],
                                     mx.ap.rearrange("p (a k) -> p a k", a=8), ALU.max)
                            mx.free(k5)
                        yield
                    mb, wmb = MB.take()
                    for qt in range(2):
                        v = m3.ap[:, :, qt:qt + 1].rearrange("p (b a) o -> p a (b o)", a=2)
                        o = mb.ap[:, qt, :].rearrange("p (a s b) -> p a s b", a=2, s=2)
                        k6 = ts([k5, wmb], o[:, :, 0, :], v, -1.0, None, ALU.mult)
                        k6 = stt([k6], o[:, :, 1, :], v, -1.0, o[:, :, 0, :], ALU.mult, ALU.subtract)
                    m3.free(k6)
                    pj, wp = PJ.take()
                    pb = pj.ap.bitcast(BF16)
                    for qt in range(2):
                        k7 = tr([k6, wp, t_idb], pb[0:32, 128 * qt:128 * qt + 128], mb.ap[:, qt, :], idb[:, :])
                    mb.free(k7)
                    mt, wmt = MT.take()
                    k8 = cp([k7, wmt], mt.ap[:, :], pb[0:32, 0:256])
                    pj.free(k8)
                    yield
                    o3, wo3 = QSr.take()
                    o3v = o3.ap[:, :, :].bitcast(F32)
                    outs.append(o3)
                    for half in range(2):
                        st, wst = ST.take()
                        sv = st.ap.rearrange("p a (b k) -> p (a b) k", b=2)
                        for i in range(4):
                            blk = 4 * half + i
                            mm([wst], sv[:, i, :], kb.ap[:, blk, bb, :], qt_.ap[:, blk, 256 * bb:256 * bb + 256], t=False)
                            k9 = mm([k8], sv[:, i, :], sel[:, 128 * blk:128 * blk + 128], mt.ap[:, :], s=False)
                        pt, wpt = PT.take()
                        k10 = act([k9, wpt], pt.ap.rearrange("p (a k) -> p a k", a=2), st.ap, ACT.Exp, scale=0.125)
                        st.free(k10)
                        yield
                        for i in range(4):
                            blk = 4 * half + i
                            pv, wpv = PV.take()
                            mm([k10, wpv, kv], pv.ap[:, 0:256], vb.ap[:, blk, bb, :], pt.ap[:, 256 * i:256 * i + 256])
                            k11 = mm(None, pv.ap[:, 256:512], w["ob64"], pt.ap[:, 256 * i:256 * i + 256])
                            rc, wrc = R2.take()
                            k12 = rcp([k11, wrc], rc.ap, pv.ap[:, 256:512])
                            k13 = tt([k12, wo3], o3v[:, blk, :], rc.ap, pv.ap[:, 0:256], ALU.mult)
                            rc.free(k13)
                            pv.free(k13)
                            if i % 2:
                                yield
                        pt.free(k11)
                    mt.free(k9)
                kb.free(k9)
                vb.free(k11)
                qt_.free(k9)
                pj, wp = PJ.take()
                for i in range(4):
                    for blk in range(8):
                        ov = outs[i // 2].ap[:, :, :].bitcast(F32)
                        mm([wp, k13], pj.ap[:, 128 * i:128 * i + 128], ov[:, blk, 128 * (i % 2):128 * (i % 2) + 128],
                           w["o"][:, 128 * blk:128 * blk + 128], s=blk == 0, t=False)
                    k14 = mm(None, pj.ap[:, 128 * i:128 * i + 128], ones1[:, :], w["bo"], s=False)
                outs[0].free(k14)
                outs[1].free(k14)
                rr, wr = RR.take()
                k15 = tt([k14, wr, xtok[c]], rr.ap[:, :, :], pj.ap.rearrange("p (a b) -> p a b", a=4),
                         X[:, 4 * c:4 * c + 4, :], ALU.add)
                pj.free(k15)
                yield
                k16 = layer_norm(c, rr.ap, k15)
                rr.free(k16)
                yield
                xtfree[c] = [rd]
                transpose_x(c, X[:, 4 * c:4 * c + 4, :], k16)
                yield
            run_pipeline([wide(c) for c in range(NCH)], 42)
            WL.done = [ends(), ends()]
            BigMem.free = ends("pe", "dve", "act")

        if sub(11):
            w = load_weights([("key", "L3f_key"), ("rw", "L3f_rw"), ("rb", "L3f_rb"), ("tri", "c_tri"), ("b2", "L3f_b2"),
                              ("one", "c_ones128"), ("buf", "c_buf"), ("buf2", "c_buf")])
            gw, sq, brow = w["buf"][:, 0:16], w["buf"][:, 16:32], w["buf2"][0:1, 0:16]
            k1 = stt(w["t"], gw, w["key"], 2.0, w["rw"], ALU.mult, ALU.add)
            k2 = tt(w["t"], sq, w["key"], w["key"], ALU.mult)
            pj, wp = PJ.take()
            k3 = mm([k2, wp], pj.ap[:, 0:16], w["one"], sq)
            k4 = tt([k3], brow, w["rb"], pj.ap[0:1, 0:16], ALU.subtract)
            pj.free(k4)
            g = gates_of(16, w, (gw, [k1, k4]), brow, "L3")
            experts(16, 512, "L3f_w1", "L3f_w2", "L3f_b1", ACT.Gelu, g, done=True)
            weights_done(w)

        s_out = DSem(Q, "d_out")
        for c in range(NCH):
            t = s_out.dma([xtok[c]], out.rearrange("b (t p) d -> p (b t) d", p=128)[:, 4 * c:4 * c + 4, :],
                          X[:, 4 * c:4 * c + 4, :])
        for d in Q.dsems:
            Q.add("sp", [Tok(d.sem, d.n)], lambda e: e.nop())

        Q.count()
        block = ctx.enter_context(nc.Block())

        @block.tensor
        def _(e):
            Q.emit("pe", e)

        @block.scalar
        def _(e):
            Q.emit("act", e)

        @block.vector
        def _(e):
            Q.emit("dve", e)

        @block.gpsimd
        def _(e):
            Q.emit("pool", e)

        @block.sync
        def _(e):
            Q.emit("sp", e)


def _bf(a):
    h = (np.ascontiguousarray(a, np.float32).view(np.uint32) >> 16).astype(np.uint16)
    return h.view(np.uint32).view(np.float32)


def _consts():
    k = np.arange(128)
    c = {"c_ident": np.eye(128, dtype=np.float32), "c_ones": np.ones((2, 512), np.float32),
         "c_kc": _bf(np.broadcast_to((k[:4, None, None, None] // 2 == k[None, None, :2, None]), (4, 128, 2, 64))
                     .reshape(4, 16384)),
         "c_pmask": ((k[:, None] // 48) == k[None, :2]).astype(np.float32),
         "c_one2": _bf(np.ones((2, 4096), np.float32)),
         "c_maskq": _bf(np.where(k[None, :] > k[:, None], np.float32(NEG), np.float32(0))),
         "c_maskk": _bf(np.where(k[:, None] > k[None, :], np.float32(NEG), np.float32(0)))}
    c["c_triu"] = (k[:, None] < k[None, :]).astype(np.float32)
    c["c_ones128"] = np.ones((128, 128), np.float32)
    c["c_anti"] = np.eye(128, dtype=np.float32)[::-1]
    c["c_buf"] = np.zeros((128, 32), np.float32)
    c["c_hm"] = (k[:, None] // 8 == np.arange(16)[None, :]).astype(np.float32)
    c["c_ob64"] = (k[:, None] // 64 == k[None, :] // 64).astype(np.float32)
    r32 = np.arange(32)
    c["c_sel"] = _bf(((r32[:, None, None] // 16 == k[None, None, :] // 64)
                      & (r32[:, None, None] % 8 == np.arange(8)[None, :, None])).reshape(32, 1024))
    e16 = np.arange(16)
    c["c_tri"] = np.broadcast_to((e16[None, :] < e16[:, None]).astype(np.float32).reshape(1, 256), (128, 256))
    c["c_iota"] = np.broadcast_to(np.concatenate([np.arange(256), 255 - np.arange(256)]).astype(np.float32), (68, 512))
    c["c_iotac"] = np.concatenate([k[:, None], k[:, None] + 128, np.ones((128, 16))], 1).astype(np.float32)
    big = np.float32(-10000.0 * 8 ** 0.5)
    hi = (np.array([big]).view(np.uint32) & np.uint32(0xFFFF0000)).view(np.float32)[0]
    lo = np.float32(big - hi)
    dq = np.where(k[None, :] > k[:, None], 1.0, 0.0)
    dk = dq.T
    one, zer = np.ones((128, 128)), np.zeros((128, 128))
    c["c_addm"] = _bf(np.concatenate([hi * dq, hi * one, hi * dk, lo * dk, hi * one, hi * dk, lo * one, lo * dk], 1))
    d = (np.arange(128) // 8) % 8
    pos = np.arange(512) % 256
    for name, sgn in (("rope0", 1.0), ("rope2", -1.0)):
        fr = np.float32(10000.0) ** (np.float32(sgn) * np.arange(0, 8, 2, dtype=np.float32) / np.float32(8))
        ang = np.arange(256, dtype=np.float32)[:, None] * fr[None, :]
        s, co = np.sin(ang.astype(np.float64)), np.cos(ang.astype(np.float64))
        c[name + "_c"] = np.ascontiguousarray(co[pos][:, d // 2].T.astype(np.float32))
        c[name + "_s"] = np.ascontiguousarray((s[pos][:, d // 2].T * np.where(d % 2, 1.0, -1.0)[:, None]).astype(np.float32))
    return c


def _layout(inp):
    p = np.arange(128)
    par, d, blk = p // 64, (p // 8) % 8, p % 8
    perm = (par * 8 + blk) * 8 + d
    swap = (par * 8 + blk) * 8 + (d ^ 1)
    a = {"x": inp["x"], "xT": np.ascontiguousarray(np.transpose(inp["x"].reshape(4096, 128)))}

    def heads(pre, wq, wk, wv, wo, bq=None, bk=None, bv=None, bo=None, rope=False):
        a[pre + "_wq"], a[pre + "_wk"], a[pre + "_wv"], a[pre + "_wo"] = wq[:, perm], wk[:, perm], wv, wo[perm]
        if rope:
            a[pre + "_wqs"], a[pre + "_wks"] = wq[:, swap], wk[:, swap]
        if bq is not None:
            a[pre + "_bq"], a[pre + "_bk"], a[pre + "_bv"] = bq[perm][:, None], bk[perm][:, None], bv[None]
            if rope:
                a[pre + "_bqs"], a[pre + "_bks"] = bq[swap][:, None], bk[swap][:, None]
        if bo is not None:
            a[pre + "_bo"] = bo[None]

    w, b = inp["L0_attn_qkv_w"], inp["L0_attn_qkv_b"]
    heads("L0a", w[:, :128], w[:, 128:256], w[:, 256:], inp["L0_attn_out_w"], b[:128], b[128:256], b[256:],
          inp["L0_attn_out_b"], rope=True)
    a["ctxT"] = np.transpose(inp["ctx_512"], (2, 0, 1))[:, :, None, :].repeat(2, axis=2).reshape(64, 2048)
    g = lambda n: inp["L0_xattn_" + n]
    heads("L0x", g("Wq"), g("Wk"), g("Wv"), g("Wp"), g("bq"), g("bk"), g("bv"), g("bp"))
    a["L0x_wcq"], a["L0x_wck"], a["L0x_wcv"] = g("Wcq")[:, perm], g("Wck")[:, perm], g("Wcv")
    a["L0x_bcq"], a["L0x_bck"], a["L0x_bcv"] = g("bcq")[perm][:, None], g("bck")[perm][:, None], g("bcv")[None]
    cols = lambda b: b.reshape(b.shape[0], -1, 128).transpose(0, 2, 1)
    kt = lambda v: v.reshape(v.shape[0], -1, 128, 128).transpose(0, 2, 1, 3).reshape(v.shape[0], 128, -1)
    g = lambda n: inp["L0_ffn_" + n]
    a["L0f_gw"], a["L0f_gb"], a["L0f_dw1"], a["L0f_db1"] = g("gate_w"), g("gate_b")[None], g("dp_w1"), g("dp_b1")[:, None]
    a["L0f_dw2"], a["L0f_db2"], a["L0f_b2"] = g("dp_w2"), g("dp_b2")[None], g("eb2")
    a["L0f_w1"], a["L0f_w2"], a["L0f_b1"] = g("ew1"), kt(g("ew2")), cols(g("eb1"))
    g = lambda n: inp["L1_attn_" + n]
    w, b = np.transpose(g("Wqkv")), g("bqkv")
    heads("L1a", w[:, :128], w[:, 128:256], w[:, 256:], np.transpose(g("Wout")), b[:128], b[128:256], b[256:], g("bout"))
    a["L1a_wg"], a["L1a_bg"] = np.transpose(g("Wgate"))[:, perm], g("bgate")[perm][None]
    a["L1a_pb"] = g("pos_bias")
    a["L1a_offc"], a["L1a_offr"] = g("offsets")[:, None], g("offsets")
    g = lambda n: inp["L1_xattn_" + n]
    wkv = np.transpose(g("Wkv"))
    heads("L1x", np.transpose(g("Wq")), wkv[:, :128], wkv[:, 128:], np.transpose(g("Wo")))
    a["L1x_wck"], a["L1x_wcv"] = wkv[:, :128][:, perm], wkv[:, 128:]
    g = lambda n: inp["L1_ffn_" + n]
    a["L1f_gw"], a["L1f_b2"], a["L1f_ga"], a["L1f_be"] = g("Wg"), g("b2"), np.transpose(g("gamma")), np.transpose(g("beta"))
    a["L1f_w1"], a["L1f_w2"], a["L1f_b1"] = g("W1"), kt(g("W2")), cols(g("b1"))
    g = lambda n: inp["L2_attn_" + n]
    w, b = np.transpose(g("Wqkv_w")), g("Wqkv_b")
    heads("L2a", w[:, :128], w[:, 128:256], w[:, 256:], np.transpose(g("out_w")), b[:128], b[128:256], b[256:], g("out_b"))
    g = lambda n: inp["L2_xattn_" + n]
    heads("L2x", g("Wq"), g("Wk"), g("Wv"), g("Wo"), g("bq"), g("bk"), g("bv"), g("bo"))
    a["L2x_wck"], a["L2x_wcv"], a["L2x_bck"], a["L2x_bcv"] = g("Wk")[:, perm], g("Wv"), g("bk")[perm][:, None], g("bv")[None]
    a["L2f_g"] = np.stack([inp["L2_ffn_g1"], inp["L2_ffn_g2"]], 1)
    g = lambda n: inp["L2_ffn_" + n]
    w = g("w_qkv")
    heads("L2f", w[:, :128], w[:, 128:256], w[:, 256:], g("w_o"), rope=True)
    a["L2f_gw"], a["L2f_w1"], a["L2f_w2"] = g("w_router"), g("w1"), kt(g("w2"))
    g = lambda n: inp["L3_attn_" + n]
    w = np.transpose(g("w_qkv"))
    a["L3a_wq"], a["L3a_wkv"], a["L3a_wo"], a["L3a_bo"] = w[:, :128], w[:, 128:], np.transpose(g("w_proj")), g("b_proj")[None]
    g = lambda n: inp["L3_xattn_" + n]
    a["L3x_wq"], a["L3x_wk"], a["L3x_wv"], a["L3x_bo"] = g("Wq"), g("Wk"), g("Wv"), g("bo")[None]
    a["L3x_wo"] = kt(g("Wo")[None])[0]
    g = lambda n: inp["L3_ffn_" + n]
    a["L3f_key"], a["L3f_rw"], a["L3f_rb"] = np.transpose(g("keys")), np.transpose(g("rw")), g("rb")[None]
    a["L3f_w1"], a["L3f_w2"] = np.transpose(g("w1"), (0, 2, 1)), kt(np.transpose(g("w2"), (0, 2, 1)))
    a["L3f_b1"], a["L3f_b2"] = cols(g("b1")), g("b2")
    return {k: np.ascontiguousarray(v) for k, v in a.items()}


def kernel(**inputs):
    import concourse.bacc as _bacc
    from concourse.bass_utils import run_bass_kernel_spmd as _run

    nc = _bacc.Bacc("TRN2", target_bir_lowering=False, num_devices=1)
    arrays = _layout({k: np.asarray(v) for k, v in inputs.items()})
    arrays.update({n: np.ascontiguousarray(v) for n, v in _consts().items()})
    aps = {n: nc.dram_tensor("in_" + n, a.shape, mybir.dt.from_np(a.dtype), kind="ExternalInput").ap()
           for n, a in arrays.items()}
    aps["scratch"] = nc.dram_tensor("scratch", (32, 640), F32).ap()
    out = nc.dram_tensor("out_0", (16, 256, 128), F32, kind="ExternalOutput").ap()
    program(nc, aps, out)
    r = _run(nc, [{"in_" + n: a for n, a in arrays.items()}], core_ids=[0])
    return r.results[0]["out_0"]
```

```python
import concourse.bass as bass
from concourse import mybir
from contextlib import ExitStack
import numpy as np

F32 = mybir.dt.float32
BF16 = mybir.dt.bfloat16
I32 = mybir.dt.int32
ALU = mybir.AluOpType
ACT = mybir.ActivationFunctionType
AX = mybir.AxisListType
NCH = 8
START, STOP = 0, 12
RS8 = float(8 ** -0.5)
NEG = -1e30


class Tok:
    def __init__(self, sem=None, val=0):
        self.sem, self.val, self.used = sem, val, False


class Queues:
    def __init__(self, nc, ctx):
        self.nc, self.ctx = nc, ctx
        self.q = {k: [] for k in ("pe", "act", "dve", "pool", "sp")}
        self.nsem = 0
        self.dsems = []
        self.new_phase()

    def sem(self, name):
        self.nsem += 1
        return self.ctx.enter_context(self.nc.semaphore(f"{name}{self.nsem}"))

    def new_phase(self):
        self.sems = {k: self.sem("s_" + k) for k in ("pe", "act", "dve", "pool")}

    def add(self, eng, waits, fn):
        t = Tok(self.sems.get(eng))
        flat = []

        def walk(w):
            if isinstance(w, Tok):
                w.used = True
                flat.append(w)
            elif w is not None:
                for v in w:
                    walk(v)
        walk(waits)
        self.q[eng].append((fn, flat, t))
        return t

    def count(self):
        n = {}
        for eng in ("pe", "act", "dve", "pool"):
            for fn, waits, t in self.q[eng]:
                if t is not None and t.used:
                    n[t.sem.name] = n.get(t.sem.name, 0) + 1
                    t.val = n[t.sem.name]

    def emit(self, eng, e):
        seen = {}
        for fn, waits, t in self.q[eng]:
            need = {}
            for w in waits:
                if seen.get(w.sem.name, 0) < w.val and need.get(w.sem.name, (None, 0))[1] < w.val:
                    need[w.sem.name] = (w.sem, w.val)
            for n, (s, v) in need.items():
                e.wait_ge(s, v)
                seen[n] = v
            ins = fn(e)
            if t is not None and t.used:
                ins.then_inc(t.sem, 1)


class Slot:
    def __init__(self, ap):
        self.ap, self.rel, self.held = ap, [], False

    def take(self):
        assert not self.held
        self.held = True
        return self.rel

    def free(self, *toks):
        self.held = False
        self.rel = list(toks)


class Ring:
    def __init__(self, slots):
        self.slots, self.n, self.line = slots, 0, []

    def take(self):
        s = self.slots[self.n % len(self.slots)]
        self.n += 1
        return s, list(s.take())


def free_slot(*rings):
    me = object()
    for r in rings:
        r.line.append(me)
    while any(r.line[0] is not me or r.slots[r.n % len(r.slots)].held for r in rings):
        yield
    for r in rings:
        r.line.pop(0)


class Turn:
    def __init__(self):
        self.held, self.line = False, []

    def enter(self):
        me = object()
        self.line.append(me)
        while self.held or self.line[0] is not me:
            yield
        self.line.pop(0)
        self.held = True

    def leave(self):
        self.held = False


class DSem:
    def __init__(self, Q, name):
        self.Q, self.sem, self.n = Q, Q.sem(name), 0
        Q.dsems.append(self)

    def dma(self, waits, out, in_, eng="sp"):
        self.n += 16
        sem = self.sem
        self.Q.add(eng, waits, lambda e: e.dma_start(out, in_).then_inc(sem, 16)).used = False
        t = Tok(self.sem, self.n)
        return t


def run_pipeline(gens, skew):
    at = [i * skew for i in range(len(gens))] if isinstance(skew, int) else skew
    live, nxt, t = [], 0, 0
    while live or nxt < len(gens):
        while nxt < len(gens) and t >= at[nxt]:
            live.append(gens[nxt])
            nxt += 1
        for g in list(live):
            try:
                next(g)
            except StopIteration:
                live.remove(g)
        t += 1


def program(nc, A, out, stop=12):
    ctx = ExitStack()
    with ctx:
        Q = Queues(nc, ctx)

        def sb(name, shape, dt=F32):
            return ctx.enter_context(nc.sbuf_tensor(name, shape, dt))

        def mm(w, o, l, r, s=True, t=True):
            return Q.add("pe", w, lambda e: e.matmul(o, l, r, start=s, stop=t))

        def tr(w, o, i, idn):
            return Q.add("pe", w, lambda e: e.transpose(o, i, idn))

        def act(w, o, i, f=ACT.Copy, scale=1.0, bias=0.0):
            return Q.add("act", w, lambda e: e.activation(o, i, f, bias=bias, scale=scale))

        def tt(w, o, a, b, op, eng="dve"):
            return Q.add(eng, w, lambda e: e.tensor_tensor(o, a, b, op))

        def ts(w, o, a, s1, s2, op0, op1=None, eng="dve"):
            if op1 is None:
                return Q.add(eng, w, lambda e: e.tensor_scalar(o, a, s1, None, op0))
            return Q.add(eng, w, lambda e: e.tensor_scalar(o, a, s1, s2, op0, op1))

        def stt(w, o, a, s, b, op0, op1):
            return Q.add("dve", w, lambda e: e.scalar_tensor_tensor(out=o, in0=a, scalar=s, in1=b, op0=op0, op1=op1))

        def red(w, o, i, op):
            return Q.add("dve", w, lambda e: e.tensor_reduce(o, i, axis=AX.X, op=op))

        def cp(w, o, i, eng="dve"):
            return Q.add(eng, w, lambda e: e.tensor_copy(o, i))

        def ms(w, o, v, eng="pool"):
            return Q.add(eng, w, lambda e: e.memset(o, v))

        def rcp(w, o, i):
            return Q.add("dve", w, lambda e: e.reciprocal(o, i))

        X = sb("X", [128, 32, 128])
        XT = sb("XT", [128, 4096])
        xtok = [None] * NCH
        xttok = [None] * NCH
        xtfree = [[] for _ in range(NCH)]
        PS = ctx.enter_context(nc.psum_tensor("ps", [128, 8, 512], F32))
        bank = [Slot(PS[:, i, :]) for i in range(8)]

        class Banks:
            def __init__(self, groups):
                self.groups, self.n = groups, 0

            def take(self):
                g = self.groups[self.n % len(self.groups)]
                self.n += 1
                w = [list(bank[i].take()) for i in g]
                ap = PS[:, g[0]:g[0] + len(g), :]

                class H:
                    pass
                h = H()
                h.ap = ap if len(g) > 1 else PS[:, g[0], :]

                def free(*toks):
                    for i in g:
                        bank[i].free(*toks)
                h.free = free
                return h, w
        MX = Banks([[0], [1]])
        ST = Banks([[2, 3], [4, 5]])
        PV = Banks([[6]])
        PJ = Banks([[7]])
        UP = Banks([[0], [1], [2], [3]])
        DN = Banks([[4], [5]])

        s_const = DSem(Q, "d_const")

        WB = sb("WB", [128, 4352])

        idf = sb("idf", [128, 128])
        idb = sb("idb", [128, 128], BF16)
        mskQ = sb("mskQ", [128, 128], BF16)
        mskK = sb("mskK", [128, 128], BF16)
        ones1 = sb("ones1", [1, 128])
        t = s_const.dma(None, idf[:, :], A["c_ident"])
        t = s_const.dma(None, mskQ[:, :].bitcast(F32), A["c_maskq"])
        t = s_const.dma(None, mskK[:, :].bitcast(F32), A["c_maskk"])
        t_c = s_const.dma(None, ones1[:, :], A["c_ones"][0:1, 0:128])
        pmask = sb("pmask", [128, 2])
        t_c = s_const.dma(None, pmask[:, :], A["c_pmask"])
        t_idb = cp(t_c, idb[:, :], idf[:, :])

        s_x = DSem(Q, "d_x")
        s_xt = DSem(Q, "d_xt")
        xd = s_x.dma(None, X[:, :, :], A["x"].rearrange("b (t p) d -> p (b t) d", p=128))
        xtd = s_xt.dma(None, XT[:, :], A["xT"])
        for c in range(NCH):
            xtok[c], xttok[c] = xd, xtd

        KS = [sb(f"KS{i}", [128, 16, 512], BF16) for i in range(2)]
        QS = [sb(f"QS{i}", [128, 8, 512], BF16) for i in range(2)]
        VA = [sb(f"VA{i}", [128, 64, 9]) for i in range(2)]
        zt = []
        for i in range(2):
            z = ms(None, KS[i][:, :, :].bitcast(I32), 0, eng="pool")
            ks_one = DSem(Q, "d_one")
            o1 = None
            for par in range(2):
                o1 = ks_one.dma(z, KS[i][96 + 2 * par:98 + 2 * par, 8 * par:8 * par + 8, :].bitcast(F32),
                                A["c_one2"].rearrange("p (a b) -> p a b", a=8))
            zq = ms(None, QS[i][96:128, :, :].bitcast(I32), 0, eng="dve")
            zv = ms(None, VA[i][:, :, 8:9], 1.0, eng="dve")
            zt.append([z, o1, zq, zv])
        KSr = Ring([Slot(KS[i]) for i in range(2)])
        QSr = Ring([Slot(QS[i]) for i in range(2)])
        EXPS = Turn()
        QX = Slot(sb("QX", [128, 8, 512], BF16))
        QX.rel = [ms(None, QX.ap[96:128, :, :].bitcast(I32), 0, eng="dve")]
        QX.ds, QX.dm = DSem(Q, "d_qs"), [DSem(Q, "d_qm"), DSem(Q, "d_qm")]
        VAr = Ring([Slot(VA[i]) for i in range(2)])
        for i in range(2):
            KSr.slots[i].rel = list(zt[i])
            QSr.slots[i].rel = list(zt[i])
            VAr.slots[i].rel = list(zt[i])
            KSr.slots[i].ds = DSem(Q, "d_ks")
            QSr.slots[i].ds = DSem(Q, "d_qs")
            QSr.slots[i].dm = [DSem(Q, "d_qm"), DSem(Q, "d_qm")]
            QSr.slots[i].dq = [DSem(Q, "d_qq"), DSem(Q, "d_qq")]

        def ring(name, n, shape, dt=F32):
            return Ring([Slot(sb(f"{name}{i}", shape, dt)) for i in range(n)])
        FF = ring("FF", 2, [128, 512])
        GG = ring("GG", 1, [128, 512])
        HH = ring("HH", 3, [128, 3, 512], BF16)
        M3 = ring("M3", 2, [128, 16, 4])
        MB = ring("MB", 2, [128, 2, 32], BF16)
        MT = ring("MT", 2, [32, 256], BF16)
        TV = ring("TV", 1, [128, 512])
        bank[6].rel = [ms(None, PS[:, 6, :], 0.0, eng="dve")]
        PT = ring("PT", 4, [128, 1024])
        RC = ring("RC", 2, [128, 32])
        OO = ring("OO", 2, [128, 2, 128])
        OC = ring("OC", 1, [128, 2, 128])
        OT = ring("OT", 2, [128, 512])
        RR = ring("RR", 2, [128, 4, 128])
        BS = ring("BS", 2, [128, 4, 6])
        MV = ring("MV", 2, [128, 4, 2])
        RSD = ring("RSD", 2, [128, 4])
        BIG = sb("BIG", [128, 10520])

        QSLOT = (0, 0, 0, 1, 1, 2)
        KSLOT = (0, 1, 2, 0, 1, 0)

        def split3(src, ts_, w):
            hh, wh = HH.take()
            t1 = act([ts_, wh], hh.ap[:, 0, 0:w], src[:, 0:w])
            t2 = tt([ts_, t1], src[:, 0:w], src[:, 0:w], hh.ap[:, 0, 0:w], ALU.subtract, eng="pool")
            t3 = act(t2, hh.ap[:, 1, 0:w], src[:, 0:w])
            t4 = tt([t2, t3], hh.ap[:, 2, 0:w], src[:, 0:w], hh.ap[:, 1, 0:w], ALU.subtract, eng="pool")
            return hh, [t1, t3, t4], t4

        def stack_q(hh, ht, slot, wslot):
            t = None
            for par in range(2):
                for s in range(6):
                    t = slot.ds.dma([ht, wslot], slot.ap[48 * par + 8 * s:48 * par + 8 * s + 8, :, :],
                                    hh.ap[64 * par:64 * par + 64, QSLOT[s], :])
            return t

        def stack_k(hh, ht, slot, wslot):
            t = None
            for par in range(2):
                for s in range(6):
                    t = slot.ds.dma([ht, wslot], slot.ap[48 * par + 8 * s:48 * par + 8 * s + 8, 8 * par:8 * par + 8, :],
                                    hh.ap[64 * par:64 * par + 64, KSLOT[s], :])
            return t

        def project(xt, xtt, W, wt, b, rope):
            pj, wp = PJ.take()
            t1 = mm([wp, xtt, wt], pj.ap, W[0], xt)
            ff, wf = FF.take()
            if rope is None:
                if b is None:
                    t2 = act([t1, wf], ff.ap[:, :], pj.ap)
                else:
                    t2 = act([t1, wf, wt], ff.ap[:, :], pj.ap, ACT.Identity, bias=b[0])
                pj.free(t2)
                return ff, t2
            gg, wg = GG.take()
            bias0 = b[0] if b is not None else 0.0
            t2 = stt([t1, wf, rope[2], wt], ff.ap[:, :], pj.ap, bias0, rope[0], ALU.add, ALU.mult)
            pj.free(t2)
            pj, wp = PJ.take()
            t3 = mm([wp], pj.ap, W[1], xt)
            bias1 = b[1] if b is not None else 0.0
            t4 = stt([t3, wg], gg.ap[:, :], pj.ap, bias1, rope[1], ALU.add, ALU.mult)
            pj.free(t4)
            t5 = tt([t2, t4], ff.ap[:, :], ff.ap[:, :], gg.ap[:, :], ALU.add, eng="pool")
            gg.free(t5)
            return ff, t5

        def neg_max(m, tm, mb, wm, order):
            for qt in range(2):
                if order == "self":
                    v = m.ap[:, :, qt:qt + 1].rearrange("p (a b) o -> p a (b o)", a=2)
                else:
                    v = m.ap[:, :, qt:qt + 1].rearrange("p (b a) o -> p a (b o)", a=2)
                o = mb.ap[:, qt, :].rearrange("p (a s b) -> p a s b", a=2, s=2)
                t1 = ts([tm, wm], o[:, :, 0, :], v, -1.0, None, ALU.mult)
                t2 = stt([t1], o[:, :, 1, :], v, -1.0, o[:, :, 0, :], ALU.mult, ALU.subtract)
            m.free(t2)
            return t2

        def max_rows(mb, t2):
            pj, wp = PJ.take()
            pb = pj.ap.bitcast(BF16)
            for qt in range(2):
                t3 = tr([t2, wp, t_idb], pb[0:32, 128 * qt:128 * qt + 128], mb.ap[:, qt, :], idb[:, :])
            mb.free(t3)
            mt, wt = MT.take()
            t4 = cp([t3, wt], mt.ap[:, :], pb[0:32, 0:256])
            pj.free(t4)
            return mt, t4

        def shift_rows(mb, t2, qslot, bb):
            mt, t4 = max_rows(mb, t2)
            t5 = qslot.dm[bb].dma([t4], qslot.ap[96:100, :, 256 * bb:256 * bb + 256], mt.ap[:, :])
            mt.free(t5)
            return t5

        def normalise(tv, t0, oo, wo, half, order):
            pj, wp = PJ.take()
            for qt in range(2):
                for g in range(2):
                    t1 = tr([t0, wp, t_c], pj.ap[:, 256 * qt + 128 * g:256 * qt + 128 * g + 128],
                            tv.ap[:, 256 * g + 128 * qt:256 * g + 128 * qt + 128], idf[:, :])
            tv.free(t1)
            rc, wr = RC.take()
            v = pj.ap.rearrange("p (q b k) -> p q b k", q=2, b=8)
            pars = (half,) if order == "self" else (0, 1)
            for i, par in enumerate(pars):
                o = 0 if order == "self" else 9 * par
                r = rc.ap[:, 16 * i:16 * i + 16].rearrange("p (q b o) -> p q b o", q=2, o=1)
                t2 = rcp([t1, wr], r, v[:, :, :, o + 8:o + 9])
                out_ = oo.ap.rearrange("p q (h d b) -> p q h b d", h=2, d=8)[:, :, par]
                t3 = tt([t2, wo], out_, v[:, :, :, o:o + 8], r.to_broadcast([128, 2, 8, 8]), ALU.mult)
            pj.free(t3)
            rc.free(t3)
            return t3

        def max_pass(qs, qd, ks, kd, mode, bias, bb, res):
            causal = mode in ("causal", "bias")
            yield from free_slot(M3)
            m3, wm = M3.take()
            for hh in range(16):
                blk = hh % 8
                mx, wx = MX.take()
                q0 = qs.ap[0:96, blk, 256 * bb:256 * bb + 256]
                k0 = ks.ap[0:96, hh, 256 * bb:256 * bb + 256]
                if causal:
                    parts = [(0, 0, 128), (1, 128, 256)]
                else:
                    parts = [(0, 0, 256), (1, 256, 256)]
                for qt, o, n in parts:
                    t1 = mm([wx, qd, kd], mx.ap[:, o:o + n], q0[:, 128 * qt:128 * qt + 128], k0[:, 0:n], t=mode == "none")
                    if mode == "bias":
                        t1 = mm([bias[2]], mx.ap[:, o:o + n], idb[:, :], bias[0][:, hh, 256 - n:256], s=False)
                    elif mode == "causal":
                        t1 = mm([t_c, t_idb], mx.ap[:, o + n - 128:o + n], idb[:, :], mskQ[:, :], s=False)
                    elif mode == "add" and qt == 0:
                        t1 = mm([bias[4], t_idb], mx.ap[:, o:o + 256], idb[:, :], bias[0][:, 0:256], s=False)
                    elif mode == "add":
                        t1 = mm([bias[4], t_idb], mx.ap[:, o + 128:o + 256], idb[:, :], bias[0][:, 0:128], s=False)
                if causal:
                    t2 = red([t1, wm], m3.ap[:, hh, 0:3], mx.ap[:, 0:384].rearrange("p (a k) -> p a k", a=3), ALU.max)
                else:
                    t2 = red([t1, wm], m3.ap[:, hh, 0:2], mx.ap.rearrange("p (a k) -> p a k", a=2), ALU.max)
                mx.free(t2)
                if hh % 2:
                    yield
            if causal:
                t2 = tt([t2], m3.ap[:, :, 1], m3.ap[:, :, 1], m3.ap[:, :, 2], ALU.max)
            mb, wm = MB.take()
            t2 = neg_max(m3, t2, mb, wm, "self")
            yield
            res.append(shift_rows(mb, t2, qs, bb))

        def exp_pass(qs, ks, va, vt, mode, bias, bb, ds, res):
            causal = mode in ("causal", "bias")
            n = 384 if causal else 512
            done = mode == "none"
            yield from EXPS.enter()
            yield from free_slot(OO)
            oo, wo = OO.take()
            behind = []
            pv = wv = None
            for s4 in range(4):
                for s2 in range(2):
                    st, wst = ST.take()
                    for i in range(2):
                        hh = 4 * s4 + 2 * s2 + i
                        q1 = qs.ap[0:100, hh % 8, 256 * bb:256 * bb + 256]
                        k1 = ks.ap[0:100, hh, 256 * bb:256 * bb + 256]
                        s_ = st.ap[:, i, :]
                        mm([wst, ds], s_[:, 0:256], k1[:, 0:128], q1, t=done)
                        if mode == "bias":
                            mm([bias[3]], s_[:, 0:256], idf[:, :], bias[1][:, hh, 0:256], s=False)
                        elif mode == "causal":
                            mm(None, s_[:, 0:128], idb[:, :], mskK[:, :], s=False)
                        elif mode == "add":
                            mm([bias[4]], s_[:, 0:128], idb[:, :], bias[1], s=False, t=False)
                            mm([bias[4]], s_[:, 0:128], idb[:, :], bias[2], s=False, t=True)
                        if causal:
                            mm(None, s_[:, 256:384], k1[:, 128:256], q1[:, 128:256], t=False)
                            if mode == "bias":
                                t3 = mm(None, s_[:, 256:384], idf[:, :], bias[1][:, hh, 0:128], s=False)
                            else:
                                t3 = mm(None, s_[:, 256:384], idb[:, :], mskK[:, :], s=False)
                        else:
                            t3 = mm(None, s_[:, 256:512], k1[:, 128:256], q1, t=done)
                            if mode == "add":
                                mm(None, s_[:, 256:512], idb[:, :], bias[5], s=False, t=False)
                                t3 = mm(None, s_[:, 256:512], idb[:, :], bias[6], s=False, t=True)
                    pt, wpt = PT.take()
                    pp = pt.ap[:, 0:2 * n].rearrange("p (a k) -> p a k", a=2)
                    t4 = act([t3, wpt], pp, st.ap[:, :, 0:n], ACT.Exp, scale=RS8)
                    st.free(t4)
                    behind.append((t4, pt, pp))
                    if s2 == 1 or s4 == 0:
                        yield
                        continue
                    (ta, pa, va_), (tb, pb_, vb_) = behind[0], behind[1]
                    behind = behind[2:]
                    pv, wv, t5 = four(s4 - 1, pv, wv, (ta, tb), (va_, vb_), va, vt, bb, causal)
                    pa.free(t5)
                    pb_.free(t5)
                    yield
                    if s4 == 2:
                        tv, wtv = TV.take()
                        t6 = act([t5, wtv], tv.ap[:, :], pv.ap)
                        pv.free(t6)
                        t6 = normalise(tv, t6, oo, wo, 0, "self")
                        pv = None
            (ta, pa, va_), (tb, pb_, vb_) = behind
            yield
            pv, wv, t5 = four(3, pv, wv, (ta, tb), (va_, vb_), va, vt, bb, causal)
            pa.free(t5)
            pb_.free(t5)
            tv, wtv = TV.take()
            t6 = act([t5, wtv], tv.ap[:, :], pv.ap)
            pv.free(t6)
            EXPS.leave()
            yield
            t6 = normalise(tv, t6, oo, wo, 1, "self")
            res.append((oo, t6, t5))

        def four(s4, pv, wv, ts_, ps_, va, vt, bb, causal):
            if pv is None:
                pv, wv = PV.take()
            g = s4 % 2
            for kt in range(2):
                for j in range(4):
                    hh = 4 * s4 + j
                    lo = 128 if kt == 1 and causal else 0
                    o = 256 if kt == 1 else 0
                    t5 = mm([ts_, wv, vt], pv.ap[32 * j:32 * j + 9, 256 * g + lo:256 * g + 256],
                            va.ap[:, (2 * bb + kt) * 16 + hh, :], ps_[j // 2][:, j % 2, o:o + 256 - lo],
                            s=kt == 0, t=kt == 1)
            return pv, wv, t5

        def to_ot(oo, to, ot, wot, bb):
            pj, wp = PJ.take()
            for qt in range(2):
                t1 = tr([to, wp, t_c], pj.ap[:, 128 * qt:128 * qt + 128], oo.ap[:, qt, :], idf[:, :])
            oo.free(t1)
            t2 = act([t1, wot], ot.ap[:, 256 * bb:256 * bb + 256], pj.ap[:, 0:256])
            pj.free(t2)
            return t2

        EPS = 1e-5
        NW = ring("NW", 2, [128, 3, 4])

        def rsqrt(w, o, v, eps):
            nw, wn = NW.take()
            a, y, t = (nw.ap[:, i, :] for i in range(3))
            k = ts([w, wn], a, v, eps, None, ALU.add)
            k = ts(k, y.bitcast(I32), a.bitcast(I32), 1, None, ALU.logical_shift_right)
            k = ts(k, y.bitcast(I32), y.bitcast(I32), -1.0, float(0x5F3759DF), ALU.mult, ALU.add)
            for i in range(3):
                k = tt(k, t, y, y, ALU.mult, eng="pool")
                k = tt(k, t, t, a, ALU.mult, eng="pool")
                k = ts(k, t, t, -0.5, 1.5, ALU.mult, ALU.add, eng="pool")
                k = tt(k, y if i < 2 else o, y, t, ALU.mult, eng="pool")
            nw.free(k)
            return k

        def layer_norm(c, r, tr_, eps_out=None, xn=None):
            bs, wb = BS.take()
            mv, wv = MV.take()
            rs, wr = RSD.take()
            for i in range(4):
                t1 = Q.add("dve", [tr_, wb], lambda e, i=i: e.bn_stats(bs.ap[:, i, :], r[:, i, :]))
            for i in range(4):
                t2 = Q.add("dve", [t1, wv], lambda e, i=i: e.bn_aggr(mv.ap[:, i, :], bs.ap[:, i, :]))
            bs.free(t2)
            t3 = rsqrt([t2, wr], rs.ap[:, 0:4], mv.ap[:, :, 1], EPS)
            for i in range(4):
                t4 = ts([t3, xtok[c]], X[:, 4 * c + i, :], r[:, i, :], mv.ap[:, i, 0:1], rs.ap[:, i:i + 1],
                        ALU.subtract, ALU.mult)
            mv.free(t4)
            rs.free(t4)
            xtok[c] = t4
            return t4

        def transpose_x(c, src, t4):
            pj, wp = PJ.take()
            for i in range(4):
                t5 = tr([t4, wp, t_c], pj.ap[:, 128 * i:128 * i + 128], src[:, i, :], idf[:, :])
            t6 = act([t5, xtfree[c]], XT[:, 512 * c:512 * c + 512], pj.ap)
            pj.free(t6)
            xttok[c] = t6
            xtfree[c] = []
            return t5

        def out_proj(c, ot, tot, Wo, wt, bo, readers, last=False, xn=None, keep=None):
            if bo is not None:
                x = X[:, 4 * c:4 * c + 4, :]
                if keep is None:
                    xtok[c] = tt([xtok[c], wt], x, x, bo.rearrange("p (o k) -> p o k", o=1).to_broadcast([128, 4, 128]),
                                 ALU.add, eng="pool")
            pj, wp = PJ.take()
            t1 = None
            for i in range(4):
                o = pj.ap[:, 128 * i:128 * i + 128]
                t1 = mm([wp, tot, wt], o, ot.ap[:, 128 * i:128 * i + 128], Wo)
            ot.free(t1)
            rr, wr = RR.take()
            t2 = tt([t1, wr, xtok[c]], rr.ap[:, :, :], pj.ap.rearrange("p (a b) -> p a b", a=4),
                    X[:, 4 * c:4 * c + 4, :], ALU.add)
            pj.free(t2)
            yield
            if keep is not None:
                xtfree[c] = readers
                x = X[:, 4 * c:4 * c + 4, :]
                xtok[c] = tt(t2, x, x, rr.ap[:, :, :], ALU.add, eng="pool")
                yield from keep(c, t2, rr.ap[:, :, :])
                rr.free(xtok[c], xttok[c])
                return
            t4 = layer_norm(c, rr.ap, t2)
            rr.free(t4)
            yield
            xtfree[c] = readers
            if xn is None:
                transpose_x(c, X[:, 4 * c:4 * c + 4, :], t4)
            else:
                yield from xn(c, t4)
            yield

        def values(c, xt, xtt, Wv, wt, bv):
            va, wv = VAr.take()
            pj, wp = PJ.take()
            for i in range(4):
                o = pj.ap[:, 128 * i:128 * i + 128]
                t1 = mm([wp, xtt, wt], o, xt[:, 128 * i:128 * i + 128], Wv)
            if bv is not None:
                for i in range(4):
                    t2 = tt([t1, wv], va.ap[:, 16 * i:16 * i + 16, 0:8],
                            pj.ap[:, 128 * i:128 * i + 128].rearrange("p (a k) -> p a k", k=8),
                            bv.rearrange("p (a k) -> p a k", k=8), ALU.add)
            else:
                t2 = act([t1, wv], va.ap[:, :, 0:8], pj.ap.rearrange("p (a k) -> p a k", k=8))
            pj.free(t2)
            return va, t2, t1

        def stack_q_half(hh, ht, slot, wslot, bb):
            for par in range(2):
                for s in range(6):
                    t = slot.dq[bb].dma([ht, wslot], slot.ap[48 * par + 8 * s:48 * par + 8 * s + 8, :, 256 * bb:256 * bb + 256],
                                        hh.ap[64 * par:64 * par + 64, QSLOT[s], 0:256])
            return t

        def self_attention(c, bb, S, Wd, mode, rope=None, bias=None, reps=1, gate=None, cross=None, xn=None, keep=None):
            S = S.setdefault(c, {})
            xt, xtt = XT[:, 512 * c:512 * c + 512], xttok[c]
            wt = Wd["t"]
            if bb == 0:
                yield from free_slot(QSr, KSr, VAr)
                S["qs"], wq = QSr.take()
                S["ks"], wk = KSr.take()
                xtt = xttok[c]
                ff, tf = project(xt, xtt, Wd["q"], wt, Wd["qb"], rope)
                yield
                hq, hqt, fr = split3(ff.ap, tf, 512)
                ff.free(fr)
                yield
                S["qd"] = stack_q(hq, hqt, S["qs"], wq)
                hq.free(S["qd"])
                ff, tf = project(xt, xtt, Wd["k"], wt, Wd["kb"], rope)
                yield
                hk, hkt, fr = split3(ff.ap, tf, 512)
                ff.free(fr)
                yield
                S["kd"] = stack_k(hk, hkt, S["ks"], wk)
                hk.free(S["kd"])
                yield from free_slot(VAr)
                S["va"], S["vt"], S["rd"] = values(c, xt, xtt, Wd["v"], wt, Wd["vb"])
                for _ in range(8):
                    yield
                yield from free_slot(OT)
                S["ot"], S["wot"] = OT.take()
                S["tot"], S["tpv"] = [None, None], [None, None]
            while "tot" not in S:
                yield
            qs, ks, qd = S["qs"], S["ks"], S["qd"]
            for rep in range(reps):
                res = []
                yield from max_pass(qs, qd, ks, S["kd"], mode, bias, bb, res)
                for _ in range(3):
                    yield
                yield from exp_pass(qs, ks, S["va"], S["vt"], mode, bias, bb, res[0], res)
                oo, to, tpv = res[1]
                if cross is not None:
                    while ("oc", bb) not in S:
                        yield
                    oc, tc = S["oc", bb]
                    to = tt([to, tc], oo.ap[:, :, :], oo.ap[:, :, :], oc.ap[:, :, :], ALU.add, eng="pool")
                    oc.free(to)
                if gate is not None:
                    to, S["rd"] = yield from gate(c, bb, oo, to)
                yield
                S["tot"][bb] = to_ot(oo, to, S["ot"], S["wot"], bb)
                S["tpv"][bb] = tpv
                yield
                if rep < reps - 1:
                    hq, hqt, fr = split3(S["ot"].ap[:, 256 * bb:256 * bb + 256], S["tot"][bb], 256)
                    qd = stack_q_half(hq, hqt, qs, [tpv], bb)
                    S["wot"] = [S["wot"], fr]
                    hq.free(qd)
                    for _ in range(GAP3):
                        yield
            if bb == 0:
                return
            tpv, tot = S["tpv"], S["tot"]
            qs.free(tpv)
            ks.free(tpv)
            S["va"].free(tpv)
            yield from out_proj(c, S["ot"], tot, Wd["o"], wt, Wd["ob"], [S["rd"], S.get("xrd"), tpv], xn=xn, keep=keep)

        def attend(skew, w, mode, **kw):
            S = {}
            units = [(c, bb) for c in range(NCH) for bb in range(2)]
            if isinstance(skew, int):
                skew = [u * skew + (12 if u % 2 else 0) for u in range(16)]
            order = sorted(range(16), key=lambda u: skew[u])
            gens = [(self_attention(*units[u], S, w, mode, **kw), skew[u]) for u in order]
            if "cross" in kw:
                gens = [g for i, u in enumerate(order) for g in ((kw["cross"](*units[u], S), skew[u]), gens[i])]
            run_pipeline([g for g, _ in gens], [t for _, t in gens])

        def ends(*engs):
            return [Q.q[k][-1][2] for k in (engs or ("pe", "act", "dve", "pool"))]

        class WL:
            turn = 0
            done = [[], []]

        def load_weights(names):
            Q_ = {}
            ds = DSem(Q, "d_w")
            half = WL.turn % 2
            WL.turn += 1
            base = half * 2176
            pos = base
            t = None
            w = WL.done[half]
            for key, name in names:
                ap = A[name]
                if key in ("vb", "ob", "cvb") or name == "L1a_bg":
                    ap = ap[0, :].partition_broadcast(128)
                k, n = ap.shape
                dst = WB[0:k, pos:pos + n]
                if ap.dtype != F32:
                    ap = ap.bitcast(F32)
                pos += n
                assert pos <= base + 2176, name
                Q_[key] = dst
                t = ds.dma(w, dst, ap)
            Q_["t"] = t
            Q_["half"] = half
            return Q_

        def weights_done(wd):
            WL.done[wd["half"]] = ends()

        SELF = [("q0", "wq"), ("q1", "wqs"), ("k0", "wk"), ("k1", "wks"), ("v", "wv"), ("o", "wo"),
                ("qb0", "bq"), ("qb1", "bqs"), ("kb0", "bk"), ("kb1", "bks"), ("vb", "bv"), ("ob", "bo")]

        def self_weights(pre, extra=()):
            names = [(k, f"{pre}_{n}") for k, n in SELF if f"{pre}_{n}" in A] + list(extra)
            w = load_weights(names)
            w["q"] = (w["q0"], w.get("q1"))
            w["k"] = (w["k0"], w.get("k1"))
            w["qb"] = (w["qb0"], w.get("qb1")) if "qb0" in w else None
            w["kb"] = (w["kb0"], w.get("kb1")) if "kb0" in w else None
            w.setdefault("vb", None)
            w.setdefault("ob", None)
            return w

        def rope_tables(name, after):
            ds = DSem(Q, "d_rope")
            C, S = BIG[:, 0:512], BIG[:, 512:1024]
            ds.dma(after, C, A[name + "_c"])
            t = ds.dma(after, S, A[name + "_s"])
            return (C, S, t)

        CT = sb("CT", [64, 2048])
        ct_t = DSem(Q, "d_ct").dma(None, CT[:, :], A["ctxT"])
        KC = BIG[:, 0:8192].bitcast(BF16).rearrange("p (a b q k) -> p a b q k", a=8, b=16, q=2)
        VB = BIG[:, 8192:8192 + 2304].rearrange("p (b a k) -> p b a k", b=16, a=8)

        class BigMem:
            free = None

        def cross_setup(Wk, bk, Wv, bv, wt):
            z2 = ms(BigMem.free, BIG[:, 8192:8192 + 2304], 0.0, eng="dve")
            ds = DSem(Q, "d_kc")
            kone = ds.dma(BigMem.free, BIG[96:100, 0:8192], A["c_kc"])
            v1 = ms(z2, VB[0:64, :, :, 8:9], 1.0, eng="dve")
            v2 = ms(z2, VB[64:128, :, :, 17:18], 1.0, eng="dve")
            kt = None
            for n in range(2):
                pj, wp = PJ.take()
                t1 = mm([wp, ct_t, wt], pj.ap.rearrange("p (a b) -> p a b", a=8), Wk,
                        CT[:, 1024 * n:1024 * n + 1024].rearrange("p (a q b) -> p a q b", a=8, q=2)[:, :, 0, :])
                ff, wf = FF.take()
                if bk is None:
                    t2 = act([t1, wf], ff.ap[:, :], pj.ap)
                else:
                    t2 = act([t1, wf], ff.ap[:, :], pj.ap, ACT.Identity, bias=bk)
                pj.free(t2)
                hk, hkt, fr = split3(ff.ap, t2, 512)
                ff.free(fr)
                qs, wq = QSr.take()
                for par in range(2):
                    for s in range(6):
                        kd = qs.ds.dma([hkt, wq], qs.ap[48 * par + 8 * s:48 * par + 8 * s + 8, :, :],
                                       hk.ap[64 * par:64 * par + 64, KSLOT[s], :])
                hk.free(kd)
                sv = qs.ap[0:96, :, :].rearrange("p a (b k) -> p a b k", b=8)
                k1 = act([kd, BigMem.free, t_c], KC[0:96, :, 8 * n:8 * n + 8, 0, :], sv, ACT.Copy,
                         scale=pmask[0:96, 0:1])
                k2 = ts([kd, BigMem.free, t_c], KC[0:96, :, 8 * n:8 * n + 8, 1, :], sv, pmask[0:96, 1:2], None,
                        ALU.mult)
                qs.free(k1, k2)
                kt = [k1, k2, kone]
            for r in range(4):
                pj, wp = PJ.take()
                for i in range(4):
                    b = 4 * r + i
                    l = CT[:, 128 * b:128 * b + 128]
                    o = pj.ap[:, 128 * i:128 * i + 128]
                    t1 = mm([wp, ct_t, wt], o, l, Wv)
                v = pj.ap.rearrange("p (i q k) -> p i q k", i=4, q=16)
                if bv is None:
                    t2 = act([t1, z2], VB[0:64, 4 * r:4 * r + 4, :, 0:8], v[0:64, :, 0:8, :])
                    t3 = act([t1, z2], VB[64:128, 4 * r:4 * r + 4, :, 9:17], v[64:128, :, 8:16, :])
                else:
                    b3 = bv.rearrange("p (q k) -> p q k", k=8)
                    for i in range(4):
                        t2 = tt([t1, z2], VB[0:64, 4 * r + i, :, 0:8], v[0:64, i, 0:8, :], b3[0:64, 0:8], ALU.add)
                        t3 = tt([t1, z2], VB[64:128, 4 * r + i, :, 9:17], v[64:128, i, 8:16, :], b3[64:128, 8:16], ALU.add)
                pj.free(t2, t3)
            return kt, [t2, t3, v1, v2]

        def cross_scores(qs, qd, kct, vbt, b, bb):
            yield from free_slot(M3)
            m3, wm = M3.take()
            for qt in range(2):
                for half in range(2):
                    mx, wx = MX.take()
                    for i in range(4):
                        blk = 4 * half + i
                        t1 = mm([wx, qd, kct], mx.ap[:, 128 * i:128 * i + 128],
                                qs.ap[0:96, blk, 256 * bb + 128 * qt:256 * bb + 128 * qt + 128],
                                KC[0:96, blk, b, :, :].rearrange("p a k -> p (a k)"))
                    t2 = red([t1, wm], m3.ap[:, 8 * half:8 * half + 8, qt],
                             mx.ap.rearrange("p (a k) -> p a k", a=8), ALU.max)
                    mx.free(t2)
                yield
            mb, wmb = MB.take()
            t2 = neg_max(m3, t2, mb, wmb, "cross")
            yield
            dm = shift_rows(mb, t2, qs, bb)
            yield
            yield
            yield
            yield from free_slot(OC)
            oo, wo = OC.take()
            yield from EXPS.enter()
            pv, wv = PV.take()
            for half in range(2):
                st, wst = ST.take()
                sv = st.ap.rearrange("p a (b k) -> p (a b) k", b=2)
                for i in range(4):
                    blk = 4 * half + i
                    t3 = mm([wst, dm], sv[:, i, :], KC[0:100, blk, b, :, :].rearrange("p a k -> p (a k)"),
                            qs.ap[0:100, blk, 256 * bb:256 * bb + 256])
                pt, wpt = PT.take()
                t4 = act([t3, wpt], pt.ap.rearrange("p (a k) -> p a k", a=2), st.ap, ACT.Exp, scale=RS8)
                st.free(t4)
                yield
                for i in range(4):
                    t5 = mm([t4, wv, vbt], pv.ap[32 * i:32 * i + 18, 256 * half:256 * half + 256],
                            VB[:, b, 4 * half + i, :], pt.ap[:, 256 * i:256 * i + 256])
                pt.free(t5)
            tv, wtv = TV.take()
            t6 = act([t5, wtv], tv.ap[:, :], pv.ap)
            pv.free(t6)
            EXPS.leave()
            yield
            t6 = normalise(tv, t6, oo, wo, 0, "cross")
            yield
            return oo, t6, t5

        def cross_attention(c, Wd, kct, vbt, xn=None):
            xt = XT[:, 512 * c:512 * c + 512]
            yield from free_slot(QSr)
            xtt = xttok[c]
            qs, wq = QSr.take()
            ff, tf = project(xt, xtt, Wd["q"], Wd["t"], Wd["qb"], None)
            rd = Q.q["pe"][-1][2]
            yield
            hq, hqt, fr = split3(ff.ap, tf, 512)
            ff.free(fr)
            qd = stack_q(hq, hqt, qs, wq)
            hq.free(qd)
            for _ in range(4):
                yield
            yield from free_slot(OT)
            ot, wot = OT.take()
            for bb in range(2):
                oo, to, tpv = yield from cross_scores(qs, qd, kct, vbt, 2 * c + bb, bb)
                tot = to_ot(oo, to, ot, wot, bb)
                yield
            qs.free(tpv)
            yield from out_proj(c, ot, tot, Wd["o"], Wd["t"], Wd["ob"], [rd], xn=xn)

        ATT_SKEW = 11
        GAP3 = 6
        REP4 = 118
        CRS_SKEW = 12
        GSK = 2
        WIDE = 16

        def rms_input(g, tg):
            def f(c, t4, own=False):
                rr, wr = RR.take()
                t5 = rms_scale(c, t4, rr, wr, own)
                yield
                pj, wp = PJ.take()
                for i in range(4):
                    t6 = tr([t5, wp], pj.ap[:, 128 * i:128 * i + 128], rr.ap[:, i, :], idf[:, :])
                rr.free(t6)
                t7 = act([t6, xtfree[c], tg], XT[:, 512 * c:512 * c + 512], pj.ap, ACT.Copy, scale=g)
                pj.free(t7)
                xttok[c] = t7
                xtfree[c] = []
            return f

        def rms_scale(c, t4, rr, wr, own=False):
            rs, wrs = RSD.take()
            bs, wb = BS.take()
            x = own if own else X[:, 4 * c:4 * c + 4, :]
            k = tt([t4, wr], rr.ap[:, :, :], x, x, ALU.mult, eng="pool")
            k = red([k, wb], bs.ap[:, :, 0], rr.ap[:, :, :], ALU.add)
            k = ts(k, bs.ap[:, :, 1], bs.ap[:, :, 0], 1.0 / 128, None, ALU.mult)
            k = rsqrt([k, wrs], rs.ap[:, 0:4], bs.ap[:, :, 1], 1e-6)
            bs.free(k)
            for i in range(4):
                k = ts(k, rr.ap[:, i, :], x[:, i, :], rs.ap[:, i:i + 1], None, ALU.mult)
            rs.free(k)
            return k

        def sub(n):
            on = START <= n < STOP
            if on:
                Q.new_phase()
            return on

        if sub(0):
            w = self_weights("L0a")
            rope = rope_tables("rope0", None)
            attend(ATT_SKEW, w, "none", rope=rope)
            weights_done(w)
            BigMem.free = ends("dve")

        if sub(1):
            w = self_weights("L0x", [("cq", "L0x_wcq"), ("ck", "L0x_wck"), ("cv", "L0x_wcv"),
                                     ("cqb", "L0x_bcq"), ("ckb", "L0x_bck"), ("cvb", "L0x_bcv")])
            kct, vbt = cross_setup(w["ck"], w["ckb"], w["cv"], w["cvb"], w["t"])

            QXr = Ring([QX])

            def cross_unit(c, bb, S):
                S = S.setdefault(c, {})
                if bb == 0:
                    yield from free_slot(QXr)
                    qx, wq = QXr.take()
                    ff, tf = project(XT[:, 512 * c:512 * c + 512], xttok[c], (w["cq"],), w["t"], (w["cqb"],), None)
                    S["xrd"] = Q.q["pe"][-1][2]
                    yield
                    hq, hqt, fr = split3(ff.ap, tf, 512)
                    ff.free(fr)
                    S["xqd"] = stack_q(hq, hqt, qx, wq)
                    hq.free(S["xqd"])
                    for _ in range(4):
                        yield
                    S["xgo"] = True
                while "xgo" not in S:
                    yield
                oc, tc, tpv = yield from cross_scores(QX, S["xqd"], kct, vbt, 2 * c + bb, bb)
                S["oc", bb] = (oc, tc)
                if bb == 1:
                    QX.free(tpv)
            attend(12, w, "causal", cross=cross_unit)
            weights_done(w)
            BigMem.free = ends("pe")

        WE = [BIG[:, 1032 * i:1032 * i + 1028] for i in range(3)]
        HB = [Slot(BIG[:, 3096 + 2048 * i:3096 + 2048 * i + 2048].rearrange("p (a b) -> p a b", a=4)) for i in range(3)]
        GW = BIG[:, 9240:9752].rearrange("p (t e) -> p t e", e=16)
        GS = [Slot(BIG[:, 9752 + 384 * i:9752 + 384 * i + 384].rearrange("p (a t e) -> p a t e", a=6, t=4))
              for i in range(2)]
        GSr = Ring(GS)

        def bc(ap, shape, pat, **kw):
            return ap.rearrange(pat, **kw).to_broadcast(shape)

        def ranks(k, o, v, E, tri):
            a, wa = PT.take()
            b, wb = PT.take()
            sh = [128, 4, E, E]
            va = a.ap[:, 0:4 * E * E].rearrange("p (t x y) -> p t x y", t=4, x=E)
            vb = b.ap[:, 0:4 * E * E].rearrange("p (t x y) -> p t x y", t=4, x=E)
            oth = bc(v, sh, "p t (o e) -> p t o e", o=1)
            own = bc(v, sh, "p t (e o) -> p t e o", o=1)
            k1 = tt([k, wa], va, oth, own, ALU.is_gt)
            k2 = tt([k, wb], vb, oth, own, ALU.is_equal)
            for t in range(4):
                k3 = tt(k2, vb[:, t], vb[:, t], tri.rearrange("p (x y) -> p x y", x=16)[:, 0:E, 0:E], ALU.mult, eng="pool")
            k4 = tt([k1, k3], va, va, vb, ALU.add, eng="pool")
            k5 = red(k4, o, va, ALU.add)
            a.free(k5)
            b.free(k4)
            return k5

        def gate_unit(c, E, w, gw, gb, kind, res):
            xt, xtt = XT[:, 512 * c:512 * c + 512], xttok[c]
            yield from free_slot(GSr)
            gs, wg = GSr.take()
            lg, rk, ex, sm, mx = (gs.ap[:, i, :, 0:E] for i in range(5))
            pj, wp = PJ.take()
            for i in range(4):
                o = pj.ap[:, 16 * i:16 * i + E]
                k = mm([wp, xtt, w["t"], gw[1]], o, xt[:, 128 * i:128 * i + 128], gw[0], t=gb is None)
                if gb is not None:
                    k = mm([gw[1]], o, ones1[:, :], gb, s=False)
            rd = k
            k = cp([k, wg], lg, pj.ap[:, 0:64].rearrange("p (t e) -> p t e", t=4)[:, :, 0:E])
            pj.free(k)
            kt = None
            if kind == "L0":
                pj, wp = PJ.take()
                k1 = mm(wp, pj.ap[0:64, :], w["dw1"], xt)
                ff, wf = FF.take()
                k1 = act([k1, wf], ff.ap[0:64, :], pj.ap[0:64, :], ACT.Relu, bias=w["db1"])
                pj.free(k1)
                yield
                pj, wp = PJ.take()
                for i in range(4):
                    mm([wp, k1], pj.ap[:, i:i + 1], ff.ap[0:64, 128 * i:128 * i + 128], w["dw2"], t=False)
                    k1 = mm(None, pj.ap[:, i:i + 1], ones1[:, :], w["db2"], s=False)
                ff.free(k1)
                z, a, e = (gs.ap[:, 5, i, 0:4] for i in range(3))
                k1 = cp(k1, z, pj.ap[:, 0:4])
                pj.free(k1)
                k1 = act(k1, a, z, ACT.Abs)
                k1 = act(k1, a, a, ACT.Exp, scale=-1.0)
                k1 = ts(k1, a, a, 1.0, None, ALU.add)
                k1 = act(k1, a, a, ACT.Ln)
                k1 = stt(k1, z, z, 0.0, a, ALU.max, ALU.add)
                k1 = ts(k1, z, z, -0.5, 1.0 / 1.5, ALU.add, ALU.mult)
                k1 = ts(k1, z, z, 0.0, 1.0, ALU.max, ALU.min)
                k1 = ts(k1, z, z, 3.0, 1.0, ALU.mult, ALU.add)
                ka = ts(k1, a, z, 1.5, 1.0, ALU.is_ge, ALU.add)
                ka = stt(ka, e, z, 2.5, a, ALU.is_gt, ALU.add)
                kt = stt(ka, a, z, 3.5, e, ALU.is_ge, ALU.add)
            yield
            if kind != "L2":
                kr = ranks(k, rk, lg, E, w["tri"])
                if kind == "L0":
                    kr = tt([kr, kt], rk, rk, bc(a, [128, 4, E], "p (t o) -> p t o", o=1), ALU.is_lt)
                else:
                    kr = ts(kr, rk, rk, 1.5 if kind == "L1" else 3.5, None, ALU.is_lt)
            yield
            k1 = red(k, sm[:, :, 0:1], lg, ALU.max)
            k1 = tt(k1, ex, lg, bc(sm[:, :, 0:1], [128, 4, E], "p t o -> p t o"), ALU.subtract)
            k1 = act(k1, ex, ex, ACT.Exp)
            if kind != "L2":
                k1 = tt([k1, kr], ex, ex, rk, ALU.mult)
            k1 = red(k1, sm[:, :, 0:1], ex, ALU.add)
            k1 = rcp(k1, sm[:, :, 1:2], sm[:, :, 0:1])
            g = GW[:, 4 * c:4 * c + 4, 0:E]
            k1 = tt([k1, BigMem.free], g, ex, bc(sm[:, :, 1:2], [128, 4, E], "p t o -> p t o"), ALU.mult)
            yield
            if kind == "L2":
                kr = ranks(k1, rk, g, E, w["tri"])
                k1 = stt(kr, g, rk, 1.5, g, ALU.is_lt, ALU.mult)
                gs.free(k1)
                res[c] = k1
                return
            res[c] = k1
            if kind == "L1":
                k2 = red(k1, sm[:, :, 2:3], g, ALU.add)
                for i in range(4):
                    x = X[:, 4 * c + i, :]
                    xtok[c] = stt([k2, xtok[c]], x, x, sm[:, i, 2:3], x, ALU.mult, ALU.add)
            gs.free(k1, xtok[c])
            pj, wp = PJ.take()
            for i in range(4):
                k2 = tr([k1, wp], pj.ap[0:E, 128 * i:128 * i + 128], g[:, i, :], idf[:, :])
            ff, wf = FF.take()
            k2 = cp([k2, wf], ff.ap[0:E, :], pj.ap[0:E, :])
            pj.free(k2)
            yield
            pj, wp = PJ.take()
            for i in range(4):
                k3 = mm([k2, wp], pj.ap[:, 128 * i:128 * i + 128], ff.ap[0:E, 128 * i:128 * i + 128], w["b2"])
            ff.free(k3)
            x = X[:, 4 * c:4 * c + 4, :]
            xtok[c] = tt([k3, xtok[c]], x, x, pj.ap.rearrange("p (a b) -> p a b", a=4), ALU.add)
            pj.free(xtok[c])
            yield

        def experts(E, F, w1, w2, b1, func, gates, kind=None, w=None, xn=None, done=None):
            nh = F // 128
            ds = [DSem(Q, "d_we") for _ in range(3)]
            wtok = {}
            last = {}
            slotfree = [BigMem.free] * 3

            def load(e):
                i = e % 3
                ds[i].dma(slotfree[i], WE[i][:, 0:F], A[w1][e])
                if b1:
                    ds[i].dma(slotfree[i], WE[i][:, 1024:1024 + nh], A[b1][e])
                wtok[e] = ds[i].dma(slotfree[i], WE[i][:, 512:512 + nh * 128], A[w2][e])
            load(0)
            load(1)
            for h in HB:
                h.rel = BigMem.free or []

            def unit(e, c):
                if c == 1 and e + 2 < E:
                    load(e + 2)
                we = WE[e % 3]
                xin, xtt = XT[:, 512 * c:512 * c + 512], xttok[c]
                nx = None
                if kind == "L1":
                    nx, wn = FF.take()
                    xtt = ts([xtt, wn, w["t"]], nx.ap[:, :], xin, w["ga"][:, e:e + 1], w["be"][:, e:e + 1], ALU.mult, ALU.add,
                             eng="pool")
                    xin = nx.ap[:, :]
                hb = HB[(e * NCH + c) % 3]
                wh = list(hb.take())
                for hc in range(nh):
                    up, wu = UP.take()
                    k1 = mm([wu, xtt, wtok[e]], up.ap, we[:, 128 * hc:128 * hc + 128], xin)
                    if func is ACT.Relu and hc % 2:
                        if b1:
                            k2 = ts([k1, wh], hb.ap[:, hc, :], up.ap, we[:, 1024 + hc:1025 + hc], 0.0, ALU.add, ALU.max)
                        else:
                            k2 = ts([k1, wh], hb.ap[:, hc, :], up.ap, 0.0, None, ALU.max)
                    elif b1:
                        k2 = act([k1, wh], hb.ap[:, hc, :], up.ap, func, bias=we[:, 1024 + hc:1025 + hc])
                    else:
                        k2 = act([k1, wh], hb.ap[:, hc, :], up.ap, func)
                    up.free(k2)
                    if hc == nh - 2:
                        k0 = k2
                if nx is not None:
                    nx.free(k1)
                yield
                yield
                dn, wd = DN.take()
                for i in range(4):
                    for hc in range(nh):
                        k3 = mm([wd, k2, k0], dn.ap[:, 128 * i:128 * i + 128], hb.ap[:, hc, 128 * i:128 * i + 128],
                                we[:, 512 + 128 * hc:640 + 128 * hc], s=hc == 0, t=hc == nh - 1)
                hb.free(k3)
                for i in range(4):
                    x = X[:, 4 * c + i, :]
                    xtok[c] = stt([k3, xtok[c], gates[c]], x, dn.ap[:, 128 * i:128 * i + 128],
                                  GW[:, 4 * c + i, e:e + 1], x, ALU.mult, ALU.add)
                dn.free(xtok[c])
                if c == NCH - 1:
                    slotfree[e % 3] = k3
                if e == E - 1:
                    yield
                    x = X[:, 4 * c:4 * c + 4, :]
                    t4 = layer_norm(c, x, xtok[c])
                    yield
                    xtfree[c] = [k1]
                    if done is None:
                        transpose_x(c, x, t4)
                    yield
            run_pipeline([unit(e, c) for e in range(E) for c in range(NCH)], 1)
            BigMem.free = ends("pe", "dve")

        def gates_of(E, w, gw, gb, kind):
            res = {}
            for s_ in GS:
                s_.rel = BigMem.free or []
            run_pipeline([gate_unit(c, E, w, gw, gb, kind, res) for c in range(NCH)], GSK)
            return res

        if sub(2):
            w = load_weights([("gw", "L0f_gw"), ("gb", "L0f_gb"), ("tri", "c_tri"), ("dw1", "L0f_dw1"), ("db1", "L0f_db1"),
                              ("dw2", "L0f_dw2"), ("db2", "L0f_db2"), ("b2", "L0f_b2")])
            g = gates_of(4, w, (w["gw"], None), w["gb"], "L0")
            experts(4, 256, "L0f_w1", "L0f_w2", "L0f_b1", ACT.Relu, g)
            weights_done(w)

        if sub(3):
            w = self_weights("L1a", [("g", "L1a_wg"), ("gb", "L1a_bg"), ("pb", "L1a_pb"), ("off", "L1a_offc"),
                                     ("it", "c_iota"), ("itc", "c_iotac"),
                                     ("anti", "c_anti")])
            KB = BIG[:, 0:4096].rearrange("p (h k) -> p h k", h=16)
            TMP = BIG[:, 4096:8192].rearrange("p (h k) -> p h k", h=16)
            QB = BIG[:, 8192:10240].bitcast(BF16).rearrange("p (h k) -> p h k", h=16)
            ds = DSem(Q, "d_tab")
            sc, wsc = PT.take()
            sd, wsd = PT.take()
            se, wse = PT.take()
            OH, OHT = sc.ap[0:68, 0:512], sc.ap[:, 512:648].rearrange("p (n o) -> p n o", n=2)
            OFR = sc.ap[:, 648:716]
            PMS = sd.ap[:, 0:32].rearrange("p (n h) -> p n h", n=2)
            CN = sd.ap[:, 32:34]
            OFRI = sd.ap[:, 100:168].bitcast(I32)
            OFCI = w["off"]
            OFC = sd.ap[0:68, 170:171]
            EO = sd.ap[0:68, 180:196]
            PM2 = se.ap[0:16, 0:512]
            EX2 = se.ap[0:16, 512:1024]
            TB = [BIG[0:16, 0:640], BIG[0:16, 640:1280]]
            td = ds.dma([wsd], OFRI, A["L1a_offr"].partition_broadcast(128))
            k = cp([td, wsc], OFR, OFRI)
            k = cp([w["t"], wsd], OFC, OFCI.bitcast(I32))
            k1 = ts([k], OH, w["it"], OFC, None, ALU.is_equal)
            for n in range(2):
                k2 = ts(None, OHT[:, n, :], OFR, w["itc"][:, n:n + 1], None, ALU.is_equal)
            pj, wp = PJ.take()
            pbt = w["pb"]
            onec = w["itc"][0:68, 2:3]
            for n in range(2):
                mm([wp, k1], pj.ap[:, 32 * n:32 * n + 16], OH[:, 128 * n:128 * n + 128], pbt)
                k3 = mm(None, pj.ap[:, 32 * n + 16:32 * n + 17], OH[:, 128 * n:128 * n + 128], onec)
            pv = pj.ap[:, 0:64].rearrange("p (n h) -> p n h", n=2)
            k4 = ts([k3], CN, pv[:, :, 16], 1.0, None, ALU.max)
            k4 = rcp(k4, CN, CN)
            for n in range(2):
                k5 = ts(k4, PMS[:, n, :], pv[:, n, 0:16], CN[:, n:n + 1], None, ALU.mult)
            pj.free(k5)
            pj, wp = PJ.take()
            for n in range(2):
                k6 = mm([wp, k5, k2], pj.ap[0:68, 0:16], OHT[:, n, :], PMS[:, n, :], s=n == 0, t=n == 1)
            k7 = tt(k6, EO, pbt, pj.ap[0:68, 0:16], ALU.subtract)
            pj.free(k7)
            k7 = act(k7, EO, EO, ACT.Exp)
            pj, wp = PJ.take()
            onem = w["itc"][0:68, 2:18]
            k8 = mm([wp], pj.ap[0:16, :], onem, OH)
            ms_ = FF.take()
            cnt = ms_[0].ap[0:16, :]
            k9 = cp([k8, ms_[1]], cnt, pj.ap[0:16, :])
            pj.free(k9)
            k10 = ts([k9, wse], PM2, cnt, 1.0, None, ALU.max)
            k10 = rcp(k10, PM2, PM2)
            pj, wp = PJ.take()
            k11 = mm([wp], pj.ap[0:16, :], pbt, OH)
            k12 = tt([k10, k11], PM2, PM2, pj.ap[0:16, :], ALU.mult)
            pj.free(k12)
            pj, wp = PJ.take()
            k13 = mm([wp, k7], pj.ap[0:16, :], EO, OH)
            k14 = ts([k13, wse], EX2, pj.ap[0:16, :], 1e-30, None, ALU.max)
            pj.free(k14)
            k14 = act(k14, EX2, EX2, ACT.Ln)
            k15 = tt([k14, k12], PM2, PM2, EX2, ALU.add)
            k15 = ts(k15, PM2, PM2, float(8 ** 0.5), None, ALU.mult)
            k16 = ts([k9], cnt, cnt, 0.0, NEG, ALU.is_equal, ALU.mult)
            k17 = None
            for n in range(2):
                k17 = ms(BigMem.free, TB[n], NEG, eng="dve")
            k18 = tt([k17, k16, k15], TB[0][:, 256:512], PM2[:, 0:256], cnt[:, 0:256], ALU.add)
            k19 = tt([k17, k16, k15], TB[1][:, 1:257], PM2[:, 256:512], cnt[:, 256:512], ALU.add)
            ms_[0].free(k19)
            sc.free(k13)
            sd.free(k13)
            se.free(k19)
            tab = A["scratch"]
            td = ds.dma([k18, k19], tab.rearrange("(n h) k -> h n k", n=2),
                        BIG[0:16, 0:1280].rearrange("p (n k) -> p n k", n=2))
            tb = tab.tensor
            td3 = ds.dma([td], TMP, bass.AP(tb, 129, [[1, 128], [640, 16], [1, 256]]))

            def turn(kd, dst):
                for i in range(8):
                    pj, wp = PJ.take()
                    k1 = mm([kd, wp], pj.ap, w["anti"], TMP[:, 2 * i:2 * i + 2, :])
                    k2 = act([k1, BigMem.free], dst[:, 2 * i:2 * i + 2, :], pj.ap.rearrange("p (h k) -> p h k", h=2))
                    pj.free(k2)
                return k1, k2
            k1, td2 = turn(td3, KB)
            td3 = ds.dma([k1], TMP, bass.AP(tb, 16 * 640 + 1, [[1, 128], [640, 16], [1, 256]]))
            k1, kq = turn(td3, QB)

            def gate1(c, bb, oo, to):
                xt = XT[:, 512 * c + 256 * bb:512 * c + 256 * bb + 256]
                pj, wp = PJ.take()
                for i in range(2):
                    k1 = mm([wp], pj.ap[:, 128 * i:128 * i + 128], xt[:, 128 * i:128 * i + 128], w["g"])
                oc, wo = OC.take()
                o2 = oc.ap[:, :, :].rearrange("p a b -> p (a b)")
                k2 = tt([k1, wo], oc.ap[:, :, :], pj.ap[:, 0:256].rearrange("p (a b) -> p a b", a=2),
                        w["gb"].rearrange("p (o k) -> p o k", o=1).to_broadcast([128, 2, 128]), ALU.add)
                pj.free(k2)
                k2 = act(k2, o2, o2, ACT.Exp, scale=-1.0)
                k3 = ts(k2, o2, o2, 1.0, None, ALU.add)
                k3 = rcp(k3, o2, o2)
                k4 = tt([k3, to], oo.ap[:, :, :], oo.ap[:, :, :], oc.ap[:, :, :], ALU.mult, eng="pool")
                oc.free(k4)
                yield
                return k4, k1
            bias = (QB, KB, kq, td2)
            attend(ATT_SKEW, w, "bias", bias=bias, gate=gate1)
            weights_done(w)
            BigMem.free = ends("pe")

        if sub(4):
            w = self_weights("L1x", [("ck", "L1x_wck"), ("cv", "L1x_wcv")])
            kct, vbt = cross_setup(w["ck"], None, w["cv"], None, w["t"])
            run_pipeline([cross_attention(c, w, kct, vbt) for c in range(NCH)], CRS_SKEW)
            weights_done(w)
            BigMem.free = ends("pe")

        if sub(5):
            w = load_weights([("gw", "L1f_gw"), ("tri", "c_tri"), ("b2", "L1f_b2"), ("ga", "L1f_ga"), ("be", "L1f_be")])
            g = gates_of(8, w, (w["gw"], None), None, "L1")

            def xhat(c):
                rr, wr = RR.take()
                bs, wb = BS.take()
                mv, wv = MV.take()
                rs, wrs = RSD.take()
                k = xtok[c]
                pj, wp = PJ.take()
                for i in range(4):
                    k = tr([xttok[c], wp], pj.ap[:, 128 * i:128 * i + 128], XT[:, 512 * c + 128 * i:512 * c + 128 * i + 128],
                           idf[:, :])
                kx = act([k, wr], rr.ap.rearrange("p a b -> p (a b)"), pj.ap)
                pj.free(kx)
                for i in range(4):
                    k1 = Q.add("dve", [kx, wb], lambda e, i=i: e.bn_stats(bs.ap[:, i, :], rr.ap[:, i, :]))
                for i in range(4):
                    k2 = Q.add("dve", [k1, wv], lambda e, i=i: e.bn_aggr(mv.ap[:, i, :], bs.ap[:, i, :]))
                bs.free(k2)
                yield
                k3 = rsqrt([k2, wrs], rs.ap[:, 0:4], mv.ap[:, :, 1], 1e-6)
                for i in range(4):
                    k4 = ts([k3], rr.ap[:, i, :], rr.ap[:, i, :], mv.ap[:, i, 0:1], rs.ap[:, i:i + 1],
                            ALU.subtract, ALU.mult)
                mv.free(k4)
                rs.free(k4)
                yield
                xtfree[c] = [k]
                t5 = transpose_x(c, rr.ap, k4)
                rr.free(t5)
            run_pipeline([xhat(c) for c in range(NCH)], 1)
            experts(8, 512, "L1f_w1", "L1f_w2", "L1f_b1", ACT.Relu, g, kind="L1", w=w)
            weights_done(w)

        if sub(6):
            w = self_weights("L2a")
            MM = BIG[:, 0:512].bitcast(BF16)
            dm = DSem(Q, "d_mask").dma(BigMem.free, BIG[:, 0:512], A["c_addm"])
            bias = (MM[:, 0:256], MM[:, 256:384], MM[:, 384:512], None, dm, MM[:, 512:768], MM[:, 768:1024])
            attend([8 * (u % 4) + (12 if u % 2 else 0) + REP4 * (u // 4) for u in range(16)], w, "add", bias=bias, reps=3)
            weights_done(w)
            BigMem.free = ends("pe")

        pre8 = None
        g8 = None
        if START <= 8 < STOP:
            g8 = sb("g8", [128, 2])
            tg8 = DSem(Q, "d_g").dma(None, g8[:, :], A["L2f_g"])
            pre8 = rms_input(g8[:, 0:1], tg8)
        if sub(7):
            w = self_weights("L2x", [("ck", "L2x_wck"), ("cv", "L2x_wcv"), ("ckb", "L2x_bck"), ("cvb", "L2x_bcv")])
            kct, vbt = cross_setup(w["ck"], w["ckb"], w["cv"], w["cvb"], w["t"])
            run_pipeline([cross_attention(c, w, kct, vbt, xn=pre8) for c in range(NCH)], CRS_SKEW)
            weights_done(w)
            BigMem.free = ends("pe")

        if sub(8):
            if START == 8:
                def first(c):
                    yield from pre8(c, xtok[c])
                run_pipeline([first(c) for c in range(NCH)], 2)
            w = self_weights("L2f")
            rope = rope_tables("rope2", BigMem.free)
            attend(ATT_SKEW, w, "causal", rope=rope, keep=rms_input(g8[:, 1:2], tg8))
            weights_done(w)
            BigMem.free = ends("pe", "dve")
            w = load_weights([("gw", "L2f_gw"), ("tri", "c_tri"), ("triu", "c_triu"), ("one", "c_ones128")])
            g = gates_of(8, w, (w["gw"], None), None, "L2")
            cur, wc = RC.take()
            cand, tmp, cn = (cur.ap[:, 8 * i:8 * i + 8] for i in (1, 2, 3))
            cu = cur.ap[:, 0:8]
            big, wb = PT.take()
            eqs, we_ = PT.take()
            gv = GW[:, :, 0:8].rearrange("p t e -> p e t")
            cmp_ = big.ap[:, 0:256].rearrange("p (e t) -> p e t", e=8)
            ex8 = [128, 8, 32]

            def b8(v):
                return bc(v, ex8, "p (e o) -> p e o", o=1)

            def total(k):
                pj, wp = PJ.take()
                k = mm([k, wp, w["t"]], pj.ap[:, 0:8], w["one"], cn)
                return pj, k
            k = ms([list(g.values()), wc, wb, we_], cu, 0.0, eng="dve")
            for bit in range(29, -1, -1):
                k = ts(k, cand.bitcast(I32), cu.bitcast(I32), 1 << bit, None, ALU.bitwise_or)
                k = tt(k, cmp_, gv, b8(cand), ALU.is_ge)
                k = red(k, cn, cmp_, ALU.add)
                pj, k = total(k)
                k = stt(k, tmp, pj.ap[:, 0:8], 159.5, cand, ALU.is_gt, ALU.mult)
                pj.free(k)
                k = tt(k, cu, cu, tmp, ALU.max)
            k = tt(k, cmp_, gv, b8(cu), ALU.is_gt)
            k = red(k, cn, cmp_, ALU.add)
            eq = eqs.ap[:, 0:256]
            ke = tt(k, eq.rearrange("p (e t) -> p e t", e=8), gv, b8(cu), ALU.is_equal)
            pj, k = total(k)
            k = ts(k, tmp, pj.ap[:, 0:8], -1.0, 160.0, ALU.mult, ALU.add)
            pj.free(k)
            pj, wp = PJ.take()
            mm([wp, ke], pj.ap[:, 0:256], w["triu"], eq)
            k2 = mm(None, pj.ap[:, 256:512], w["one"], eq)
            tot_, run_ = eqs.ap[:, 256:512], eqs.ap[:, 512:768]
            k2 = cp(k2, tot_, pj.ap[:, 256:512])
            zero = eqs.ap[:, 768:800]
            kz = ms(we_, zero, 0.0, eng="dve")
            for e_ in range(8):
                k3 = Q.add("dve", [k2, kz], lambda e, e_=e_: e.tensor_tensor_scan(
                    run_[:, 32 * e_:32 * e_ + 32], tot_[:, 32 * e_:32 * e_ + 32], zero, 0.0, ALU.add, ALU.add))
            k3 = tt(k3, run_, run_, tot_, ALU.subtract)
            k3 = tt(k3, run_, run_, pj.ap[:, 0:256], ALU.add)
            pj.free(k3)
            r3 = run_.rearrange("p (e t) -> p e t", e=8)
            k3 = tt([k3, k], r3, r3, b8(tmp), ALU.is_lt)
            k3 = tt(k3, run_, run_, eq, ALU.mult)
            k3 = tt(k3, cmp_, cmp_, r3, ALU.add)
            k3 = tt(k3, gv, gv, cmp_, ALU.mult)
            cur.free(k3)
            big.free(k3)
            eqs.free(k3)
            experts(8, 256, "L2f_w1", "L2f_w2", None, ACT.Relu, {c: k3 for c in range(NCH)})
            weights_done(w)

        def linear_attention(c, w):
            xt, xtt = XT[:, 512 * c:512 * c + 512], xttok[c]
            pj, wp = PJ.take()
            k = mm([wp, xtt, w["t"]], pj.ap, w["q"], xt)
            ff, wf = FF.take()
            kq = act([k, wf], ff.ap[:, :], pj.ap, ACT.Relu)
            pj.free(kq)
            yield
            ot, wot = OT.take()
            for bb in range(2):
                pj, wp = PJ.take()
                for i in range(2):
                    rd = mm([wp], pj.ap[:, 256 * i:256 * i + 256], xt[:, 256 * bb + 128 * i:256 * bb + 128 * i + 128],
                            w["kv"])
                kv, wkv = PT.take()
                v = pj.ap.rearrange("p (i k) -> p i k", i=2)
                kr = kv.ap[:, 0:256].rearrange("p (i k) -> p i k", i=2)
                vr = kv.ap[:, 256:256 + 258].rearrange("p (i k) -> p i k", i=2)
                bd = kv.ap[:, 600:744]
                zz = kv.ap[:, 760:792].rearrange("p (i k) -> p i k", i=2)
                k1 = act([rd, wkv], kr, v[:, :, 0:128], ACT.Relu)
                k2 = act([rd, wkv], vr[:, :, 0:128], v[:, :, 128:256])
                k3 = ms(wkv, vr[:, :, 128:129], 1.0, eng="pool")
                pj.free(k1, k2)
                yield
                pj, wp = PJ.take()
                for i in range(2):
                    k4 = mm([wp, k1, k2, k3], pj.ap[:, 0:129], kr[:, i, :], vr[:, i, :], s=i == 0, t=i == 1)
                k5 = tt([k4], bd[:, 0:128].rearrange("p (h d) -> p h d", h=16),
                        pj.ap[:, 0:128].rearrange("p (h d) -> p h d", h=16),
                        bc(w["hm"], [128, 16, 8], "p (h o) -> p h o", o=1), ALU.mult)
                k6 = tt([k4], bd[:, 128:144], w["hm"], pj.ap[:, 128:129].to_broadcast([128, 16]), ALU.mult)
                pj.free(k6)
                yield
                pj, wp = PJ.take()
                o = pj.ap[:, 0:288].rearrange("p (i k) -> p i k", i=2)
                for i in range(2):
                    k7 = mm([wp, k6, k5, kq], o[:, i, :], ff.ap[:, 256 * bb + 128 * i:256 * bb + 128 * i + 128], bd)
                k8 = ts([k7], zz, o[:, :, 128:144], float(np.finfo(np.float32).eps), None, ALU.add)
                k8 = rcp(k8, zz, zz)
                oo, wo = OO.take()
                for i in range(2):
                    k9 = tt([k8, wo], oo.ap[:, i, :].rearrange("p (h d) -> p h d", h=16),
                            o[:, i, 0:128].rearrange("p (h d) -> p h d", h=16),
                            bc(zz[:, i, :], [128, 16, 8], "p (h o) -> p h o", o=1), ALU.mult)
                pj.free(k9)
                kv.free(k9, k7)
                yield
                tot = to_ot(oo, k9, ot, wot, bb)
                if bb == 1:
                    ff.free(k7)
                yield
            yield from out_proj(c, ot, tot, w["o"], w["t"], w["ob"], [rd])

        if sub(9):
            w = load_weights([("q", "L3a_wq"), ("kv", "L3a_wkv"), ("o", "L3a_wo"), ("ob", "L3a_bo"), ("hm", "c_hm")])
            run_pipeline([linear_attention(c, w) for c in range(NCH)], 4)
            weights_done(w)
            BigMem.free = ends("pe", "dve")

        if sub(10):
            dw = DSem(Q, "d_w")
            pos = 0
            w = {}
            for key, name in (("q", "L3x_wq"), ("k", "L3x_wk"), ("v", "L3x_wv"), ("o", "L3x_wo"), ("sel", "c_sel"),
                              ("ob64", "c_ob64"), ("bo", "L3x_bo")):
                k_, n_ = A[name].shape
                if key == "sel":
                    w[key] = BIG[0:k_, 8704:8704 + n_]
                    wtk = dw.dma([WL.done, BigMem.free], w[key], A[name])
                    continue
                w[key] = WB[0:k_, pos:pos + n_]
                pos += n_
                assert pos <= 4352
                wtk = dw.dma(WL.done, w[key], A[name])
            sel = w["sel"].bitcast(BF16)
            KB2 = [Slot(BIG[:, 2048 * i:2048 * i + 2048].rearrange("p (a b k) -> p a b k", a=8, b=2)) for i in range(2)]
            VB2 = [Slot(BIG[:, 4096 + 2048 * i:6144 + 2048 * i].rearrange("p (a b k) -> p a b k", a=8, b=2)) for i in range(2)]
            R2 = [Slot(BIG[:, o:o + 256]) for o in (8192, 8448, 9216, 9472)]
            z0 = ms(BigMem.free, BIG[:, 9216:9728], 0.0, eng="dve")
            z = ms(BigMem.free, BIG[:, 0:8192], 0.0, eng="dve")
            for s_ in KB2 + VB2 + R2:
                s_.rel = [z, z0]
            QT2 = Ring([Slot(KS[i][:, :, :].bitcast(F32).rearrange("p a b -> p (a b)").rearrange("p (a b) -> p a b", a=8))
                        for i in range(2)])
            for i in range(2):
                QT2.slots[i].rel = KSr.slots[i].rel
            KB2, VB2, R2 = Ring(KB2), Ring(VB2), Ring(R2)
            MX2, PV2 = Banks([[0]]), Banks([[6], [1]])
            O3r = Ring(QSr.slots + [QX])

            def wide(c):
                yield from free_slot(QT2, KB2, VB2)
                xt, xtt = XT[:, 512 * c:512 * c + 512], xttok[c]
                qt_, wq = QT2.take()
                kb, wk = KB2.take()
                vb, wv = VB2.take()
                for blk in range(8):
                    pj, wp = PJ.take()
                    rd = mm([wp, xtt, wtk], pj.ap, w["q"][:, 128 * blk:128 * blk + 128], xt)
                    kq = act([rd, wq], qt_.ap[:, blk, :], pj.ap)
                    pj.free(kq)
                    yield
                for half in range(2):
                    pj, wp = PJ.take()
                    for i in range(4):
                        k1 = mm([wp, ct_t], pj.ap[:, 128 * i:128 * i + 128].rearrange("p (a k) -> p a k", a=2),
                                w["k"][:, 512 * half + 128 * i:512 * half + 128 * i + 128],
                                CT[:, 256 * c:256 * c + 256].rearrange("p (a q k) -> p a q k", a=2, q=2)[:, :, 0, :])
                    v = pj.ap.rearrange("p (i a k) -> p i a k", i=4, a=2)
                    k2 = act([k1, wk], kb.ap[0:64, 4 * half:4 * half + 4, :, 0:64], v[0:64])
                    k3 = cp([k1, wk], kb.ap[64:128, 4 * half:4 * half + 4, :, 64:128], v[64:128])
                    pj.free(k2, k3)
                    kk = [k2, k3] if half == 0 else kk + [k2, k3]
                    yield
                kv = []
                for bb in range(2):
                    for half in range(2):
                        pj, wp = PJ.take()
                        k1 = mm([wp], pj.ap, CT[:, 256 * c + 128 * bb:256 * c + 128 * bb + 128],
                                w["v"][:, 512 * half:512 * half + 512])
                        v = pj.ap.rearrange("p (i a k) -> p i a k", i=4, a=2)
                        k2 = act([k1, wv], vb.ap[0:64, 4 * half:4 * half + 4, bb, 0:64], v[0:64, :, 0, :])
                        k3 = cp([k1, wv], vb.ap[64:128, 4 * half:4 * half + 4, bb, 64:128], v[64:128, :, 1, :])
                        pj.free(k2, k3)
                        kv += [k2, k3]
                        yield
                outs = []
                for bb in range(2):
                    yield from free_slot(M3)
                    m3, wm = M3.take()
                    for qt in range(2):
                        for half in range(2):
                            mx, wx = MX2.take()
                            for i in range(4):
                                blk = 4 * half + i
                                k4 = mm([wx, kk, kq], mx.ap[:, 128 * i:128 * i + 128],
                                        qt_.ap[:, blk, 256 * bb + 128 * qt:256 * bb + 128 * qt + 128], kb.ap[:, blk, bb, :])
                            k5 = red([k4, wm], m3.ap[:, 8 * half:8 * half + 8, qt],
                                     mx.ap.rearrange("p (a k) -> p a k", a=8), ALU.max)
                            mx.free(k5)
                        yield
                    mb, wmb = MB.take()
                    for qt in range(2):
                        v = m3.ap[:, :, qt:qt + 1].rearrange("p (b a) o -> p a (b o)", a=2)
                        o = mb.ap[:, qt, :].rearrange("p (a s b) -> p a s b", a=2, s=2)
                        k6 = ts([k5, wmb], o[:, :, 0, :], v, -1.0, None, ALU.mult)
                        k6 = stt([k6], o[:, :, 1, :], v, -1.0, o[:, :, 0, :], ALU.mult, ALU.subtract)
                    m3.free(k6)
                    pj, wp = PJ.take()
                    pb = pj.ap.bitcast(BF16)
                    for qt in range(2):
                        k7 = tr([k6, wp, t_idb], pb[0:32, 128 * qt:128 * qt + 128], mb.ap[:, qt, :], idb[:, :])
                    mb.free(k7)
                    mt, wmt = MT.take()
                    k8 = cp([k7, wmt], mt.ap[:, :], pb[0:32, 0:256])
                    pj.free(k8)
                    yield
                    yield from free_slot(O3r)
                    o3, wo3 = O3r.take()
                    o3v = o3.ap[:, :, :].bitcast(F32)
                    outs.append(o3)
                    for half in range(2):
                        st, wst = ST.take()
                        sv = st.ap.rearrange("p a (b k) -> p (a b) k", b=2)
                        for i in range(4):
                            blk = 4 * half + i
                            mm([wst], sv[:, i, :], kb.ap[:, blk, bb, :], qt_.ap[:, blk, 256 * bb:256 * bb + 256], t=False)
                            k9 = mm([k8], sv[:, i, :], sel[:, 128 * blk:128 * blk + 128], mt.ap[:, :], s=False)
                        pt, wpt = PT.take()
                        k10 = act([k9, wpt], pt.ap.rearrange("p (a k) -> p a k", a=2), st.ap, ACT.Exp, scale=0.125)
                        st.free(k10)
                        yield
                        for i in range(4):
                            blk = 4 * half + i
                            pv, wpv = PV2.take()
                            mm([k10, wpv, kv], pv.ap[:, 0:256], vb.ap[:, blk, bb, :], pt.ap[:, 256 * i:256 * i + 256])
                            k11 = mm(None, pv.ap[:, 256:512], w["ob64"], pt.ap[:, 256 * i:256 * i + 256])
                            rc, wrc = R2.take()
                            k12 = rcp([k11, wrc], rc.ap, pv.ap[:, 256:512])
                            k13 = tt([k12, wo3], o3v[:, blk, :], rc.ap, pv.ap[:, 0:256], ALU.mult)
                            rc.free(k13)
                            pv.free(k13)
                            if i % 2:
                                yield
                        pt.free(k11)
                    mt.free(k9)
                kb.free(k9)
                vb.free(k11)
                qt_.free(k9)
                pj, wp = PJ.take()
                for i in range(4):
                    for blk in range(8):
                        ov = outs[i // 2].ap[:, :, :].bitcast(F32)
                        mm([wp, k13], pj.ap[:, 128 * i:128 * i + 128], ov[:, blk, 128 * (i % 2):128 * (i % 2) + 128],
                           w["o"][:, 128 * blk:128 * blk + 128], s=blk == 0, t=False)
                    k14 = mm(None, pj.ap[:, 128 * i:128 * i + 128], ones1[:, :], w["bo"], s=False)
                outs[0].free(k14)
                outs[1].free(k14)
                rr, wr = RR.take()
                k15 = tt([k14, wr, xtok[c]], rr.ap[:, :, :], pj.ap.rearrange("p (a b) -> p a b", a=4),
                         X[:, 4 * c:4 * c + 4, :], ALU.add)
                pj.free(k15)
                yield
                k16 = layer_norm(c, rr.ap, k15)
                rr.free(k16)
                yield
                xtfree[c] = [rd]
                transpose_x(c, X[:, 4 * c:4 * c + 4, :], k16)
                yield
            run_pipeline([wide(c) for c in range(NCH)], WIDE)
            WL.done = [ends(), ends()]
            BigMem.free = ends("pe", "dve", "act")

        if sub(11):
            w = load_weights([("key", "L3f_key"), ("rw", "L3f_rw"), ("rb", "L3f_rb"), ("tri", "c_tri"), ("b2", "L3f_b2"),
                              ("one", "c_ones128"), ("buf", "c_buf"), ("buf2", "c_buf")])
            gw, sq, brow = w["buf"][:, 0:16], w["buf"][:, 16:32], w["buf2"][0:1, 0:16]
            k1 = stt(w["t"], gw, w["key"], 2.0, w["rw"], ALU.mult, ALU.add)
            k2 = tt(w["t"], sq, w["key"], w["key"], ALU.mult)
            pj, wp = PJ.take()
            k3 = mm([k2, wp], pj.ap[:, 0:16], w["one"], sq)
            k4 = tt([k3], brow, w["rb"], pj.ap[0:1, 0:16], ALU.subtract)
            pj.free(k4)
            g = gates_of(16, w, (gw, [k1, k4]), brow, "L3")
            experts(16, 512, "L3f_w1", "L3f_w2", "L3f_b1", ACT.Gelu, g, done=True)
            weights_done(w)

        s_out = DSem(Q, "d_out")
        for c in range(NCH):
            t = s_out.dma([xtok[c]], out.rearrange("b (t p) d -> p (b t) d", p=128)[:, 4 * c:4 * c + 4, :],
                          X[:, 4 * c:4 * c + 4, :])
        for d in Q.dsems:
            Q.add("sp", [Tok(d.sem, d.n)], lambda e: e.nop())

        Q.count()
        block = ctx.enter_context(nc.Block())

        @block.tensor
        def _(e):
            Q.emit("pe", e)

        @block.scalar
        def _(e):
            Q.emit("act", e)

        @block.vector
        def _(e):
            Q.emit("dve", e)

        @block.gpsimd
        def _(e):
            Q.emit("pool", e)

        @block.sync
        def _(e):
            Q.emit("sp", e)


def _bf(a):
    h = (np.ascontiguousarray(a, np.float32).view(np.uint32) >> 16).astype(np.uint16)
    return h.view(np.uint32).view(np.float32)


def _consts():
    k = np.arange(128)
    c = {"c_ident": np.eye(128, dtype=np.float32), "c_ones": np.ones((2, 512), np.float32),
         "c_kc": _bf(np.broadcast_to((k[:4, None, None, None] // 2 == k[None, None, :2, None]), (4, 128, 2, 64))
                     .reshape(4, 16384)),
         "c_pmask": ((k[:, None] // 48) == k[None, :2]).astype(np.float32),
         "c_one2": _bf(np.ones((2, 4096), np.float32)),
         "c_maskq": _bf(np.where(k[None, :] > k[:, None], np.float32(NEG), np.float32(0))),
         "c_maskk": _bf(np.where(k[:, None] > k[None, :], np.float32(NEG), np.float32(0)))}
    c["c_triu"] = (k[:, None] < k[None, :]).astype(np.float32)
    c["c_ones128"] = np.ones((128, 128), np.float32)
    c["c_anti"] = np.eye(128, dtype=np.float32)[::-1]
    c["c_buf"] = np.zeros((128, 32), np.float32)
    c["c_hm"] = (k[:, None] // 8 == np.arange(16)[None, :]).astype(np.float32)
    c["c_ob64"] = (k[:, None] // 64 == k[None, :] // 64).astype(np.float32)
    r32 = np.arange(32)
    c["c_sel"] = _bf(((r32[:, None, None] // 16 == k[None, None, :] // 64)
                      & (r32[:, None, None] % 8 == np.arange(8)[None, :, None])).reshape(32, 1024))
    e16 = np.arange(16)
    c["c_tri"] = np.broadcast_to((e16[None, :] < e16[:, None]).astype(np.float32).reshape(1, 256), (128, 256))
    c["c_iota"] = np.broadcast_to(np.concatenate([np.arange(256), 255 - np.arange(256)]).astype(np.float32), (68, 512))
    c["c_iotac"] = np.concatenate([k[:, None], k[:, None] + 128, np.ones((128, 16))], 1).astype(np.float32)
    big = np.float32(-10000.0 * 8 ** 0.5)
    hi = (np.array([big]).view(np.uint32) & np.uint32(0xFFFF0000)).view(np.float32)[0]
    lo = np.float32(big - hi)
    dq = np.where(k[None, :] > k[:, None], 1.0, 0.0)
    dk = dq.T
    one, zer = np.ones((128, 128)), np.zeros((128, 128))
    c["c_addm"] = _bf(np.concatenate([hi * dq, hi * one, hi * dk, lo * dk, hi * one, hi * dk, lo * one, lo * dk], 1))
    d = (np.arange(128) // 8) % 8
    pos = np.arange(512) % 256
    for name, sgn in (("rope0", 1.0), ("rope2", -1.0)):
        fr = np.float32(10000.0) ** (np.float32(sgn) * np.arange(0, 8, 2, dtype=np.float32) / np.float32(8))
        ang = np.arange(256, dtype=np.float32)[:, None] * fr[None, :]
        s, co = np.sin(ang.astype(np.float64)), np.cos(ang.astype(np.float64))
        c[name + "_c"] = np.ascontiguousarray(co[pos][:, d // 2].T.astype(np.float32))
        c[name + "_s"] = np.ascontiguousarray((s[pos][:, d // 2].T * np.where(d % 2, 1.0, -1.0)[:, None]).astype(np.float32))
    return c


def _layout(inp):
    p = np.arange(128)
    par, d, blk = p // 64, (p // 8) % 8, p % 8
    perm = (par * 8 + blk) * 8 + d
    swap = (par * 8 + blk) * 8 + (d ^ 1)
    a = {"x": inp["x"], "xT": np.ascontiguousarray(np.transpose(inp["x"].reshape(4096, 128)))}

    def heads(pre, wq, wk, wv, wo, bq=None, bk=None, bv=None, bo=None, rope=False):
        a[pre + "_wq"], a[pre + "_wk"], a[pre + "_wv"], a[pre + "_wo"] = wq[:, perm], wk[:, perm], wv, wo[perm]
        if rope:
            a[pre + "_wqs"], a[pre + "_wks"] = wq[:, swap], wk[:, swap]
        if bq is not None:
            a[pre + "_bq"], a[pre + "_bk"], a[pre + "_bv"] = bq[perm][:, None], bk[perm][:, None], bv[None]
            if rope:
                a[pre + "_bqs"], a[pre + "_bks"] = bq[swap][:, None], bk[swap][:, None]
        if bo is not None:
            a[pre + "_bo"] = bo[None]

    w, b = inp["L0_attn_qkv_w"], inp["L0_attn_qkv_b"]
    heads("L0a", w[:, :128], w[:, 128:256], w[:, 256:], inp["L0_attn_out_w"], b[:128], b[128:256], b[256:],
          inp["L0_attn_out_b"], rope=True)
    a["ctxT"] = np.transpose(inp["ctx_512"], (2, 0, 1))[:, :, None, :].repeat(2, axis=2).reshape(64, 2048)
    g = lambda n: inp["L0_xattn_" + n]
    heads("L0x", g("Wq"), g("Wk"), g("Wv"), g("Wp"), g("bq"), g("bk"), g("bv"), g("bp"))
    a["L0x_wcq"], a["L0x_wck"], a["L0x_wcv"] = g("Wcq")[:, perm], g("Wck")[:, perm], g("Wcv")
    a["L0x_bcq"], a["L0x_bck"], a["L0x_bcv"] = g("bcq")[perm][:, None], g("bck")[perm][:, None], g("bcv")[None]
    cols = lambda b: b.reshape(b.shape[0], -1, 128).transpose(0, 2, 1)
    kt = lambda v: v.reshape(v.shape[0], -1, 128, 128).transpose(0, 2, 1, 3).reshape(v.shape[0], 128, -1)
    g = lambda n: inp["L0_ffn_" + n]
    a["L0f_gw"], a["L0f_gb"], a["L0f_dw1"], a["L0f_db1"] = g("gate_w"), g("gate_b")[None], g("dp_w1"), g("dp_b1")[:, None]
    a["L0f_dw2"], a["L0f_db2"], a["L0f_b2"] = g("dp_w2"), g("dp_b2")[None], g("eb2")
    a["L0f_w1"], a["L0f_w2"], a["L0f_b1"] = g("ew1"), kt(g("ew2")), cols(g("eb1"))
    g = lambda n: inp["L1_attn_" + n]
    w, b = np.transpose(g("Wqkv")), g("bqkv")
    heads("L1a", w[:, :128], w[:, 128:256], w[:, 256:], np.transpose(g("Wout")), b[:128], b[128:256], b[256:], g("bout"))
    a["L1a_wg"], a["L1a_bg"] = np.transpose(g("Wgate"))[:, perm], g("bgate")[perm][None]
    a["L1a_pb"] = g("pos_bias")
    a["L1a_offc"], a["L1a_offr"] = g("offsets")[:, None], g("offsets")
    g = lambda n: inp["L1_xattn_" + n]
    wkv = np.transpose(g("Wkv"))
    heads("L1x", np.transpose(g("Wq")), wkv[:, :128], wkv[:, 128:], np.transpose(g("Wo")))
    a["L1x_wck"], a["L1x_wcv"] = wkv[:, :128][:, perm], wkv[:, 128:]
    g = lambda n: inp["L1_ffn_" + n]
    a["L1f_gw"], a["L1f_b2"], a["L1f_ga"], a["L1f_be"] = g("Wg"), g("b2"), np.transpose(g("gamma")), np.transpose(g("beta"))
    a["L1f_w1"], a["L1f_w2"], a["L1f_b1"] = g("W1"), kt(g("W2")), cols(g("b1"))
    g = lambda n: inp["L2_attn_" + n]
    w, b = np.transpose(g("Wqkv_w")), g("Wqkv_b")
    heads("L2a", w[:, :128], w[:, 128:256], w[:, 256:], np.transpose(g("out_w")), b[:128], b[128:256], b[256:], g("out_b"))
    g = lambda n: inp["L2_xattn_" + n]
    heads("L2x", g("Wq"), g("Wk"), g("Wv"), g("Wo"), g("bq"), g("bk"), g("bv"), g("bo"))
    a["L2x_wck"], a["L2x_wcv"], a["L2x_bck"], a["L2x_bcv"] = g("Wk")[:, perm], g("Wv"), g("bk")[perm][:, None], g("bv")[None]
    a["L2f_g"] = np.stack([inp["L2_ffn_g1"], inp["L2_ffn_g2"]], 1)
    g = lambda n: inp["L2_ffn_" + n]
    w = g("w_qkv")
    heads("L2f", w[:, :128], w[:, 128:256], w[:, 256:], g("w_o"), rope=True)
    a["L2f_gw"], a["L2f_w1"], a["L2f_w2"] = g("w_router"), g("w1"), kt(g("w2"))
    g = lambda n: inp["L3_attn_" + n]
    w = np.transpose(g("w_qkv"))
    a["L3a_wq"], a["L3a_wkv"], a["L3a_wo"], a["L3a_bo"] = w[:, :128], w[:, 128:], np.transpose(g("w_proj")), g("b_proj")[None]
    g = lambda n: inp["L3_xattn_" + n]
    a["L3x_wq"], a["L3x_wk"], a["L3x_wv"], a["L3x_bo"] = g("Wq"), g("Wk"), g("Wv"), g("bo")[None]
    a["L3x_wo"] = kt(g("Wo")[None])[0]
    g = lambda n: inp["L3_ffn_" + n]
    a["L3f_key"], a["L3f_rw"], a["L3f_rb"] = np.transpose(g("keys")), np.transpose(g("rw")), g("rb")[None]
    a["L3f_w1"], a["L3f_w2"] = np.transpose(g("w1"), (0, 2, 1)), kt(np.transpose(g("w2"), (0, 2, 1)))
    a["L3f_b1"], a["L3f_b2"] = cols(g("b1")), g("b2")
    return {k: np.ascontiguousarray(v) for k, v in a.items()}


def kernel(**inputs):
    import concourse.bacc as _bacc
    from concourse.bass_utils import run_bass_kernel_spmd as _run

    nc = _bacc.Bacc("TRN2", target_bir_lowering=False, num_devices=1)
    arrays = _layout({k: np.asarray(v) for k, v in inputs.items()})
    arrays.update({n: np.ascontiguousarray(v) for n, v in _consts().items()})
    aps = {n: nc.dram_tensor("in_" + n, a.shape, mybir.dt.from_np(a.dtype), kind="ExternalInput").ap()
           for n, a in arrays.items()}
    aps["scratch"] = nc.dram_tensor("scratch", (32, 640), F32).ap()
    out = nc.dram_tensor("out_0", (16, 256, 128), F32, kind="ExternalOutput").ap()
    program(nc, aps, out)
    r = _run(nc, [{"in_" + n: a for n, a in arrays.items()}], core_ids=[0])
    return r.results[0]["out_0"]
```
